# Optimizing a Trainium2 kernel written in Bass

```python
import numpy as np
import jax
import jax.numpy as jnp

def _softmax(x, axis=-1):
    return jax.nn.softmax(x, axis=axis)

def _gelu(x):
    return jax.nn.gelu(x, approximate=True)

def _silu(x):
    return jax.nn.silu(x)

def _sigmoid(x):
    return jax.nn.sigmoid(x)

def _layernorm(x, axis=-1, eps=1e-05):
    m = jnp.mean(x, axis=axis, keepdims=True)
    v = jnp.var(x, axis=axis, keepdims=True)
    return (x - m) / jnp.sqrt(v + eps)

def _scatter_add(tgt, idx, src, axis=0):
    return tgt.at[idx].add(src)

def _segment_sum(src, seg, n):
    return jax.ops.segment_sum(src, seg, n)
kernel_name = 'mk_xattn_seq_d4_seqx_r4_e2b37e'

def setup_inputs(seed: int=0):
    np.random.seed(seed)
    _w = jnp.asarray

    def _rec_inputs():
        import jax
        import jax.numpy as jnp
        _rk = jax.random.key(seed)
        x = -0.0002928 + 1 * jax.random.normal(jax.random.fold_in(_rk, 1), (2, 1024, 256), jnp.float32)
        _lenS = 1024 - jax.random.randint(jax.random.fold_in(_rk, 7), (2,), 0, max(1, 1024 // 4) + 1, jnp.int32)
        _lenS2 = 77 - jax.random.randint(jax.random.fold_in(_rk, 8), (2,), 0, max(1, 77 // 4) + 1, jnp.int32)
        _ctx_1024P = jax.random.normal(jax.random.fold_in(_rk, 11), (2, 16, 256), jnp.float32)
        _ctx_1024c = jax.random.dirichlet(jax.random.fold_in(_rk, 511), 0.3 * jnp.ones((16,), jnp.float32), (2, 77))
        _ctx_1024t = jnp.einsum('bsk,bkd->bsd', _ctx_1024c, _ctx_1024P)
        _ctx_1024t = _ctx_1024t * jax.lax.rsqrt(jnp.mean(jnp.square(_ctx_1024t)) + 1e-12) * 0.953939
        ctx_1024 = 0.000227908 + 0.99994 * (_ctx_1024t + 0.3 * jax.random.normal(jax.random.fold_in(_rk, 611), (2, 77, 256), jnp.float32))
        itok_BxS_0_255 = jax.random.randint(jax.random.fold_in(_rk, 12), (2, 1024), 0, 64, jnp.int32)
        _validS = jnp.arange(1024)[None, :] < _lenS[:, None]
        _validS2 = jnp.arange(77)[None, :] < _lenS2[:, None]
        _causal = jnp.tril(jnp.ones((1024, 1024), dtype=bool))
        mask_Bx1x1xS2_if1 = jnp.where(jnp.ones((2, 1, 1, 77), dtype=bool), 1, 0).astype(jnp.int32)
        return (x, ctx_1024, itok_BxS_0_255, mask_Bx1x1xS2_if1)
    x, ctx_1024, itok_BxS_0_255, mask_Bx1x1xS2_if1 = _rec_inputs()

    def _L0_xattn_setup():
        import jax, jax.numpy as jnp
        import numpy as np
        B, T, S, D, H, F = (2, 512, 128, 256, 16, 1024)
        DH = D // H
        EPS = 1e-05

        def _ln(x, g, b):
            m = x.mean(-1, keepdims=True)
            v = ((x - m) ** 2).mean(-1, keepdims=True)
            return (x - m) * jax.lax.rsqrt(v + EPS) * g + b
        key = jax.random.key(seed)
        ks = jax.random.split(key, 8)
        w = lambda k, shape: jax.random.normal(k, shape, dtype=jnp.float32) * 0.02
        return {'x': jax.random.normal(ks[0], (B, T, D), dtype=jnp.float32), 'context': jax.random.normal(ks[1], (B, S, D), dtype=jnp.float32), 'w_qkv': w(ks[2], (D, 3 * D)), 'b_qkv': jnp.zeros((3 * D,), jnp.float32), 'w_ckv': w(ks[3], (D, 2 * D)), 'b_ckv': jnp.zeros((2 * D,), jnp.float32), 'g1': jnp.ones((D,), jnp.float32), 'be1': jnp.zeros((D,), jnp.float32), 'g2': jnp.ones((D,), jnp.float32), 'be2': jnp.zeros((D,), jnp.float32), 'gf': jnp.ones((D,), jnp.float32), 'bf': jnp.zeros((D,), jnp.float32), 'w1': w(ks[4], (D, F)), 'b1': jnp.zeros((F,), jnp.float32), 'w2': w(ks[5], (F, D)), 'b2': jnp.zeros((D,), jnp.float32)}
    _L0_xattn_all = _L0_xattn_setup()
    _L0_xattn_in = {k: v for k, v in _L0_xattn_all.items() if k in ('w_qkv', 'b_qkv', 'w_ckv', 'b_ckv', 'g1', 'be1', 'g2', 'be2', 'gf', 'bf', 'w1', 'b1', 'w2', 'b2')}
    del _L0_xattn_all

    def _L1_xattn_setup():
        import jax, jax.numpy as jnp
        import numpy as np
        NEG = -4294967295.0
        EPS = 1e-08
        H = 4
        L = 3

        def _layer_norm(x, g, b):
            mean = jnp.mean(x, axis=-1, keepdims=True)
            std = jnp.std(x, axis=-1, keepdims=True, ddof=1)
            return g * (x - mean) / (std + EPS) + b

        def _mha_layer(q, k, v, Wq, bq, Wk, bk, Wv, bv, gamma, beta):
            B, Sq, d = q.shape
            Sk = k.shape[1]
            dh = d // H
            Q = jax.nn.relu(q @ Wq + bq)
            K = jax.nn.relu(k @ Wk + bk)
            V = jax.nn.relu(v @ Wv + bv)
            Qh = Q.reshape(B, Sq, H, dh).transpose(2, 0, 1, 3)
            Kh = K.reshape(B, Sk, H, dh).transpose(2, 0, 1, 3)
            Vh = V.reshape(B, Sk, H, dh).transpose(2, 0, 1, 3)
            scores = jnp.einsum('hbqd,hbkd->hbqk', Qh, Kh) / jnp.sqrt(jnp.float32(dh))
            key_mask = jnp.sign(jnp.abs(jnp.sum(k, axis=-1)))
            scores = jnp.where(key_mask[None, :, None, :] == 0.0, NEG, scores)
            attn = jax.nn.softmax(scores, axis=-1)
            query_mask = jnp.sign(jnp.abs(jnp.sum(q, axis=-1)))
            attn = attn * query_mask[None, :, :, None]
            out = jnp.einsum('hbqk,hbkd->hbqd', attn, Vh)
            out = out.transpose(1, 2, 0, 3).reshape(B, Sq, d)
            out = out + q
            return _layer_norm(out, gamma, beta)
        key = jax.random.key(seed)
        ks = jax.random.split(key, 8)
        B, S, d = (2, 512, 256)
        inp = {'queries': jax.random.normal(ks[0], (B, S, d), jnp.float32), 'keys': jax.random.normal(ks[1], (B, S, d), jnp.float32), 'values': jax.random.normal(ks[2], (B, S, d), jnp.float32), 'Wq': jax.random.normal(ks[3], (L, d, d), jnp.float32) * 0.02, 'bq': jnp.zeros((L, d), jnp.float32), 'Wk': jax.random.normal(ks[4], (L, d, d), jnp.float32) * 0.02, 'bk': jnp.zeros((L, d), jnp.float32), 'Wv': jax.random.normal(ks[5], (L, d, d), jnp.float32) * 0.02, 'bv': jnp.zeros((L, d), jnp.float32), 'gamma': jnp.ones((L, d), jnp.float32), 'beta': jnp.zeros((L, d), jnp.float32), 'Wff': jax.random.normal(ks[6], (L, d, d), jnp.float32) * 0.02, 'bff': jnp.zeros((L, d), jnp.float32)}
        return inp
    _L1_xattn_all = _L1_xattn_setup()
    _L1_xattn_in = {k: v for k, v in _L1_xattn_all.items() if k in ('Wq', 'bq', 'Wk', 'bk', 'Wv', 'bv', 'gamma', 'beta', 'Wff', 'bff')}
    del _L1_xattn_all

    def _L2_xattn_setup():
        import jax, jax.numpy as jnp
        import numpy as np
        import math
        EPS_RMS = 1.1920929e-07
        EPS_DEN = 1e-06

        def rmsnorm(x, gamma):
            ms = jnp.mean(x * x, axis=-1, keepdims=True)
            return x * jax.lax.rsqrt(ms + EPS_RMS) * gamma
        key = jax.random.key(seed)
        ks = jax.random.split(key, 8)
        B, T, K, D = (4, 1024, 64, 256)
        x_tokens = jax.random.normal(ks[0], (B, T, D), dtype=jnp.float32)
        ctx = jax.random.normal(ks[1], (B, K, D), dtype=jnp.float32)
        idx = jnp.sort(jax.random.randint(ks[2], (B, T), 0, K), axis=-1)
        s = 1.0 / math.sqrt(D)
        Wq = jax.random.normal(ks[3], (D, D), dtype=jnp.float32) * s
        Wk = jax.random.normal(ks[4], (D, D), dtype=jnp.float32) * s
        Wv = jax.random.normal(ks[5], (D, D), dtype=jnp.float32) * s
        Wo = jax.random.normal(ks[6], (D, D), dtype=jnp.float32) * s
        return {'x_tokens': x_tokens, 'ctx': ctx, 'ctx_index_per_token': idx, 'gamma_q': jnp.ones((D,), jnp.float32), 'gamma_kv': jnp.ones((D,), jnp.float32), 'Wq': Wq, 'Wk': Wk, 'Wv': Wv, 'Wo': Wo}
    _L2_xattn_all = _L2_xattn_setup()
    _L2_xattn_in = {k: v for k, v in _L2_xattn_all.items() if k in ('gamma_q', 'gamma_kv', 'Wq', 'Wk', 'Wv', 'Wo')}
    del _L2_xattn_all

    def _L3_xattn_setup():
        import jax, jax.numpy as jnp
        import numpy as np
        EMBED = 256
        HEADS = 16
        HEAD_DIM = EMBED // HEADS
        FF = 4 * EMBED
        EPS = 1e-05

        def layernorm(x, g, b):
            mu = jnp.mean(x, axis=-1, keepdims=True)
            var = jnp.mean((x - mu) ** 2, axis=-1, keepdims=True)
            return (x - mu) * jax.lax.rsqrt(var + EPS) * g + b
        key = jax.random.key(seed)
        ks = jax.random.split(key, 16)
        B, S = (2, 512)
        f32 = jnp.float32
        inp = {'value': jax.random.normal(ks[0], (B, S, EMBED), f32), 'key': jax.random.normal(ks[1], (B, S, EMBED), f32), 'query': jax.random.normal(ks[2], (B, S, EMBED), f32), 'mask': jnp.ones((B, 1, 1, S), jnp.int32), 'wv': jax.random.normal(ks[3], (HEAD_DIM, HEAD_DIM), f32) * 0.02, 'wk': jax.random.normal(ks[4], (HEAD_DIM, HEAD_DIM), f32) * 0.02, 'wq': jax.random.normal(ks[5], (HEAD_DIM, HEAD_DIM), f32) * 0.02, 'w_out': jax.random.normal(ks[6], (EMBED, EMBED), f32) * 0.02, 'b_out': jnp.zeros((EMBED,), f32), 'g1': jnp.ones((EMBED,), f32), 'beta1': jnp.zeros((EMBED,), f32), 'w_ff1': jax.random.normal(ks[7], (EMBED, FF), f32) * 0.02, 'b_ff1': jnp.zeros((FF,), f32), 'w_ff2': jax.random.normal(ks[8], (FF, EMBED), f32) * 0.02, 'b_ff2': jnp.zeros((EMBED,), f32), 'g2': jnp.ones((EMBED,), f32), 'beta2': jnp.zeros((EMBED,), f32)}
        return inp
    _L3_xattn_all = _L3_xattn_setup()
    _L3_xattn_in = {k: v for k, v in _L3_xattn_all.items() if k in ('wv', 'wk', 'wq', 'w_out', 'b_out', 'g1', 'beta1', 'w_ff1', 'b_ff1', 'w_ff2', 'b_ff2', 'g2', 'beta2')}
    del _L3_xattn_all
    return {'x': x, 'ctx_1024': ctx_1024, 'itok_BxS_0_255': itok_BxS_0_255, 'mask_Bx1x1xS2_if1': mask_Bx1x1xS2_if1, 'L0_xattn_w_qkv': _L0_xattn_in['w_qkv'], 'L0_xattn_b_qkv': _L0_xattn_in['b_qkv'], 'L0_xattn_w_ckv': _L0_xattn_in['w_ckv'], 'L0_xattn_b_ckv': _L0_xattn_in['b_ckv'], 'L0_xattn_g1': _L0_xattn_in['g1'], 'L0_xattn_be1': _L0_xattn_in['be1'], 'L0_xattn_g2': _L0_xattn_in['g2'], 'L0_xattn_be2': _L0_xattn_in['be2'], 'L0_xattn_gf': _L0_xattn_in['gf'], 'L0_xattn_bf': _L0_xattn_in['bf'], 'L0_xattn_w1': _L0_xattn_in['w1'], 'L0_xattn_b1': _L0_xattn_in['b1'], 'L0_xattn_w2': _L0_xattn_in['w2'], 'L0_xattn_b2': _L0_xattn_in['b2'], 'L1_xattn_Wq': _L1_xattn_in['Wq'], 'L1_xattn_bq': _L1_xattn_in['bq'], 'L1_xattn_Wk': _L1_xattn_in['Wk'], 'L1_xattn_bk': _L1_xattn_in['bk'], 'L1_xattn_Wv': _L1_xattn_in['Wv'], 'L1_xattn_bv': _L1_xattn_in['bv'], 'L1_xattn_gamma': _L1_xattn_in['gamma'], 'L1_xattn_beta': _L1_xattn_in['beta'], 'L1_xattn_Wff': _L1_xattn_in['Wff'], 'L1_xattn_bff': _L1_xattn_in['bff'], 'L2_xattn_gamma_q': _L2_xattn_in['gamma_q'], 'L2_xattn_gamma_kv': _L2_xattn_in['gamma_kv'], 'L2_xattn_Wq': _L2_xattn_in['Wq'], 'L2_xattn_Wk': _L2_xattn_in['Wk'], 'L2_xattn_Wv': _L2_xattn_in['Wv'], 'L2_xattn_Wo': _L2_xattn_in['Wo'], 'L3_xattn_wv': _L3_xattn_in['wv'], 'L3_xattn_wk': _L3_xattn_in['wk'], 'L3_xattn_wq': _L3_xattn_in['wq'], 'L3_xattn_w_out': _L3_xattn_in['w_out'], 'L3_xattn_b_out': _L3_xattn_in['b_out'], 'L3_xattn_g1': _L3_xattn_in['g1'], 'L3_xattn_beta1': _L3_xattn_in['beta1'], 'L3_xattn_w_ff1': _L3_xattn_in['w_ff1'], 'L3_xattn_b_ff1': _L3_xattn_in['b_ff1'], 'L3_xattn_w_ff2': _L3_xattn_in['w_ff2'], 'L3_xattn_b_ff2': _L3_xattn_in['b_ff2'], 'L3_xattn_g2': _L3_xattn_in['g2'], 'L3_xattn_beta2': _L3_xattn_in['beta2']}

def reference(x, ctx_1024, itok_BxS_0_255, mask_Bx1x1xS2_if1, L0_xattn_w_qkv, L0_xattn_b_qkv, L0_xattn_w_ckv, L0_xattn_b_ckv, L0_xattn_g1, L0_xattn_be1, L0_xattn_g2, L0_xattn_be2, L0_xattn_gf, L0_xattn_bf, L0_xattn_w1, L0_xattn_b1, L0_xattn_w2, L0_xattn_b2, L1_xattn_Wq, L1_xattn_bq, L1_xattn_Wk, L1_xattn_bk, L1_xattn_Wv, L1_xattn_bv, L1_xattn_gamma, L1_xattn_beta, L1_xattn_Wff, L1_xattn_bff, L2_xattn_gamma_q, L2_xattn_gamma_kv, L2_xattn_Wq, L2_xattn_Wk, L2_xattn_Wv, L2_xattn_Wo, L3_xattn_wv, L3_xattn_wk, L3_xattn_wq, L3_xattn_w_out, L3_xattn_b_out, L3_xattn_g1, L3_xattn_beta1, L3_xattn_w_ff1, L3_xattn_b_ff1, L3_xattn_w_ff2, L3_xattn_b_ff2, L3_xattn_g2, L3_xattn_beta2):
    import jax
    import jax.numpy as jnp

    def _L0_xattn_ref(x, context, w_qkv, b_qkv, w_ckv, b_ckv, g1, be1, g2, be2, gf, bf, w1, b1, w2, b2):
        import jax, jax.numpy as jnp
        import numpy as np
        B, T, S, D, H, F = (2, 512, 128, 256, 16, 1024)
        DH = D // H
        EPS = 1e-05

        def _ln(x, g, b):
            m = x.mean(-1, keepdims=True)
            v = ((x - m) ** 2).mean(-1, keepdims=True)
            return (x - m) * jax.lax.rsqrt(v + EPS) * g + b
        b, t, d = x.shape
        s = context.shape[1]
        h, dh = (H, d // H)
        qkv = (_ln(x, g1, be1) @ w_qkv + b_qkv).reshape(b, t, 3, h, dh)
        q, k_self, v_self = (qkv[:, :, 0], qkv[:, :, 1], qkv[:, :, 2])
        ckv = (context @ w_ckv + b_ckv).reshape(b, s, 2, h, dh)
        k_ctx, v_ctx = (ckv[:, :, 0], ckv[:, :, 1])
        k = jnp.concatenate([k_self, k_ctx], axis=1)
        v = jnp.concatenate([v_self, v_ctx], axis=1)
        scale = 1.0 / jnp.sqrt(jnp.float32(dh))
        scores = jnp.einsum('bthd,bshd->bhts', q, k) * scale
        i = jnp.arange(t)[:, None]
        j = jnp.arange(t + s)[None, :]
        mask = (j >= t) | (j <= i)
        scores = jnp.where(mask, scores, -jnp.inf)
        attn = jax.nn.softmax(scores, axis=-1)
        attn_out = jnp.einsum('bhts,bshd->bthd', attn, v).reshape(b, t, d)
        x = x + attn_out
        hdn = _ln(_ln(x, g2, be2), gf, bf) @ w1 + b1
        hdn = jax.nn.gelu(hdn, approximate=False)
        x = x + (hdn @ w2 + b2)
        return x

    def _L1_xattn_ref(queries, keys, values, Wq, bq, Wk, bk, Wv, bv, gamma, beta, Wff, bff):
        import jax, jax.numpy as jnp
        import numpy as np
        NEG = -4294967295.0
        EPS = 1e-08
        H = 4
        L = 3

        def _layer_norm(x, g, b):
            mean = jnp.mean(x, axis=-1, keepdims=True)
            std = jnp.std(x, axis=-1, keepdims=True, ddof=1)
            return g * (x - mean) / (std + EPS) + b

        def _mha_layer(q, k, v, Wq, bq, Wk, bk, Wv, bv, gamma, beta):
            B, Sq, d = q.shape
            Sk = k.shape[1]
            dh = d // H
            Q = jax.nn.relu(q @ Wq + bq)
            K = jax.nn.relu(k @ Wk + bk)
            V = jax.nn.relu(v @ Wv + bv)
            Qh = Q.reshape(B, Sq, H, dh).transpose(2, 0, 1, 3)
            Kh = K.reshape(B, Sk, H, dh).transpose(2, 0, 1, 3)
            Vh = V.reshape(B, Sk, H, dh).transpose(2, 0, 1, 3)
            scores = jnp.einsum('hbqd,hbkd->hbqk', Qh, Kh) / jnp.sqrt(jnp.float32(dh))
            key_mask = jnp.sign(jnp.abs(jnp.sum(k, axis=-1)))
            scores = jnp.where(key_mask[None, :, None, :] == 0.0, NEG, scores)
            attn = jax.nn.softmax(scores, axis=-1)
            query_mask = jnp.sign(jnp.abs(jnp.sum(q, axis=-1)))
            attn = attn * query_mask[None, :, :, None]
            out = jnp.einsum('hbqk,hbkd->hbqd', attn, Vh)
            out = out.transpose(1, 2, 0, 3).reshape(B, Sq, d)
            out = out + q
            return _layer_norm(out, gamma, beta)
        q, k, v = (queries, keys, values)
        enc = q
        for i in range(L):
            enc = _mha_layer(q, k, v, Wq[i], bq[i], Wk[i], bk[i], Wv[i], bv[i], gamma[i], beta[i])
            enc = jax.nn.leaky_relu(enc @ Wff[i] + bff[i], negative_slope=0.2) + enc
            q, k, v = (enc, enc, enc)
        return enc

    def _L2_xattn_ref(x_tokens, ctx, ctx_index_per_token, gamma_q, gamma_kv, Wq, Wk, Wv, Wo):
        import jax, jax.numpy as jnp
        import numpy as np
        import math
        EPS_RMS = 1.1920929e-07
        EPS_DEN = 1e-06

        def rmsnorm(x, gamma):
            ms = jnp.mean(x * x, axis=-1, keepdims=True)
            return x * jax.lax.rsqrt(ms + EPS_RMS) * gamma
        B, T, D = x_tokens.shape
        K = ctx.shape[1]
        H = 16
        hd = D // H

        def split(x):
            return x.reshape(B, -1, H, hd).transpose(0, 2, 1, 3)
        q = split(rmsnorm(x_tokens, gamma_q) @ Wq.T)
        kn = rmsnorm(ctx, gamma_kv)
        k = split(kn @ Wk.T)
        v = split(kn @ Wv.T)
        ctx_pos = jnp.arange(K)[None, None, :]
        mask = (jnp.abs(ctx_pos - ctx_index_per_token[:, :, None]) <= 1)[:, None]
        scores = jnp.einsum('bhqd,bhkd->bhqk', q, k) / math.sqrt(hd)
        w = jnp.square(jax.nn.relu(scores))
        w = jnp.where(mask, w, 0.0)
        denom = jnp.maximum(w.sum(-1, keepdims=True), EPS_DEN)
        out = jnp.einsum('bhqk,bhkd->bhqd', w / denom, v)
        out = out.transpose(0, 2, 1, 3).reshape(B, T, D)
        return x_tokens + out @ Wo.T

    def _L3_xattn_ref(value, key, query, mask, wv, wk, wq, w_out, b_out, g1, beta1, w_ff1, b_ff1, w_ff2, b_ff2, g2, beta2):
        import jax, jax.numpy as jnp
        import numpy as np
        EMBED = 256
        HEADS = 16
        HEAD_DIM = EMBED // HEADS
        FF = 4 * EMBED
        EPS = 1e-05

        def layernorm(x, g, b):
            mu = jnp.mean(x, axis=-1, keepdims=True)
            var = jnp.mean((x - mu) ** 2, axis=-1, keepdims=True)
            return (x - mu) * jax.lax.rsqrt(var + EPS) * g + b
        B, S, E = query.shape
        v = value.reshape(B, -1, HEADS, HEAD_DIM) @ wv
        k = key.reshape(B, -1, HEADS, HEAD_DIM) @ wk
        q = query.reshape(B, -1, HEADS, HEAD_DIM) @ wq
        scores = jnp.einsum('bqhd,bkhd->bhqk', q, k)
        scores = jnp.where(mask == 0, jnp.float32(-1e+20), scores)
        attn = jax.nn.softmax(scores / jnp.sqrt(jnp.float32(EMBED)), axis=-1)
        out = jnp.einsum('bhqk,bkhd->bqhd', attn, v).reshape(B, S, E)
        attention = out @ w_out + b_out
        x = layernorm(attention + query, g1, beta1)
        ff = jax.nn.relu(x @ w_ff1 + b_ff1) @ w_ff2 + b_ff2
        return layernorm(ff + x, g2, beta2)
    x = _L0_xattn_ref(x, ctx_1024, L0_xattn_w_qkv, L0_xattn_b_qkv, L0_xattn_w_ckv, L0_xattn_b_ckv, L0_xattn_g1, L0_xattn_be1, L0_xattn_g2, L0_xattn_be2, L0_xattn_gf, L0_xattn_bf, L0_xattn_w1, L0_xattn_b1, L0_xattn_w2, L0_xattn_b2)
    x = _L1_xattn_ref(x, ctx_1024, ctx_1024, L1_xattn_Wq, L1_xattn_bq, L1_xattn_Wk, L1_xattn_bk, L1_xattn_Wv, L1_xattn_bv, L1_xattn_gamma, L1_xattn_beta, L1_xattn_Wff, L1_xattn_bff)
    x = _L2_xattn_ref(x, ctx_1024, itok_BxS_0_255, L2_xattn_gamma_q, L2_xattn_gamma_kv, L2_xattn_Wq, L2_xattn_Wk, L2_xattn_Wv, L2_xattn_Wo)
    x = _L3_xattn_ref(ctx_1024, ctx_1024, x, mask_Bx1x1xS2_if1, L3_xattn_wv, L3_xattn_wk, L3_xattn_wq, L3_xattn_w_out, L3_xattn_b_out, L3_xattn_g1, L3_xattn_beta1, L3_xattn_w_ff1, L3_xattn_b_ff1, L3_xattn_w_ff2, L3_xattn_b_ff2, L3_xattn_g2, L3_xattn_beta2)
    return x

_drawn_inputs = setup_inputs


def setup_inputs(seed=0):
    import zlib

    import numpy as np

    out = dict(_drawn_inputs(seed))
    spreads = {'L0_xattn_b_qkv': (0.0, 0.1),
     'L0_xattn_b_ckv': (0.0, 0.1),
     'L0_xattn_g1': (1.0, 0.6),
     'L0_xattn_be1': (0.0, 0.1),
     'L0_xattn_g2': (1.0, 0.2),
     'L0_xattn_be2': (0.0, 0.1),
     'L0_xattn_gf': (1.0, 0.2),
     'L0_xattn_bf': (0.0, 0.1),
     'L0_xattn_b1': (0.0, 0.1),
     'L0_xattn_b2': (0.0, 0.1),
     'L1_xattn_bq': (0.0, 0.8),
     'L1_xattn_bk': (0.0, 0.8),
     'L1_xattn_bv': (0.0, 0.1),
     'L1_xattn_gamma': (1.0, 0.2),
     'L1_xattn_beta': (0.0, 0.1),
     'L1_xattn_bff': (0.0, 0.1),
     'L2_xattn_gamma_q': (1.0, 0.2),
     'L2_xattn_gamma_kv': (1.0, 0.2),
     'L3_xattn_b_out': (0.0, 0.1),
     'L3_xattn_g1': (1.0, 0.2),
     'L3_xattn_beta1': (0.0, 0.1),
     'L3_xattn_b_ff1': (0.0, 0.1),
     'L3_xattn_b_ff2': (0.0, 0.1),
     'L3_xattn_g2': (1.0, 0.2),
     'L3_xattn_beta2': (0.0, 0.1)}
    factors = {'L1_xattn_Wq': 4.443,
     'L1_xattn_Wk': 3.874,
     'L3_xattn_wv': 6.363,
     'L3_xattn_wk': 8.0,
     'L3_xattn_wq': 8.0,
     'L3_xattn_w_out': 6.627}
    for name, (base, spread) in spreads.items():
        noise = np.random.default_rng([zlib.crc32(name.encode()), seed]).standard_normal(out[name].shape)
        drawn = base * np.exp(spread * noise) if base else spread * noise
        out[name] = jnp.asarray(drawn.astype(out[name].dtype))
    for name, factor in factors.items():
        out[name] = (out[name] * factor).astype(out[name].dtype)
    return out
```

```python
from contextlib import ExitStack

import concourse.bass as bass
from concourse import mybir

F32 = mybir.dt.float32
F32R = mybir.dt.float32r
BF16 = mybir.dt.bfloat16
I32 = mybir.dt.int32
ALU = mybir.AluOpType
ACT = mybir.ActivationFunctionType
AX = mybir.AxisListType
ds = bass.ds

B, T, D, F, SC = 2, 1024, 256, 1024, 77
P = 128
TOK = B * T
NT = TOK // P
TB = T // P
CH = 512
NC = TOK // CH
KT = D // P

ROWS_L0 = ["bv", "bcv", "b2", "g1", "be1", "g2", "be2", "gf", "bf"]
ROWS_L1 = ["bv0", "bv1", "bv2", "gamma0", "gamma1", "gamma2", "beta0", "beta1", "beta2", "bff0", "bff1", "bff2"]
ROWS_L2 = ["gq", "gkv"]
ROWS_L3 = ["bout", "g1", "beta1", "bff2", "g2", "beta2"]
COLS = {"L0q": 0, "L0k": 2, "L0c": 4, "L0f": 6, "L1q": 14, "L1k": 20, "L3f": 26}
NCOLS = 34

MASKED = -1.0e37
NEG1 = -4294967296.0
NEG3_ROUND = -9.972771014849226e+19
LOWEST = -3.0e38

Q_PART = [0, 0, 0, 1, 1, 2]
K_PART = [0, 1, 2, 0, 1, 0]
K16 = 16 * len(Q_PART)
M_ROWS = 3
SEMAPHORES = 18


class LoadSems:
    def __init__(self, s):
        (self.x, self.w0, self.w1a, self.w1b, self.w1c, self.w2, self.w3, self.ctx, self.masks, self.cleared,
         self.out) = s


class NormSems:
    def __init__(self, s):
        self.step, self.var_ready, self.std_ready, self.normed = s


class TurnSems:
    def __init__(self, s):
        self.turned, self.taken = s


class SquareSems:
    def __init__(self, s):
        self.product2, self.taken2 = s


class FeedForwardSems:
    def __init__(self, s):
        self.hid_product, self.hid_ready, self.hid_used, self.added = s


class KeyMaskSems:
    def __init__(self, s):
        self.row_ready, self.turned, self.row_cast, self.stored, self.spread = s


class ProjectSems:
    def __init__(self, s):
        self.product, self.evacuated, self.split, self.step, self.v_product, self.v_taken, self.v_ready = s[0:7]
        self.stored, self.v_stored = s[7:9], s[9:11]


class AttentionSems:
    def __init__(self, s):
        (self.s_ready, self.p_ready, self.gated, self.pv_tile, self.copied, self.chunk_ready, self.chunk_free,
         self.max_ready, self.max_split, self.cleared, self.sending) = s[0:11]
        self.loaded = s[11:13]


class FeatureItem:
    def __init__(self, mms, n, func, bias, src, dst):
        self.mms, self.n, self.func, self.bias, self.src, self.dst = mms, n, func, bias, src, dst


class ValueItem:
    def __init__(self, mms, p, row, g, dst):
        self.mms, self.p, self.row, self.g, self.dst = mms, p, row, g, dst


class KeyTile:
    def __init__(self, c, kind, j, diag, q0, first, last, index):
        self.c, self.kind, self.j, self.diag, self.q0 = c, kind, j, diag, q0
        self.first, self.last, self.index = first, last, index


class Attention:
    def __init__(self, dh, n, ctx, self_keys, causal, window, scale, masked, query_mask):
        self.dh, self.n, self.ctx, self.self, self.causal = dh, n, ctx, self_keys, causal
        self.window, self.scale, self.masked, self.query_mask = window, scale, masked, query_mask


class MaxRows:
    def __init__(self, sems):
        self.total, self.sems = 0, sems


class Weights:
    def __init__(self, qkv=None, ckv=None, w1=None, w2=None, out=None, bd=None):
        self.qkv, self.ckv, self.w1, self.w2, self.out, self.bd = qkv, ckv, w1, w2, out, bd


def build(nc, a, out):
    with ExitStack() as ctx:
        program(nc, ctx, a, out)


def program(nc, ctx, a, out):
    def sb(name, shape, dt=F32):
        return ctx.enter_context(nc.sbuf_tensor(name, shape, dt))

    def lasting(prefix, n):
        return [ctx.enter_context(nc.semaphore(f"{prefix}_{i}")) for i in range(n)]

    sets = [[ctx.enter_context(nc.semaphore(f"set{r}_{i}")) for i in range(SEMAPHORES)] for r in range(3)]
    taken = {}

    def sems(stage, kind, count):
        n = taken.get(stage, 0)
        taken[stage] = n + count
        assert taken[stage] <= SEMAPHORES
        return kind(sets[stage % 3][n:n + count])

    def dram(name, shape, dt):
        return nc.dram_tensor(name, shape, dt, kind="Internal").ap()

    X = sb("x_res", [P, NT, D])
    Y = sb("y_tok", [P, NT * D])
    XT = sb("x_feat", [P, NT * D])
    WA = sb("w_even", [P, 6656])
    WB = sb("w_odd", [P, 4096])
    RA = sb("rows_even", [P, len(ROWS_L0), D])
    RB = sb("rows_odd", [P, len(ROWS_L1), D])
    STK = sb("stacks", [P, 2, 8192], F32R)
    VS = sb("v_group", [P, 2, 1152])
    OT = sb("o_feat", [P, CH])
    OD = sb("o_denom", [64, CH])
    SCR = sb("scratch", [P, CH])
    MB = sb("mask_rows", [P, TOK], BF16)
    COL = sb("cols", [P, NCOLS])
    CTXN = sb("ctx_tok", [P, B, D])
    CTXT = sb("ctx_feat", [P, KT, B * SC])
    ID = sb("ident", [P, P])
    IDB = sb("ident_bf", [P, P], BF16)
    CM_S = sb("causal_q_rows", [P, P], BF16)
    CM_T = sb("causal_k_rows", [P, P], BF16)
    ONES = sb("ones", [P, 32])
    ONESC = sb("ones_ctx", [P, 32])
    STATS = sb("stats", [P, NT, 6])
    MV = sb("mean_var", [P, NT, 2])
    VE = sb("var_eps", [P, NT])
    SD = sb("std", [P, NT])
    RS = sb("rstd", [P, NT])
    MXP = sb("max_parts", [P, 96])
    MX = sb("max_rows", [P, 32])
    MT = sb("neg_max", [32, P])
    MP = sb("neg_max_parts", [32, 2, 3, P], BF16)
    MPR = sb("neg_max_parts_r", [16, 2, 2, P], F32R)
    RC = sb("recip", [P, 16])
    KC = sb("ctx_key_sum", [P, B])
    KZ = sb("key_zero", [P, NT])
    KB = sb("key_bias", [P, NT])
    QM = sb("query_mask", [P, NT])
    KSUM = sb("key_sum", [P, NT])
    KZB = sb("key_zero_rows", [NT, P], BF16)
    MI = sb("mask_int", [P, B * SC + B], I32)
    POS = sb("position", [P, 1])
    POSI = sb("position_int", [P, 1], I32)
    PS = ctx.enter_context(nc.psum_tensor("banks", [P, 8, CH], F32))

    X2 = X[:, :, :].rearrange("p t d -> p (t d)")
    Y3 = Y[:, :].rearrange("p (t d) -> p t d", d=D)
    XTF = XT[:, :].rearrange("p (k n) -> p k n", k=KT)
    PB = XT[:, :].rearrange("p (s r h n) -> p s r h n", s=2, r=2, h=2)

    Q3 = dram("q_parts", (3, B * D, T), BF16)
    K3 = dram("k_parts", (3, B * D, T), BF16)
    C3 = dram("kctx_parts", (3, B * D, SC), BF16)
    Q2 = dram("q_parts_r", (2, B * D, T), F32)
    K2 = dram("k_parts_r", (2, B * D, T), F32)
    C2 = dram("kctx_parts_r", (2, B * D, SC), F32)
    V16 = dram("v16", (B, 4, P, 9, 128), F32)
    V64 = dram("v64", (B, 2, P, 8, 128), F32)
    KM = dram("key_mask_row", (NT, P), BF16)

    stage_done = ctx.enter_context(nc.semaphore("stage_done"))
    stages = {}

    def next_stage(e, who):
        e.drain().then_inc(stage_done, 1)
        stages[who] = stages.get(who, 0) + 1
        e.wait_ge(stage_done, 5 * stages[who])
        if who == "gpsimd":
            for sem in sets[(stages[who] - 1) % 3]:
                e.sem_clear(sem)

    def need(e, sem, value):
        if not (isinstance(value, int) and value <= 0):
            e.wait_ge(sem, value)

    def wview(W, off, k, n):
        return W[:, off:off + k * n].rearrange("p (k n) -> p k n", k=k)

    W0 = Weights(qkv=wview(WA, 0, KT, 768), ckv=wview(WA, 1536, KT, 512),
                         w1=wview(WA, 2560, KT, F), w2=wview(WA, 4608, F // P, D))
    W1 = [{n: wview(WB, (l % 2 * 4 + j) * 512, KT, D) for j, n in enumerate("qkvf")} for l in range(3)]
    W2 = {n: wview(WB, 2048 + j * 512, KT, D) for j, n in enumerate("qkvo")}
    W3 = Weights(w1=wview(WA, 0, KT, F), w2=wview(WA, 2048, F // P, D), out=wview(WA, 4096, KT, D),
                         bd=[WA[:, 4608 + 128 * j:4608 + 128 * (j + 1)] for j in range(3)])

    def row(R, names, name):
        return R[:, names.index(name), :]

    ld = LoadSems(lasting("load", 11))

    def kp(w):
        return w.rearrange("(k p) n -> p k n", p=P)

    def load_sync(e):
        e.dma_start(X[:, :, :], a["x"].rearrange("b (t p) d -> p (b t) d", p=P)).then_inc(ld.x, 16)
        e.dma_start(CTXN[0:SC, :, :], a["ctx"].rearrange("b s d -> s b d")).then_inc(ld.x, 16)
        e.dma_start(COL[:, :], a["cols"]).then_inc(ld.x, 16)
        e.dma_start(RA[:, :, :], a["rows0"].partition_broadcast(P)).then_inc(ld.x, 16)
        for w, name in ((W0.qkv, "w_qkv"), (W0.ckv, "w_ckv"), (W0.w1, "w1"), (W0.w2, "w2")):
            e.dma_start(w, kp(a[name])).then_inc(ld.w0, 16)
        e.dma_start(RB[:, :, :], a["rows1"].partition_broadcast(P)).then_inc(ld.x, 16)
        load_layer(e, 0, ld.w1a)
        load_layer(e, 1, ld.w1b)
        e.wait_ge(ld.x, 80)
        e.wait_ge(ld.w0, 64)

    def load_layer(e, l, sem):
        for n in "qkvf":
            e.dma_start(W1[l][n], kp(a["W" + n][l])).then_inc(sem, 16)

    def load_block2(e):
        for n in "qkvo":
            e.dma_start(W2[n], kp(a["W2" + n])).then_inc(ld.w2, 16)

    def load_block3(e):
        e.dma_start(RA[:, 0:8, :], a["rows23"].partition_broadcast(P)).then_inc(ld.w3, 16)
        for w, n in ((W3.w1, "w3_1"), (W3.w2, "w3_2"), (W3.out, "w3_out")):
            e.dma_start(w, kp(a[n])).then_inc(ld.w3, 16)
        e.wait_ge(ld.cleared, 1)
        for j, n in enumerate("qkv"):
            for h in range(8):
                e.dma_start(W3.bd[j][16 * h:16 * h + 16, 16 * h:16 * h + 16], a["w3" + n]).then_inc(ld.w3, 16)
        e.dma_start(MI[:, 0:B * SC], a["mask"].rearrange("b s -> (b s)").partition_broadcast(P)).then_inc(ld.w3, 16)
        e.dma_start(MI[0:SC, B * SC:B * SC + B], a["mask"].rearrange("b s -> s b"), allow_slow_non_contiguous=True).then_inc(ld.w3, 16)
    W3_LOADS = 4 + 24 + 2

    def load_pool(e):
        fill(e, ID[:, :], 0.0)
        fill(e, IDB[:, :], 0.0)
        fill(e, CM_S[:, :], 0.0)
        fill(e, CM_T[:, :], 0.0)
        fill(e, ONES[:, :], 1.0)
        fill(e, ONESC[:, :], 1.0)
        fill(e, KB[:, :], 0.0)
        e.iota(POSI[:, :], pattern=[[0, 1]], base=0, channel_multiplier=1)
        e.drain()
        e.tensor_copy(POS[:, :], POSI[:, :])
        e.drain()
        for m in (ID, IDB):
            e.affine_select(out=m[:, :], in_=m[:, :], compare_op=ALU.not_equal, fill=1.0,
                            base=0, pattern=[[-1, P]], channel_multiplier=1)
            e.drain()
        e.drain()
        e.affine_select(out=ONESC[:, :], in_=ONESC[:, :], compare_op=ALU.is_ge, fill=0.0,
                        base=SC - 1, pattern=[[0, 32]], channel_multiplier=-1)
        e.drain()
        e.affine_select(out=CM_S[:, :], in_=CM_S[:, :], compare_op=ALU.is_ge, fill=MASKED,
                        base=0, pattern=[[-1, P]], channel_multiplier=1)
        e.drain()
        e.affine_select(out=CM_T[:, :], in_=CM_T[:, :], compare_op=ALU.is_ge, fill=MASKED,
                        base=0, pattern=[[1, P]], channel_multiplier=-1)

    def ln(stage):
        return sems(stage, NormSems, 4)

    def ln_vector(e, s, src, dst, g, b, mode, eps, nt=NT, p=P, per=4):
        n = 0
        for t in range(nt):
            e.bn_stats(STATS[0:p, t, :], src[0:p, t, :]).then_inc(s.step, 1)
        n += nt
        e.wait_ge(s.step, n)
        for t in range(nt):
            e.bn_aggr(MV[0:p, t, :], STATS[0:p, t, :]).then_inc(s.step, 1)
        n += nt
        e.wait_ge(s.step, n)
        mean, var = MV[0:p, 0:nt, 0], MV[0:p, 0:nt, 1]
        if mode == "rms":
            e.tensor_tensor(VE[0:p, 0:nt], mean, mean, ALU.mult).then_inc(s.step, 1)
            e.wait_ge(s.step, n + 1)
            e.scalar_tensor_tensor(VE[0:p, 0:nt], VE[0:p, 0:nt], eps, var, ALU.add, ALU.add).then_inc(s.var_ready, 1)
            n += 1
        elif mode == "unbiased":
            e.tensor_scalar(VE[0:p, 0:nt], var, D / (D - 1.0), None, ALU.mult).then_inc(s.var_ready, 1)
        else:
            e.tensor_scalar(VE[0:p, 0:nt], var, eps, None, ALU.add).then_inc(s.var_ready, 1)
        e.wait_ge(s.std_ready, 1)
        if mode == "unbiased":
            e.tensor_scalar(SD[0:p, 0:nt], SD[0:p, 0:nt], eps, None, ALU.add).then_inc(s.step, 1)
            n += 1
            e.wait_ge(s.step, n)
        e.reciprocal(RS[0:p, 0:nt], SD[0:p, 0:nt]).then_inc(s.step, 1)
        n += 1
        e.wait_ge(s.step, n)
        for c in range(nt // per):
            for t in range(per * c, per * c + per):
                if mode == "rms":
                    e.tensor_scalar(dst[0:p, t, :], src[0:p, t, :], RS[0:p, t:t + 1], None, ALU.mult).then_inc(s.step, 1)
                else:
                    e.tensor_scalar(dst[0:p, t, :], src[0:p, t, :], MV[0:p, t, 0:1], RS[0:p, t:t + 1],
                                    ALU.subtract, ALU.mult).then_inc(s.step, 1)
            n += per
            e.wait_ge(s.step, n)
            d = dst[0:p, per * c:per * c + per, :]
            gb = g[0:p, :].unsqueeze(1).broadcast_to([p, per, D])
            if b is None:
                e.tensor_tensor(d, d, gb, ALU.mult).then_inc(s.normed, 1)
            else:
                e.tensor_tensor(d, d, gb, ALU.mult).then_inc(s.step, 1)
                n += 1
                e.wait_ge(s.step, n)
                e.tensor_tensor(d, d, b[0:p, :].unsqueeze(1).broadcast_to([p, per, D]), ALU.add).then_inc(s.normed, 1)

    def ln_scalar(e, s, nt=NT, p=P):
        e.wait_ge(s.var_ready, 1)
        e.activation(SD[0:p, 0:nt], VE[0:p, 0:nt], ACT.Sqrt).then_inc(s.std_ready, 1)

    def turn_tensor(e, s, src, ready=None, ctx_taken=None):
        for c in range(NC):
            if c == 3 and ctx_taken is not None:
                e.wait_ge(ctx_taken, 1)
            if ready is not None:
                e.wait_ge(ready, c + 1)
            for k in range(KT):
                for j in range(4):
                    t = e.transpose(PS[:, 2 * c + k, j * P:(j + 1) * P], src(4 * c + j, k), ID[:, :])
                t.then_inc(s.turned, 1)

    def turn_scalar(e, s):
        for c in range(NC):
            for k in range(KT):
                e.wait_ge(s.turned, 2 * c + k + 1)
                e.activation(XTF[:, k, c * CH:(c + 1) * CH], PS[:, 2 * c + k, :], ACT.Copy).then_inc(s.taken, 1)

    def tokens(src3):
        return lambda t, k: src3[:, t, k * P:(k + 1) * P]

    def turn_ctx_tensor(e, s, src, ready=None, value=1):
        if ready is not None:
            e.wait_ge(ready, value)
        for b in range(B):
            for k in range(KT):
                e.transpose(PS[:, 7, (k * B + b) * P:(k * B + b) * P + SC], src[0:SC, b, k * P:(k + 1) * P],
                            ID[0:SC, 0:SC]).then_inc(s.turned, 1)

    def turn_ctx_scalar(e, s):
        e.wait_ge(s.turned, B * KT)
        e.activation(CTXT[:, :, :].rearrange("p k (b n) -> p k b n", b=B),
                     PS[:, 7, :].rearrange("p (k b n) -> p k b n", k=KT, b=B)[:, :, :, 0:SC],
                     ACT.Copy).then_inc(s.taken, 1)

    RBUF = Y[:, 0:1024].rearrange("p (s n) -> p s n", s=2)
    P3 = Y[:, 1024:2560].bitcast(BF16).rearrange("p (s k n) -> p s k n", s=2, k=3)
    VT = Y[:, 2560:3584].rearrange("p (s n) -> p s n", s=2)
    P2 = STK[:, 0, 0:2048].rearrange("p (s k n) -> p s k n", s=2, k=2)

    def project_tensor(e, s, feat, vals):
        for i, it in enumerate(feat):
            need(e, s.evacuated, i - 3)
            for j, (l, r) in enumerate(it.mms):
                m = e.matmul(PS[0:P, i % 4, 0:it.n], l, r, start=(j == 0), stop=(j == len(it.mms) - 1))
            m.then_inc(s.product, 1)
        for i, v in enumerate(vals):
            need(e, s.v_taken, i - 3)
            for sl, mms in v.mms:
                for j, (l, r) in enumerate(mms):
                    m = e.matmul(PS[0:v.p, 4 + i % 4, sl], l, r, start=(j == 0), stop=(j == len(mms) - 1))
            m.then_inc(s.v_product, 1)

    def project_scalar(e, s, feat):
        for i, it in enumerate(feat):
            e.wait_ge(s.product, i + 1)
            need(e, s.split, i - 1)
            e.activation(RBUF[:, i % 2, 0:it.n], PS[:, i % 4, 0:it.n], it.func, bias=it.bias).then_inc(s.evacuated, 1)

    def project_vector(e, s, feat, vals, parts, relu):
        steps = 0
        def step(ins):
            nonlocal steps
            ins.then_inc(s.step, 1)
            steps += 1
            e.wait_ge(s.step, steps)
        vw = 32 if parts == 3 else 64
        hv = D // (16 if parts == 3 else 64)
        if parts == 3:
            step(e.memset(VT[:, :, :], 1.0))
        def value(i):
            v = vals[i]
            e.wait_ge(s.v_product, i + 1)
            if i >= 2:
                e.wait_ge(s.v_stored[i % 2], 16 * (i // 2))
            dst = VT[0:v.p, i % 2, 0:hv * vw].rearrange("p (h w) -> p h w", w=vw)[:, :, 0:D // hv]
            src = PS[0:v.p, 4 + i % 4, 0:D].rearrange("p (h w) -> p h w", h=hv)
            if v.row is None:
                e.tensor_copy(dst, src).then_inc(s.v_taken, 1)
            else:
                r = v.row[0:v.p, :].rearrange("p (h w) -> p h w", h=hv)
                e.tensor_tensor(dst, src, r, ALU.add).then_inc(s.v_taken, 1)
            if relu:
                e.wait_ge(s.v_taken, i + 1)
                e.tensor_scalar(dst, dst, 0.0, None, ALU.max).then_inc(s.v_ready, 1)
        for i, it in enumerate(feat):
            e.wait_ge(s.evacuated, i + 1)
            if i >= 2:
                e.wait_ge(s.stored[i % 2], 16 * parts * (i // 2))
            r = RBUF[:, i % 2, 0:it.n]
            if parts == 3:
                p1, p2, p3 = (P3[:, i % 2, k, 0:it.n] for k in range(3))
                step(e.tensor_copy(p1, r))
                step(e.tensor_tensor(r, r, p1, ALU.subtract))
                step(e.tensor_copy(p2, r))
                e.tensor_tensor(p3, r, p2, ALU.subtract).then_inc(s.split, 1)
            else:
                hi, lo = P2[:, i % 2, 0, 0:it.n], P2[:, i % 2, 1, 0:it.n]
                step(e.tensor_copy(hi, r))
                e.tensor_tensor(lo, r, hi.bitcast(F32), ALU.subtract).then_inc(s.split, 1)
        for i in range(len(vals)):
            value(i)

    def project_sync(e, s, feat, vals, parts, relu):
        for i, it in enumerate(feat):
            e.wait_ge(s.split, i + 1)
            for k in range(parts):
                src = (P3 if parts == 3 else P2.bitcast(F32))[:, i % 2, k, 0:it.n]
                e.dma_start(it.dst(k), it.src(src)).then_inc(s.stored[i % 2], 16)
        for i, v in enumerate(vals):
            e.wait_ge(s.v_ready if relu else s.v_taken, i + 1)
            e.dma_start(v.dst, VT[0:v.p, i % 2, 0:v.g * 128].rearrange("p (g w) -> p g w", g=v.g)).then_inc(s.v_stored[i % 2], 16)
        for u in range(2):
            e.wait_ge(s.stored[u], 16 * parts * ((len(feat) + 1 - u) // 2))
            e.wait_ge(s.v_stored[u], 16 * ((len(vals) + 1 - u) // 2))

    def project(stage):
        return sems(stage, ProjectSems, 11)

    def q_items(w, off, dst, bias, func, diag=False):
        its = []
        for c in range(NC):
            b, half = c // 2, c % 2
            for m in range(KT):
                if diag:
                    mms = [(w, XTF[:, m, c * CH:(c + 1) * CH])]
                else:
                    mms = [(w[:, k, off + m * P:off + (m + 1) * P], XTF[:, k, c * CH:(c + 1) * CH]) for k in range(KT)]
                its.append(FeatureItem(
                    mms=mms, n=CH, func=func, bias=0.0 if bias is None else COL[:, bias + m:bias + m + 1],
                    src=lambda x: x,
                    dst=lambda k, b=b, m=m, h=half: dst[k, b * D + m * P:b * D + (m + 1) * P, h * CH:(h + 1) * CH]))
        return its

    def c_items(w, off, dst, bias, func, diag=False):
        its = []
        for m in range(KT):
            if diag:
                mms = [(w, CTXT[:, m, :])]
            else:
                mms = [(w[:, k, off + m * P:off + (m + 1) * P], CTXT[:, k, :]) for k in range(KT)]
            its.append(FeatureItem(
                mms=mms, n=B * SC, func=func, bias=0.0 if bias is None else COL[:, bias + m:bias + m + 1],
                src=lambda x: x.rearrange("p (b n) -> p b n", b=B),
                dst=lambda k, m=m: dst[k].rearrange("(b f) n -> f b n", b=B)[m * P:(m + 1) * P]))
        return its

    def v_items(w, off, rowv, dst, ngroup, tile0):
        its = []
        for t in range(NT):
            b = t // TB
            mms = [(XTF[:, k, t * P:(t + 1) * P], w[:, k, off:off + D]) for k in range(KT)]
            its.append(ValueItem(mms=[(slice(0, D), mms)], p=P, row=rowv, g=ngroup,
                                       dst=dst[b, :, :, t % TB + tile0, :].rearrange("g p w -> p g w")))
        return its

    def vc_items(w, off, rowv, dst, ngroup, diag=False):
        its = []
        for b in range(B):
            lhs = [CTXT[:, k, b * SC:(b + 1) * SC] for k in range(KT)]
            if diag:
                mms = [(slice(k * P, (k + 1) * P), [(lhs[k], w)]) for k in range(KT)]
            else:
                mms = [(slice(0, D), [(lhs[k], w[:, k, off:off + D]) for k in range(KT)])]
            its.append(ValueItem(mms=mms, p=SC, row=rowv, g=ngroup,
                                       dst=dst[b, :, 0:SC, 0, :].rearrange("g p w -> p g w")))
        return its

    m_rows = MaxRows(lasting("max_rows_slot", 2))

    def attention(stage, dh, groups, ctx_keys=False, self_keys=False, causal=False, window=False, scale=1.0,
                  masked=False, query_mask=False):
        A = Attention(dh=dh, n=groups, ctx=ctx_keys, self_keys=self_keys, causal=causal, window=window, scale=scale,
                            masked=masked, query_mask=query_mask)
        A.s = sems(stage, AttentionSems, 13)
        A.nh = 4 if dh == 16 else 2
        A.loop = not masked
        A.pairs = A.nh // 2
        A.tiles = []
        for c in range(2):
            n_self = 0 if not self_keys else 4 * (c + 1) if causal else TB
            keys = [("ctx", 0)] * ctx_keys + [("self", j) for j in range(n_self)]
            for i, (kind, j) in enumerate(keys):
                diag = causal and kind == "self" and j >= 4 * c
                A.tiles.append(KeyTile(c=c, kind=kind, j=j, diag=diag, q0=P * (j - 4 * c) if diag else 0,
                                               first=i == 0, last=i == len(keys) - 1, index=len(A.tiles)))
        A.nt = len(A.tiles)
        A.nt0 = sum(t.c == 0 for t in A.tiles)
        A.steps = A.nt * A.pairs
        A.chunks = []
        if not window:
            for h in range(A.nh):
                if ctx_keys:
                    A.chunks += [("ctx", h, 0, 0), ("ctx", h, 4, 0)]
                if self_keys:
                    A.chunks += [("self", h, i, half) for i in range(TB) for half in range(2)
                                 if not causal or i * P >= half * CH]
        A.a_per = len(A.chunks) + (not window)
        A.parts = 3 if dh == 16 else 2
        A.rows_before = m_rows.total
        m_rows.total += 0 if window else 16 * A.parts * (groups // 2)
        A.outs = ("E",) if dh == 16 else ("D", "E")
        A.loads = 6 * (1 + ctx_keys + self_keys) + 1 + self_keys if dh == 16 else 7
        return A

    def order(A, what):
        if what == "first":
            return [[("A", 0, i) for i in range(len(A.chunks))] + [("M", 0, 0)] * (not A.window)]
        if what == "tail":
            return [[("C", -1, 1)] + [(w, -1, 1) for w in A.outs]]
        o = [[] for _ in range(A.nt + 1)]
        if what != "step0":
            o[0].append(("C", -1, 1))
            o[1] += [(w, -1, 1) for w in A.outs]
        if what != "last":
            for i in range(len(A.chunks)):
                o[i * A.nt // len(A.chunks)].append(("A", 1, i))
        o[min(A.nt0 + 1, A.nt)].insert(0, ("C", 0, 0))
        o[min(A.nt0 + 2, A.nt)] += [(w, 0, 0) for w in A.outs]
        if what != "last" and not A.window:
            o[A.nt].append(("M", 1, 0))
        return o

    def numbered(A, what, g, u):
        ne = len(A.outs)
        if what == "first":
            at = lambda g: 0
        elif what == "step0":
            at = lambda g: A.a_per
        elif what == "tail":
            at = lambda g: g * (A.a_per + 2 * ne) - ne
        else:
            at = lambda g: g * (A.a_per + 2 * ne) + (A.a_per - ne)
        base, parity = at(g), at(u) % 2
        n, res = 0, []
        for items in order(A, what):
            r = []
            for w, dg, i in items:
                r.append((w, dg, i, base + n, 6 + (parity + n) % 2))
                n += w != "C"
            res.append(r)
        return res

    def each_group(A, e, run):
        run("first", 0, 0, 0)
        run("step0", 0, 0, 0)
        def two(i):
            run("step", i * 2 + 1, 1, i)
            run("step", i * 2 + 2, 0, i + 1)
        if A.loop:
            with e.Fori(0, (A.n - 2) // 2) as i:
                two(i)
        else:
            for i in range((A.n - 2) // 2):
                two(i)
        run("last", A.n - 1, 1, (A.n - 1) // 2)
        run("tail", A.n, 0, A.n // 2)

    def next_slot(g, u, use):
        return g + 1, 1 - u, use if u == 0 else use + 1

    def slot16(u):
        q = STK[:, u, 0:2048].bitcast(BF16).rearrange("p (h n) -> p h n", h=4)
        k = STK[:, u, 2048:4352].bitcast(BF16).rearrange("p (h n) -> p h n", h=4)
        return q, k

    def slot64(u):
        return [STK[:, u, 2048 * i:2048 * (i + 1)].rearrange("p (h n) -> p h n", h=2) for i in range(4)]

    def attention_sync(e, A):
        s = A.s
        def load(g, u):
            sem = s.loaded[u]
            if A.dh == 16:
                q, k = slot16(u)
                def rows(parts, part):
                    return parts[part, ds(g * 64, 64), :].rearrange("(h d) n -> d h n", h=4)
                for i in range(len(Q_PART)):
                    sl = slice(16 * i, 16 * i + 16)
                    e.dma_start(q[sl, :, :], rows(Q3, Q_PART[i])).then_inc(sem, 16)
                    if A.ctx:
                        e.dma_start(k[sl, :, 0:SC], rows(C3, K_PART[i])).then_inc(sem, 16)
                    if A.self:
                        e.dma_start(k[sl, :, P:P + T], rows(K3, K_PART[i])).then_inc(sem, 16)
                v = V16.rearrange("b g p t w -> (b g p) (t w)")
                if A.self:
                    e.dma_start(VS[:, u, 128:1152], v[ds(g * P, P), 128:1152]).then_inc(sem, 16)
                e.dma_start(VS[0:SC, u, 0:128], v[ds(g * P, SC), 0:128]).then_inc(sem, 16)
            else:
                qa, qb, ka, kb = (x.bitcast(F32) for x in slot64(u))
                def rows(parts, part):
                    return parts[part, g * P:(g + 1) * P, :].rearrange("(h d) n -> d h n", h=2)
                k, n = (K2, T) if A.self else (C2, SC)
                for dst, src in ((qa[0:64], rows(Q2, 0)), (qa[64:P], rows(Q2, 1)), (qb[0:64], rows(Q2, 0)),
                                 (ka[0:64, :, 0:n], rows(k, 0)), (ka[64:P, :, 0:n], rows(k, 0)),
                                 (kb[0:64, :, 0:n], rows(k, 1))):
                    e.dma_start(dst, src).then_inc(sem, 16)
                v = V64.rearrange("b g p t w -> (b g) p (t w)")
                if A.self:
                    e.dma_start(VS[:, u, 0:1024], v[g]).then_inc(sem, 16)
                else:
                    e.dma_start(VS[0:SC, u, 0:128], v[g, 0:SC, 0:128]).then_inc(sem, 16)
        e.wait_ge(s.cleared, 1)
        load(0, 0)
        load(1, 1)
        def two(i):
            for u in range(2):
                e.wait_ge(s.pv_tile, (i * 2 + u + 1) * A.nt)
                load(i * 2 + 2 + u, u)
        if A.loop:
            with e.Fori(0, (A.n - 2) // 2) as i:
                two(i)
        else:
            for i in range((A.n - 2) // 2):
                two(i)

    def fill(e, where, value):
        e.memset(where, value)
        e.drain()

    def attention_gpsimd(e, A):
        s = A.s
        for u in range(2):
            fill(e, VS[:, u, :], 0.0)
            if A.dh == 16:
                k = slot16(u)[1]
                fill(e, k[:, :, 0:P], 0.0)
                fill(e, k[K16:K16 + M_ROWS, :, 0:SC], 1.0)
                if A.self:
                    fill(e, k[K16:K16 + M_ROWS, :, P:P + T], 1.0)
            else:
                qa, qb, ka, kb = (x.bitcast(F32) for x in slot64(u))
                fill(e, qb[64:96, :, :], 0.0)
                if A.ctx:
                    fill(e, ka[:, :, 0:P], 0.0)
                    fill(e, kb[0:64, :, 0:P], 0.0)
                fill(e, kb[64:96, :, :], 0.0)
                fill(e, kb[64:66, :, 0:T if A.self else SC], 1.0)
        e.drain().then_inc(s.cleared, 1)
        if A.window:
            return
        def run(what, g, u, use):
            if what in ("last", "tail"):
                return
            if what != "first":
                g, u, use = next_slot(g, u, use)
            e.wait_ge(s.loaded[u], (use + 1) * 16 * A.loads)
            e.wait_ge(s.max_split, g + 1)
            e.sem_inc(s.sending, 1)
            for k in range(A.parts):
                if A.dh == 16:
                    dst, src = slot16(u)[0][K16 + k:K16 + k + 1], MP[0:32, u, k, :]
                else:
                    dst, src = slot64(u)[1][64 + k:65 + k].bitcast(F32), MPR[0:16, u, k, :].bitcast(F32)
                e.dma_start(dst.rearrange("o h (t n) -> o (h t) n", n=P), src).then_inc(m_rows.sems[u], 16)
        each_group(A, e, run)

    def attention_tensor(e, A):
        s = A.s
        V = VS[:, :, :].rearrange("p u (t h w) -> p u t h w", t=9, h=4) if A.dh == 16 else \
            VS[:, :, 0:1024].rearrange("p u (t h w) -> p u t h w", t=8, h=2)
        e.wait_ge(s.cleared, 1)

        def chunk(w, dg, i, n, bank, g, u):
            need(e, s.chunk_free, n - 1)
            if w == "A":
                v = u if dg == 0 else 1 - u
                kind, h, qt, half = A.chunks[i]
                q, k = slot16(v) if A.dh == 16 else slot64(v)[0::2]
                rows = K16 if A.dh == 16 else P
                if kind == "ctx":
                    wide = SC if A.dh == 16 else SC + 1
                    for j in range(4):
                        m = e.matmul(PS[:, bank, j * 80:j * 80 + wide], q[0:rows, h, (qt + j) * P:(qt + j + 1) * P],
                                     k[0:rows, h, 0:wide], start=True, stop=True, skip_group_check=True)
                else:
                    wide = min(CH, (qt + 1) * P - half * CH) if A.causal else CH
                    diag = A.causal and qt // 4 == half
                    k0 = half * CH + (P if A.dh == 16 else 0)
                    m = e.matmul(PS[:, bank, 0:wide], q[0:rows, h, qt * P:(qt + 1) * P], k[0:rows, h, k0:k0 + wide],
                                 start=True, stop=not diag, skip_group_check=True)
                    if diag:
                        m = e.matmul(PS[:, bank, wide - P:wide], IDB[:, :], CM_S[:, :], start=False, stop=True,
                                     skip_group_check=True)
            elif w == "M":
                e.wait_ge(s.max_ready, g + dg + 1)
                m = e.transpose(PS[0:A.nh * TB, bank, 0:P], MX[:, 0:A.nh * TB], ID[:, :])
            else:
                e.wait_ge(s.copied, (g + dg) * 2 + i + 1)
                rows = OT[:, :] if w == "E" else OD[:, :]
                p = P if w == "E" else 64
                for j in range(4):
                    m = e.transpose(PS[:, bank, j * p:(j + 1) * p], rows[:, j * P:(j + 1) * P], ID[0:p, 0:p])
            m.then_inc(s.chunk_ready, 1)

        def scores(t, r, g, u):
            st = t.index * A.pairs + r
            need(e, s.gated if A.window else s.p_ready, g * A.steps + (st - 1))
            for hh in range(2):
                h, bank = 2 * r + hh, 2 * (st % 2) + hh
                o = PS[:, bank, 0:CH - t.q0]
                qs = slice(t.c * CH + t.q0, (t.c + 1) * CH)
                if A.dh == 16:
                    q, k = slot16(u)
                    rows = K16 + M_ROWS * (not A.window)
                    k0 = 0 if t.kind == "ctx" else P + t.j * P
                    m = e.matmul(o, k[0:rows, h, k0:k0 + P], q[0:rows, h, qs], start=True, stop=not t.diag,
                                 skip_group_check=True)
                    if t.diag:
                        m = e.matmul(PS[:, bank, 0:P], IDB[:, :], CM_T[:, :], start=False, stop=True, skip_group_check=True)
                else:
                    qa, qb, ka, kb = slot64(u)
                    ks = slice(t.j * P, (t.j + 1) * P)
                    e.matmul(o, ka[:, h, ks], qa[:, h, qs], start=True, stop=False)
                    m = e.matmul(o, kb[0:96, h, ks], qb[0:96, h, qs], start=False, stop=True)
            m.then_inc(s.s_ready, 1)

        def with_v(t, g, u):
            e.wait_ge(s.p_ready, g * A.steps + (t.index + 1) * A.pairs)
            if t.first:
                need(e, s.copied, (g - 1) * 2 + t.c + 1 if A.dh == 16 else g * 2 + t.c)
            bank = 4 + t.c if A.dh == 16 else 4
            vt = t.j + (1 if t.kind == "self" and A.dh == 16 else 0)
            w = P // A.nh
            for h in range(A.nh):
                m = e.matmul(PS[w * h:w * (h + 1), bank, t.q0:CH], V[:, u, vt, h, :],
                             PB[:, t.index % 2, h // 2, h % 2, 0:CH - t.q0], start=t.first, stop=t.last,
                             skip_group_check=True)
            if A.dh == 64:
                ones = ONESC if t.kind == "ctx" else ONES
                for h in range(2):
                    m = e.matmul(PS[32 * h:32 * (h + 1), 5, :], ones[:, :], PB[:, t.index % 2, 0, h, :],
                                 start=t.first, stop=t.last, skip_group_check=True)
            m.then_inc(s.pv_tile, 1)

        def run(what, g, u, use):
            work = numbered(A, what, g, u)
            if what == "first":
                e.wait_ge(s.loaded[0], 16 * A.loads)
            elif what in ("step0", "step"):
                _, nu, nuse = next_slot(g, u, use)
                e.wait_ge(s.loaded[nu], (nuse + 1) * 16 * A.loads)
            if what in ("first", "tail"):
                for x in work[0]:
                    if x[0] != "C":
                        chunk(*x, g, u)
                return
            if not A.window:
                e.wait_ge(m_rows.sems[u], (use + 1) * (16 * A.parts) + A.rows_before)
            for i in range(A.nt + 1):
                if i < A.nt:
                    for r in range(A.pairs):
                        scores(A.tiles[i], r, g, u)
                if i > 0:
                    with_v(A.tiles[i - 1], g, u)
                for x in work[i]:
                    if x[0] != "C":
                        chunk(*x, g, u)
        each_group(A, e, run)

    def attention_scalar(e, A):
        s = A.s
        def run(what, g, u, use):
            if what in ("first", "tail"):
                return
            for t in A.tiles:
                for r in range(A.pairs):
                    st = t.index * A.pairs + r
                    e.wait_ge(s.gated if A.window else s.s_ready, g * A.steps + (st + 1))
                    need(e, s.pv_tile, g * A.nt + (t.index - 1))
                    dst = PB[:, t.index % 2, r, :, 0:CH - t.q0]
                    if A.window:
                        e.activation(dst, dst, ACT.Square, scale=A.scale).then_inc(s.p_ready, 1)
                    else:
                        bias = 0.0
                        if A.masked:
                            b = g // (A.n // B)
                            col = b if t.kind == "ctx" else b * TB + t.j
                            bias = KB[:, col:col + 1]
                        e.activation(dst, PS[:, 2 * (st % 2):2 * (st % 2) + 2, 0:CH - t.q0], ACT.Exp, scale=A.scale,
                                     bias=bias).then_inc(s.p_ready, 1)
        each_group(A, e, run)

    def attention_vector(e, A):
        s = A.s
        maxp = MXP[:, 0:A.nh * TB * 3].rearrange("p (h t s) -> p h t s", h=A.nh, t=TB)
        e.memset(MXP[:, :], LOWEST)
        e.drain()

        def gate(t, r, g):
            st = t.index * A.pairs + r
            e.wait_ge(s.s_ready, g * A.steps + (st + 1))
            need(e, s.pv_tile, g * A.nt + (t.index - 1))
            win = MB[:, ds(g // (A.n // B) * T + t.c * CH, CH)].unsqueeze(1).broadcast_to([P, 2, CH])
            e.scalar_tensor_tensor(PB[:, t.index % 2, r, :, :], PS[:, 2 * (st % 2):2 * (st % 2) + 2, :], 0.0, win,
                                   ALU.max, ALU.mult).then_inc(s.gated, 1)

        def part_of_max(i, n, bank, g):
            kind, h, qt, half = A.chunks[i]
            if A.masked:
                need(e, s.chunk_free, n)
            if kind == "ctx":
                src = PS[:, bank, 0:320].rearrange("p (j n) -> p j n", j=4)[:, :, 0:SC]
                if A.masked:
                    m = MB[:, ds(g // (A.n // B) * SC, SC)].unsqueeze(1).broadcast_to([P, 4, SC])
                    tmp = SCR[:, 0:4 * SC].rearrange("p (j n) -> p j n", j=4)
                    e.tensor_tensor(tmp, src, m, ALU.add)
                    e.drain()
                    src = tmp
                e.tensor_reduce(maxp[:, h, qt:qt + 4, 2], src, AX.X, ALU.max).then_inc(s.chunk_free, 1)
            elif A.masked:
                k0 = g // (A.n // B) * T + half * CH
                e.tensor_tensor_reduce(SCR[:, :], PS[:, bank, :], MB[:, k0:k0 + CH], 1.0, LOWEST, ALU.add, ALU.max,
                                       maxp[:, h, qt, half:half + 1]).then_inc(s.chunk_free, 1)
            else:
                wide = min(CH, (qt + 1) * P - half * CH)
                e.tensor_reduce(maxp[:, h, qt, half:half + 1], PS[:, bank, 0:wide], AX.X, ALU.max).then_inc(s.chunk_free, 1)
            if i == len(A.chunks) - 1:
                e.drain()
                e.tensor_reduce(MX[:, 0:A.nh * TB].rearrange("p (h t) -> p h t", h=A.nh), maxp, AX.X, ALU.max)\
                    .then_inc(s.max_ready, 1)

        def split_max(v, bank):
            w = A.nh * TB
            mt = MT[0:w, :]
            e.tensor_scalar(mt, PS[0:w, bank, 0:P], -1.0, None, ALU.mult).then_inc(s.chunk_free, 1)
            e.drain()
            if A.dh == 16:
                p1, p2, p3 = (MP[0:w, v, k, :] for k in range(3))
                e.tensor_copy(p1, mt)
                e.drain()
                e.tensor_tensor(mt, mt, p1, ALU.subtract)
                e.drain()
                e.tensor_copy(p2, mt)
                e.drain()
                e.tensor_tensor(p3, mt, p2, ALU.subtract).then_inc(s.max_split, 1)
            else:
                hi, lo = MPR[0:w, v, 0, :], MPR[0:w, v, 1, :]
                e.tensor_copy(hi, mt)
                e.drain()
                e.tensor_tensor(lo, mt, hi.bitcast(F32), ALU.subtract).then_inc(s.max_split, 1)

        def reciprocal(den, g, c):
            rc = RC[:, 0:4 * A.nh].rearrange("p (j h) -> p j h", j=4)
            if A.window:
                e.tensor_scalar(rc, den, 1e-6, None, ALU.max)
                e.drain()
                den = rc
            r = e.reciprocal(rc, den)
            if A.query_mask:
                t0 = g // (A.n // B) * TB + 4 * c
                e.drain()
                r = e.tensor_tensor(rc, rc, QM[:, t0:t0 + 4].unsqueeze(2).broadcast_to([P, 4, A.nh]), ALU.mult)
            return r

        def output(w, n, bank, g, c):
            if w == "D":
                den = PS[:, bank, 0:256].rearrange("p (j h w) -> p j h w", j=4, h=2)[:, :, :, 0]
                reciprocal(den, g, c).then_inc(s.chunk_free, 1)
                return
            o = PS[:, bank, :].rearrange("p (j h w) -> p j h w", j=4, h=A.nh)
            if A.dh == 16:
                reciprocal(o[:, :, :, 16], g, c)
            e.drain()
            per = A.n // B
            b = g // per
            dst = Y[:, :].rearrange("p (b c j g w) -> p b c j g w", b=B, c=2, j=4, g=per)[
                :, ds(b, 1), c, :, ds(g % per, 1), :].rearrange("p o j q (h w) -> p (o j q) h w", h=A.nh)
            rc = RC[:, 0:4 * A.nh].rearrange("p (j h) -> p j h", j=4).unsqueeze(3).broadcast_to([P, 4, A.nh, A.dh])
            e.tensor_tensor(dst, o[:, :, :, 0:A.dh], rc, ALU.mult).then_inc(s.chunk_free, 1)

        def run(what, g, u, use):
            for idx, items in enumerate(numbered(A, what, g, u)):
                if A.window and what not in ("first", "tail") and idx < A.nt:
                    for r in range(A.pairs):
                        gate(A.tiles[idx], r, g)
                for w, dg, i, n, bank in items:
                    if w == "C":
                        last = A.nt0 if i == 0 else A.nt
                        e.wait_ge(s.pv_tile, (g + dg) * A.nt + last)
                        if A.dh == 64:
                            e.tensor_copy(OD[:, :], PS[0:64, 5, :])
                        e.tensor_copy(OT[:, :], PS[:, 4 + i if A.dh == 16 else 4, :]).then_inc(s.copied, 1)
                        continue
                    e.wait_ge(s.chunk_ready, n + 1)
                    if w == "A":
                        part_of_max(i, n, bank, g + dg)
                    elif w == "M":
                        split_max(u if dg == 0 else 1 - u, bank)
                    else:
                        output(w, n, bank, g + dg, i)
        each_group(A, e, run)

    HID = Y[:, :].rearrange("p (m n) -> p m n", m=F // P)
    MT_F = F // P

    def ffn_tensor(e, s, w1, w2):
        def hidden(i):
            c, m = divmod(i, MT_F)
            need(e, s.hid_ready, i - 3)
            for k in range(KT):
                mm = e.matmul(PS[:, i % 4, :], w1[:, k, m * P:(m + 1) * P], XTF[:, k, c * CH:(c + 1) * CH],
                              start=k == 0, stop=k == KT - 1)
            mm.then_inc(s.hid_product, 1)

        def second(i):
            c, m = divmod(i, MT_F)
            e.wait_ge(s.hid_ready, i + 1)
            if m == 0:
                need(e, s.added, 2 * (c - 1))
            for t in range(4):
                mm = e.matmul(PS[:, 4 + 2 * (c % 2) + t // 2, t % 2 * D:(t % 2 + 1) * D], HID[:, m, t * P:(t + 1) * P],
                              w2[:, m, :], start=m == 0 and t % 2 == 0, stop=m == MT_F - 1, skip_group_check=True)
            mm.then_inc(s.hid_used, 1)
        n = NC * MT_F
        for i in range(n + 2):
            if i < n:
                hidden(i)
            if i >= 2:
                second(i - 2)

    def ffn_scalar(e, s, func, col):
        for i in range(NC * MT_F):
            e.wait_ge(s.hid_product, i + 1)
            need(e, s.hid_used, i - 7)
            m = i % MT_F
            e.activation(HID[:, m, :], PS[:, i % 4, :], func, bias=COL[:, col + m:col + m + 1]).then_inc(s.hid_ready, 1)

    def add_row(e, r):
        e.tensor_tensor(X[:, :, :], X[:, :, :], r.unsqueeze(1).broadcast_to([P, NT, D]), ALU.add)
        e.drain()

    def ffn_vector(e, s, b2):
        add_row(e, b2)
        for c in range(NC):
            e.wait_ge(s.hid_used, (c + 1) * MT_F)
            for k in range(2):
                x = X[:, 4 * c + 2 * k:4 * c + 2 * k + 2, :]
                e.tensor_tensor(x, x, PS[:, 4 + 2 * (c % 2) + k, :].rearrange("p (t d) -> p t d", t=2), ALU.add)\
                    .then_inc(s.added, 1)

    def square_tensor(e, s, w, base=0):
        for j in range(NT // 2):
            need(e, s.taken2, j - 3)
            for t in range(2):
                for k in range(KT):
                    tt = 2 * j + t
                    m = e.matmul(PS[:, j % 4, t * D:(t + 1) * D], XTF[:, k, tt * P:(tt + 1) * P], w[:, k, :],
                                 start=k == 0, stop=k == KT - 1, skip_group_check=True)
            m.then_inc(s.product2, 1)

    def square_vector(e, s, bias=None, leaky=None):
        if bias is not None:
            add_row(e, bias)
        for j in range(NT // 2):
            e.wait_ge(s.product2, j + 1)
            o = PS[:, j % 4, :].rearrange("p (t d) -> p t d", t=2)
            x = X[:, 2 * j:2 * j + 2, :]
            if leaky is None:
                e.tensor_tensor(x, x, o, ALU.add).then_inc(s.taken2, 1)
            else:
                y = SCR[:, :].rearrange("p (t d) -> p t d", t=2)
                z = OT[:, :].rearrange("p (t d) -> p t d", t=2)
                e.tensor_tensor(y, o, leaky.unsqueeze(1).broadcast_to([P, 2, D]), ALU.add).then_inc(s.taken2, 1)
                e.drain()
                e.scalar_tensor_tensor(z, y, 0.2, y, ALU.mult, ALU.max)
                e.drain()
                e.tensor_tensor(x, x, z, ALU.add)

    def add_attention(e):
        e.tensor_tensor(X2, X2, Y[:, :], ALU.add)
        e.drain()

    def key_masks_vector(e, layer):
        e.tensor_reduce(KSUM[:, :], X[:, :, :], AX.X, ALU.add)
        e.drain()
        e.tensor_scalar(QM[:, :], KSUM[:, :], 0.0, None, ALU.not_equal)
        if layer == 0:
            e.tensor_reduce(KC[0:SC, :], CTXN[0:SC, :, :], AX.X, ALU.add)
            e.drain()
            e.tensor_scalar(KZ[0:SC, 0:B], KC[0:SC, :], 0.0, None, ALU.is_equal)
            e.drain()
            e.tensor_scalar(KB[0:SC, 0:B], KZ[0:SC, 0:B], NEG1, None, ALU.mult)
        else:
            e.tensor_scalar(KZ[:, :], KSUM[:, :], 0.0, None, ALU.is_equal)
            e.drain()
            e.tensor_scalar(KB[:, :], KZ[:, :], NEG1, None, ALU.mult)

    turn = lambda n: sems(n, TurnSems, 2)
    sq = lambda n: sems(n, SquareSems, 2)
    ff = lambda n: sems(n, FeedForwardSems, 4)
    mk = lambda n: sems(n, KeyMaskSems, 5)

    L = [6 + 5 * l for l in range(3)]
    at0 = attention(3, 16, 8, ctx_keys=True, self_keys=True, causal=True, scale=0.25)
    at1 = [attention(L[0] + 2, 64, 4, ctx_keys=True, scale=0.125, masked=True, query_mask=True)] + \
          [attention(L[l] + 2, 64, 4, self_keys=True, scale=0.125, masked=True, query_mask=True) for l in (1, 2)]
    at2 = attention(23, 16, 8, ctx_keys=True, window=True, scale=0.25)
    at3 = attention(28, 16, 8, ctx_keys=True, scale=0.0625, masked=True)
    p0, p1, p2, p3 = project(2), [project(l + 1) for l in L], project(22), project(27)
    ln0, ln02, ln0f = ln(1), ln(4), ln(4)
    ln1 = [ln(l + 3) for l in L]
    ln2, ln2c = ln(21), ln(21)
    ln3, ln3o = ln(31), ln(33)
    tn0, tn0c, tn0f = turn(1), turn(1), turn(4)
    tn1, tn1f, m1 = [turn(l) for l in L], [turn(l + 3) for l in L], [mk(l) for l in L]
    tn2, tn2c, tn2o = turn(21), turn(21), turn(24)
    tn3, tn3c, tn3o, tn3f = turn(26), turn(26), turn(29), turn(31)
    sq1, sq2, sq3 = [sq(l + 4) for l in L], sq(25), sq(30)
    ff0, ff3 = ff(5), ff(32)

    ID_F, RELU = ACT.Identity, ACT.Relu
    feat0 = q_items(W0.qkv, 0, Q3, COLS["L0q"], ID_F) + q_items(W0.qkv, D, K3, COLS["L0k"], ID_F) + \
        c_items(W0.ckv, 0, C3, COLS["L0c"], ID_F)
    val0 = v_items(W0.qkv, 2 * D, row(RA, ROWS_L0, "bv"), V16, 4, 1) + vc_items(W0.ckv, D, row(RA, ROWS_L0, "bcv"), V16, 4)
    feat1, val1 = [], []
    for l in range(3):
        w, bq, bk, bv = W1[l], COLS["L1q"] + 2 * l, COLS["L1k"] + 2 * l, row(RB, ROWS_L1, f"bv{l}")
        feat1.append(q_items(w["q"], 0, Q2, bq, RELU) +
                     (c_items(w["k"], 0, C2, bk, RELU) if l == 0 else q_items(w["k"], 0, K2, bk, RELU)))
        val1.append(vc_items(w["v"], 0, bv, V64, 2) if l == 0 else v_items(w["v"], 0, bv, V64, 2, 0))
    feat2 = q_items(W2["q"], 0, Q3, None, ID_F) + c_items(W2["k"], 0, C3, None, ID_F)
    val2 = vc_items(W2["v"], 0, None, V16, 4)
    feat3 = q_items(W3.bd[0], 0, Q3, None, ID_F, diag=True) + c_items(W3.bd[1], 0, C3, None, ID_F, diag=True)
    val3 = vc_items(W3.bd[2], 0, None, V16, 4, diag=True)

    r3 = lambda n: RA[:, ROWS_L3.index(n), :]
    r2 = lambda n: RA[:, 6 + ROWS_L2.index(n), :]

    block = ctx.enter_context(nc.Block())

    @block.sync
    def _(e):
        nxt = lambda: next_stage(e, "sync")
        load_sync(e)
        nxt()
        nxt()
        project_sync(e, p0, feat0, val0, 3, False)
        nxt()
        attention_sync(e, at0)
        nxt()
        nxt()
        nxt()
        load_block3(e)
        for l in range(3):
            if l == 1:
                load_layer(e, 2, ld.w1c)
            if l == 2:
                load_block2(e)
            m = m1[l]
            n = B if l == 0 else NT
            p = SC if l == 0 else P
            e.wait_ge(m.row_cast, 1)
            km = KM.rearrange("t p -> (t p)")[0:n * p]
            e.dma_start(km.rearrange("(t p) -> t p", p=p), KZB[0:n, 0:p]).then_inc(m.stored, 16)
            e.wait_ge(m.stored, 16)
            e.dma_start(MB[:, 0:n * p], km.partition_broadcast(P)).then_inc(m.spread, 16)
            e.wait_ge(m.spread, 16)
            e.wait_ge([ld.w1a, ld.w1b, ld.w1c][l], 64)
            nxt()
            project_sync(e, p1[l], feat1[l], val1[l], 2, True)
            nxt()
            attention_sync(e, at1[l])
            nxt()
            nxt()
            nxt()
        e.dma_start(VS[:, :, :].rearrange("p u n -> p (u n)")[:, 0:TOK].bitcast(I32),
                    a["idx"].rearrange("b t -> (b t)").partition_broadcast(P)).then_inc(ld.masks, 16)
        e.wait_ge(ld.w2, 64)
        e.wait_ge(ld.w3, 16 * W3_LOADS)
        nxt()
        project_sync(e, p2, feat2, val2, 3, False)
        nxt()
        attention_sync(e, at2)
        nxt()
        nxt()
        nxt()
        e.dma_start(CTXN[0:SC, :, :], a["ctx"].rearrange("b s d -> s b d")).then_inc(ld.ctx, 16)
        e.wait_ge(ld.ctx, 16)
        nxt()
        project_sync(e, p3, feat3, val3, 3, False)
        nxt()
        attention_sync(e, at3)
        nxt()
        nxt()
        nxt()
        nxt()
        nxt()
        o = out.rearrange("b (t p) d -> p (b t) d", p=P)
        for c in range(NC):
            e.wait_ge(ln3o.normed, c + 1)
            e.dma_start(o[:, 4 * c:4 * c + 4, :], X[:, 4 * c:4 * c + 4, :]).then_inc(ld.out, 16)
        e.wait_ge(ld.out, 16 * NC)

    @block.gpsimd
    def _(e):
        nxt = lambda: next_stage(e, "gpsimd")
        load_pool(e)
        nxt()
        nxt()
        nxt()
        attention_gpsimd(e, at0)
        nxt()
        nxt()
        nxt()
        e.memset(WA[:, 4608:4992], 0.0).then_inc(ld.cleared, 1)
        for l in range(3):
            nxt()
            nxt()
            attention_gpsimd(e, at1[l])
            nxt()
            nxt()
            nxt()
        nxt()
        nxt()
        attention_gpsimd(e, at2)
        for _ in range(3):
            nxt()
        nxt()
        nxt()
        attention_gpsimd(e, at3)
        for _ in range(5):
            nxt()

    @block.tensor
    def _(e):
        nxt = lambda: next_stage(e, "tensor")
        nxt()
        turn_ctx_tensor(e, tn0c, CTXN)
        turn_tensor(e, tn0, tokens(Y3), ln0.normed, tn0c.taken)
        nxt()
        project_tensor(e, p0, feat0, val0)
        nxt()
        attention_tensor(e, at0)
        nxt()
        turn_tensor(e, tn0f, tokens(Y3), ln0f.normed)
        nxt()
        ffn_tensor(e, ff0, W0.w1, W0.w2)
        nxt()
        for l in range(3):
            turn_tensor(e, tn1[l], tokens(X))
            n, p = (B, SC) if l == 0 else (NT, P)
            e.wait_ge(m1[l].row_ready, 1)
            e.wait_ge(tn1[l].taken, 1)
            e.transpose(PS[0:n, 0, 0:p], KZ[0:p, 0:n], ID[0:p, 0:p]).then_inc(m1[l].turned, 1)
            nxt()
            project_tensor(e, p1[l], feat1[l], val1[l])
            nxt()
            attention_tensor(e, at1[l])
            nxt()
            turn_tensor(e, tn1f[l], tokens(X), ln1[l].normed)
            nxt()
            square_tensor(e, sq1[l], W1[l]["f"])
            nxt()
        turn_ctx_tensor(e, tn2c, CTXN, ln2c.normed)
        turn_tensor(e, tn2, tokens(Y3), ln2.normed, tn2c.taken)
        nxt()
        project_tensor(e, p2, feat2, val2)
        nxt()
        attention_tensor(e, at2)
        nxt()
        turn_tensor(e, tn2o, tokens(Y3))
        nxt()
        square_tensor(e, sq2, W2["o"])
        nxt()
        turn_ctx_tensor(e, tn3c, CTXN, ld.ctx, 16)
        turn_tensor(e, tn3, tokens(X), None, tn3c.taken)
        nxt()
        project_tensor(e, p3, feat3, val3)
        nxt()
        attention_tensor(e, at3)
        nxt()
        turn_tensor(e, tn3o, tokens(Y3))
        nxt()
        square_tensor(e, sq3, W3.out)
        nxt()
        turn_tensor(e, tn3f, tokens(X), ln3.normed)
        nxt()
        ffn_tensor(e, ff3, W3.w1, W3.w2)
        nxt()

    @block.scalar
    def _(e):
        nxt = lambda: next_stage(e, "scalar")
        nxt()
        turn_ctx_scalar(e, tn0c)
        ln_scalar(e, ln0)
        turn_scalar(e, tn0)
        nxt()
        project_scalar(e, p0, feat0)
        nxt()
        attention_scalar(e, at0)
        nxt()
        ln_scalar(e, ln02)
        ln_scalar(e, ln0f)
        turn_scalar(e, tn0f)
        nxt()
        ffn_scalar(e, ff0, ACT.Gelu, COLS["L0f"])
        nxt()
        for l in range(3):
            turn_scalar(e, tn1[l])
            n, p = (B, SC) if l == 0 else (NT, P)
            e.wait_ge(m1[l].turned, 1)
            e.activation(KZB[0:n, 0:p], PS[0:n, 0, 0:p], ACT.Copy, scale=NEG1 * 8).then_inc(m1[l].row_cast, 1)
            nxt()
            project_scalar(e, p1[l], feat1[l])
            nxt()
            attention_scalar(e, at1[l])
            nxt()
            ln_scalar(e, ln1[l])
            turn_scalar(e, tn1f[l])
            nxt()
            nxt()
        ln_scalar(e, ln2c, B, SC)
        turn_ctx_scalar(e, tn2c)
        ln_scalar(e, ln2)
        turn_scalar(e, tn2)
        nxt()
        project_scalar(e, p2, feat2)
        nxt()
        attention_scalar(e, at2)
        nxt()
        turn_scalar(e, tn2o)
        nxt()
        nxt()
        turn_ctx_scalar(e, tn3c)
        turn_scalar(e, tn3)
        nxt()
        project_scalar(e, p3, feat3)
        nxt()
        attention_scalar(e, at3)
        nxt()
        turn_scalar(e, tn3o)
        nxt()
        nxt()
        ln_scalar(e, ln3)
        turn_scalar(e, tn3f)
        nxt()
        ffn_scalar(e, ff3, ACT.Relu, COLS["L3f"])
        nxt()
        ln_scalar(e, ln3o)

    @block.vector
    def _(e):
        nxt = lambda: next_stage(e, "vector")
        nxt()
        ln_vector(e, ln0, X, Y3, row(RA, ROWS_L0, "g1"), row(RA, ROWS_L0, "be1"), "layer", 1e-5)
        nxt()
        project_vector(e, p0, feat0, val0, 3, False)
        nxt()
        attention_vector(e, at0)
        nxt()
        add_attention(e)
        ln_vector(e, ln02, X, Y3, row(RA, ROWS_L0, "g2"), row(RA, ROWS_L0, "be2"), "layer", 1e-5)
        e.drain()
        ln_vector(e, ln0f, Y3, Y3, row(RA, ROWS_L0, "gf"), row(RA, ROWS_L0, "bf"), "layer", 1e-5)
        nxt()
        ffn_vector(e, ff0, row(RA, ROWS_L0, "b2"))
        nxt()
        for l in range(3):
            key_masks_vector(e, l)
            e.drain().then_inc(m1[l].row_ready, 1)
            nxt()
            project_vector(e, p1[l], feat1[l], val1[l], 2, True)
            nxt()
            attention_vector(e, at1[l])
            nxt()
            add_attention(e)
            ln_vector(e, ln1[l], X, X, row(RB, ROWS_L1, f"gamma{l}"), row(RB, ROWS_L1, f"beta{l}"), "unbiased", 1e-8)
            nxt()
            square_vector(e, sq1[l], leaky=row(RB, ROWS_L1, f"bff{l}"))
            nxt()
        e.wait_ge(ld.w3, 16 * W3_LOADS)
        ln_vector(e, ln2c, CTXN, CTXN, r2("gkv"), None, "rms", 1.1920929e-07, B, SC, B)
        e.drain()
        ln_vector(e, ln2, X, Y3, r2("gq"), None, "rms", 1.1920929e-07)
        e.wait_ge(ld.masks, 16)
        ix = VS[:, :, :].rearrange("p u n -> p (u n)")[:, 0:TOK]
        e.tensor_scalar(ix, ix.bitcast(I32), POS[:, 0:1], None, ALU.subtract)
        e.drain()
        e.tensor_tensor(ix, ix, ix, ALU.mult)
        e.drain()
        e.tensor_scalar(MB[:, :], ix, 1.0, None, ALU.is_le)
        nxt()
        project_vector(e, p2, feat2, val2, 3, False)
        nxt()
        attention_vector(e, at2)
        nxt()
        nxt()
        square_vector(e, sq2)
        nxt()
        e.tensor_scalar(MB[:, 0:B * SC], MI[:, 0:B * SC], 0.0, NEG3_ROUND, ALU.is_equal, ALU.mult)
        e.tensor_scalar(KB[0:SC, 0:B], MI[0:SC, B * SC:B * SC + B], 0.0, NEG3_ROUND / 16, ALU.is_equal, ALU.mult)
        nxt()
        project_vector(e, p3, feat3, val3, 3, False)
        nxt()
        attention_vector(e, at3)
        nxt()
        nxt()
        square_vector(e, sq3, bias=r3("bout"))
        nxt()
        ln_vector(e, ln3, X, X, r3("g1"), r3("beta1"), "layer", 1e-5)
        nxt()
        ffn_vector(e, ff3, r3("bff2"))
        nxt()
        ln_vector(e, ln3o, X, X, r3("g2"), r3("beta2"), "layer", 1e-5)


def kernel(**inputs):
    import numpy as np
    import concourse.bacc as bacc
    from concourse.bass_utils import run_bass_kernel_spmd

    g = {k: np.asarray(v) for k, v in inputs.items()}
    l0, l1, l2, l3 = (lambda n, p=f"L{i}_xattn_": g[p + n] for i in range(4))
    cols = lambda v: v.reshape(-1, P).T
    arrays = {
        "x": g["x"], "ctx": g["ctx_1024"], "idx": g["itok_BxS_0_255"],
        "mask": g["mask_Bx1x1xS2_if1"].reshape(B, SC),
        "w_qkv": l0("w_qkv"), "w_ckv": l0("w_ckv"), "w1": l0("w1"), "w2": l0("w2"),
        "Wq": l1("Wq"), "Wk": l1("Wk"), "Wv": l1("Wv"), "Wf": l1("Wff"),
        "W2q": l2("Wq").T, "W2k": l2("Wk").T, "W2v": l2("Wv").T, "W2o": l2("Wo").T,
        "w3q": l3("wq"), "w3k": l3("wk"), "w3v": l3("wv"), "w3_out": l3("w_out"), "w3_1": l3("w_ff1"), "w3_2": l3("w_ff2"),
        "rows0": np.stack([l0("b_qkv")[2 * D:], l0("b_ckv")[D:], l0("b2"), l0("g1"), l0("be1"), l0("g2"), l0("be2"),
                           l0("gf"), l0("bf")]),
        "rows1": np.concatenate([l1("bv"), l1("gamma"), l1("beta"), l1("bff")]),
        "rows23": np.stack([l3("b_out"), l3("g1"), l3("beta1"), l3("b_ff2"), l3("g2"), l3("beta2"),
                            l2("gamma_q"), l2("gamma_kv")]),
        "cols": np.concatenate([cols(l0("b_qkv")[:2 * D]), cols(l0("b_ckv")[:D]), cols(l0("b1")),
                                cols(l1("bq").reshape(-1)), cols(l1("bk").reshape(-1)), cols(l3("b_ff1"))], axis=1),
    }
    nc = bacc.Bacc("TRN2", target_bir_lowering=False, num_devices=1)
    sent, args = {}, {}
    for name, v in arrays.items():
        v = np.ascontiguousarray(v)
        sent[f"in_{name}"] = v
        args[name] = nc.dram_tensor(f"in_{name}", v.shape, mybir.dt.from_np(v.dtype), kind="ExternalInput").ap()
    res = nc.dram_tensor("out_0", (B, T, D), F32, kind="ExternalOutput").ap()
    build(nc, args, res)
    r = run_bass_kernel_spmd(nc, [sent], core_ids=[0])
    return r.results[0]["out_0"]
```

```python
from contextlib import ExitStack

import concourse.bass as bass
from concourse import mybir

F32 = mybir.dt.float32
F32R = mybir.dt.float32r
BF16 = mybir.dt.bfloat16
I32 = mybir.dt.int32
ALU = mybir.AluOpType
ACT = mybir.ActivationFunctionType
AX = mybir.AxisListType
ds = bass.ds

B, T, D, F, SC = 2, 1024, 256, 1024, 77
P = 128
TOK = B * T
NT = TOK // P
TB = T // P
CH = 512
NC = TOK // CH
KT = D // P

ROWS_L0 = ["bv", "bcv", "b2", "g1", "be1", "g2", "be2", "gf", "bf"]
ROWS_L1 = ["bv0", "bv1", "bv2", "gamma0", "gamma1", "gamma2", "beta0", "beta1", "beta2", "bff0", "bff1", "bff2"]
ROWS_L2 = ["gq", "gkv"]
ROWS_L3 = ["bout", "g1", "beta1", "bff2", "g2", "beta2"]
COLS = {"L0q": 0, "L0k": 2, "L0c": 4, "L0f": 6, "L1q": 14, "L1k": 20, "L3f": 26}
NCOLS = 34

MASKED = -1.0e37
NEG1 = -4294967296.0
NEG3_ROUND = -9.972771014849226e+19
LOWEST = -3.0e38

Q_RUNS = [(0, 3), (0, 2), (0, 1)]
K_RUNS = [(0, 3), (1, 3), (2, 3)]
K16 = 96
M_ROWS = 3
SEMAPHORES = 18


class LoadSems:
    def __init__(self, s):
        (self.x, self.w0, self.w1a, self.w1b, self.w1c, self.w2, self.w3, self.ctx, self.masks, self.cleared,
         self.out) = s


class NormSems:
    def __init__(self, s):
        self.step, self.var_ready, self.std_ready, self.normed = s


class TurnSems:
    def __init__(self, s):
        self.turned, self.taken = s


class SquareSems:
    def __init__(self, s):
        self.product2, self.taken2 = s


class FeedForwardSems:
    def __init__(self, s):
        self.hid_product, self.hid_ready, self.hid_used, self.added = s


class KeyMaskSems:
    def __init__(self, s):
        self.row_ready, self.turned, self.row_cast, self.stored, self.spread = s


class ProjectSems:
    def __init__(self, s):
        self.product, self.evacuated, self.split, self.step, self.v_product, self.v_taken, self.v_ready = s[0:7]
        self.stored, self.v_stored = s[7:9], s[9:11]


class AttentionSems:
    def __init__(self, s):
        (self.s_ready, self.p_ready, self.gated, self.pv_tile, self.copied, self.chunk_ready, self.chunk_free,
         self.max_ready, self.max_split, self.cleared, self.sending) = s[0:11]
        self.loaded = s[11:18]


class FeatureItem:
    def __init__(self, mms, n, func, bias, src, dst):
        self.mms, self.n, self.func, self.bias, self.src, self.dst = mms, n, func, bias, src, dst


class ValueItem:
    def __init__(self, mms, p, row, g, dst):
        self.mms, self.p, self.row, self.g, self.dst = mms, p, row, g, dst


class KeyTile:
    def __init__(self, c, kind, j, diag, q0, first, last, index):
        self.c, self.kind, self.j, self.diag, self.q0 = c, kind, j, diag, q0
        self.first, self.last, self.index = first, last, index


class Attention:
    def __init__(self, dh, n, ctx, self_keys, causal, window, scale, masked, query_mask):
        self.dh, self.n, self.ctx, self.self, self.causal = dh, n, ctx, self_keys, causal
        self.window, self.scale, self.masked, self.query_mask = window, scale, masked, query_mask


class MaxRows:
    def __init__(self, sems):
        self.total, self.sems = [0] * len(sems), sems


class Weights:
    def __init__(self, qkv=None, ckv=None, w1=None, w2=None, out=None, bd=None):
        self.qkv, self.ckv, self.w1, self.w2, self.out, self.bd = qkv, ckv, w1, w2, out, bd


def build(nc, a, out):
    with ExitStack() as ctx:
        program(nc, ctx, a, out)


def program(nc, ctx, a, out):
    def sb(name, shape, dt=F32):
        return ctx.enter_context(nc.sbuf_tensor(name, shape, dt))

    def lasting(prefix, n):
        return [ctx.enter_context(nc.semaphore(f"{prefix}_{i}")) for i in range(n)]

    sets = [[ctx.enter_context(nc.semaphore(f"set{r}_{i}")) for i in range(SEMAPHORES)] for r in range(3)]
    taken = {}

    def sems(stage, kind, count):
        n = taken.get(stage, 0)
        taken[stage] = n + count
        assert taken[stage] <= SEMAPHORES
        return kind(sets[stage % 3][n:n + count])

    def dram(name, shape, dt):
        return nc.dram_tensor(name, shape, dt, kind="Internal").ap()

    X = sb("x_res", [P, NT, D])
    Y = sb("y_tok", [P, NT * D])
    XT = sb("x_feat", [P, NT * D])
    WA = sb("w_even", [P, 6656])
    WB = sb("w_odd", [P, 4096])
    RA = sb("rows_even", [P, len(ROWS_L0), D])
    RB = sb("rows_odd", [P, len(ROWS_L1), D])
    STK = sb("stacks", [P, 2, 8192], F32R)
    VS = sb("v_group", [P, 2, 1152])
    OT = sb("o_feat", [P, CH])
    OD = sb("o_denom", [64, CH])
    SCR = sb("scratch", [P, CH])
    MB = sb("mask_rows", [P, TOK], BF16)
    COL = sb("cols", [P, NCOLS])
    CTXN = sb("ctx_tok", [P, B, D])
    CTXT = sb("ctx_feat", [P, KT, B * SC])
    ID = sb("ident", [P, P])
    IDB = sb("ident_bf", [P, P], BF16)
    CM_S = sb("causal_q_rows", [P, P], BF16)
    CM_T = sb("causal_k_rows", [P, P], BF16)
    ONES = sb("ones", [P, 32])
    ONESC = sb("ones_ctx", [P, 32])
    STATS = sb("stats", [P, NT, 6])
    MV = sb("mean_var", [P, NT, 2])
    VE = sb("var_eps", [P, NT])
    SD = sb("std", [P, NT])
    RS = sb("rstd", [P, NT])
    MXP = sb("max_parts", [P, 96])
    MX = sb("max_rows", [P, 32])
    MT = sb("neg_max", [32, P])
    MP = sb("neg_max_parts", [32, 3, 3, P], BF16)
    MPR = sb("neg_max_parts_r", [16, 3, 2, P], F32R)
    RC = sb("recip", [P, 16])
    KC = sb("ctx_key_sum", [P, B])
    KZ = sb("key_zero", [P, NT])
    KB = sb("key_bias", [P, NT])
    QM = sb("query_mask", [P, NT])
    KSUM = sb("key_sum", [P, NT])
    KZB = sb("key_zero_rows", [NT, P], BF16)
    MI = sb("mask_int", [P, B * SC + B], I32)
    POS = sb("position", [P, 1])
    POSI = sb("position_int", [P, 1], I32)
    PS = ctx.enter_context(nc.psum_tensor("banks", [P, 8, CH], F32))

    X2 = X[:, :, :].rearrange("p t d -> p (t d)")
    Y3 = Y[:, :].rearrange("p (t d) -> p t d", d=D)
    XTF = XT[:, :].rearrange("p (k n) -> p k n", k=KT)
    PB = XT[:, :].rearrange("p (s r h n) -> p s r h n", s=2, r=2, h=2)

    Q3 = dram("q_parts", (B * 2, 3, 16, 8, T), BF16)
    K3 = dram("k_parts", (B * 2, 3, 16, 8, T), BF16)
    C3 = dram("kctx_parts", (B, 2, 3, 16, 8, SC), BF16)
    Q2 = dram("q_parts_r", (2, B * D, T), F32)
    K2 = dram("k_parts_r", (2, B * D, T), F32)
    C2 = dram("kctx_parts_r", (2, B * D, SC), F32)
    V16 = dram("v16", (B, 4, P, 9, 128), F32)
    V64 = dram("v64", (B, 2, P, 8, 128), F32)
    KM = dram("key_mask_row", (NT, P), BF16)

    stage_done = ctx.enter_context(nc.semaphore("stage_done"))
    stages = {}

    def next_stage(e, who):
        e.drain().then_inc(stage_done, 1)
        stages[who] = stages.get(who, 0) + 1
        e.wait_ge(stage_done, 5 * stages[who])
        if who == "gpsimd":
            for sem in sets[(stages[who] - 1) % 3]:
                e.sem_clear(sem)

    def need(e, sem, value):
        if not (isinstance(value, int) and value <= 0):
            e.wait_ge(sem, value)

    def wview(W, off, k, n):
        return W[:, off:off + k * n].rearrange("p (k n) -> p k n", k=k)

    W0 = Weights(qkv=wview(WA, 0, KT, 768), ckv=wview(WA, 1536, KT, 512),
                         w1=wview(WA, 2560, KT, F), w2=wview(WA, 4608, F // P, D))
    W1 = [{n: wview(WB, (l % 2 * 4 + j) * 512, KT, D) for j, n in enumerate("qkvf")} for l in range(3)]
    W2 = {n: wview(WB, 2048 + j * 512, KT, D) for j, n in enumerate("qkvo")}
    W3 = Weights(w1=wview(WA, 0, KT, F), w2=wview(WA, 2048, F // P, D), out=wview(WA, 4096, KT, D),
                         bd=[WA[:, 4608 + 128 * j:4608 + 128 * (j + 1)] for j in range(5)])

    def row(R, names, name):
        return R[:, names.index(name), :]

    ld = LoadSems(lasting("load", 11))

    def kp(w):
        return w.rearrange("(k p) n -> p k n", p=P)

    def load_sync(e):
        e.dma_start(X[:, :, :], a["x"].rearrange("b (t p) d -> p (b t) d", p=P)).then_inc(ld.x, 16)
        e.dma_start(CTXN[0:SC, :, :], a["ctx"].rearrange("b s d -> s b d")).then_inc(ld.x, 16)
        e.dma_start(COL[:, :], a["cols"]).then_inc(ld.x, 16)
        e.dma_start(RA[:, :, :], a["rows0"].partition_broadcast(P)).then_inc(ld.x, 16)
        for w, name in ((W0.qkv, "w_qkv"), (W0.ckv, "w_ckv"), (W0.w1, "w1"), (W0.w2, "w2")):
            e.dma_start(w, kp(a[name])).then_inc(ld.w0, 16)
        e.dma_start(RB[:, :, :], a["rows1"].partition_broadcast(P)).then_inc(ld.x, 16)
        load_layer(e, 0, ld.w1a)
        e.wait_ge(ld.x, 80)
        e.wait_ge(ld.w0, 64)

    def load_layer(e, l, sem):
        for n in "qkvf":
            e.dma_start(W1[l][n], kp(a["W" + n][l])).then_inc(sem, 16)

    def load_block2(e):
        for n in "qkvo":
            e.dma_start(W2[n], kp(a["W2" + n])).then_inc(ld.w2, 16)

    def load_block3(e):
        e.dma_start(RA[:, 0:8, :], a["rows23"].partition_broadcast(P)).then_inc(ld.w3, 16)
        for w, n in ((W3.w1, "w3_1"), (W3.w2, "w3_2"), (W3.out, "w3_out")):
            e.dma_start(w, kp(a[n])).then_inc(ld.w3, 16)
        e.wait_ge(ld.cleared, 1)
        for j, n in enumerate("qkv"):
            for h in range(8):
                e.dma_start(W3.bd[j][16 * h:16 * h + 16, 16 * h:16 * h + 16], a["w3" + n]).then_inc(ld.w3, 16)
        e.dma_start(MI[:, 0:B * SC], a["mask"].rearrange("b s -> (b s)").partition_broadcast(P)).then_inc(ld.w3, 16)
        e.dma_start(MI[0:SC, B * SC:B * SC + B], a["mask"].rearrange("b s -> s b"), allow_slow_non_contiguous=True).then_inc(ld.w3, 16)
    W3_LOADS = 4 + 24 + 2

    def load_pool(e):
        fill(e, ID[:, :], 0.0)
        fill(e, IDB[:, :], 0.0)
        fill(e, CM_S[:, :], 0.0)
        fill(e, CM_T[:, :], 0.0)
        fill(e, ONES[:, :], 1.0)
        fill(e, ONESC[:, :], 1.0)
        fill(e, KB[:, :], 0.0)
        e.iota(POSI[:, :], pattern=[[0, 1]], base=0, channel_multiplier=1)
        e.drain()
        e.tensor_copy(POS[:, :], POSI[:, :])
        e.drain()
        for m in (ID, IDB):
            e.affine_select(out=m[:, :], in_=m[:, :], compare_op=ALU.not_equal, fill=1.0,
                            base=0, pattern=[[-1, P]], channel_multiplier=1)
            e.drain()
        e.drain()
        e.affine_select(out=ONESC[:, :], in_=ONESC[:, :], compare_op=ALU.is_ge, fill=0.0,
                        base=SC - 1, pattern=[[0, 32]], channel_multiplier=-1)
        e.drain()
        e.affine_select(out=CM_S[:, :], in_=CM_S[:, :], compare_op=ALU.is_ge, fill=MASKED,
                        base=0, pattern=[[-1, P]], channel_multiplier=1)
        e.drain()
        e.affine_select(out=CM_T[:, :], in_=CM_T[:, :], compare_op=ALU.is_ge, fill=MASKED,
                        base=0, pattern=[[1, P]], channel_multiplier=-1)

    def ln(stage):
        return sems(stage, NormSems, 4)

    def ln_vector(e, s, src, dst, g, b, mode, eps, nt=NT, p=P, per=4):
        n = 0
        for t in range(nt):
            e.bn_stats(STATS[0:p, t, :], src[0:p, t, :]).then_inc(s.step, 1)
        n += nt
        e.wait_ge(s.step, n)
        for t in range(nt):
            e.bn_aggr(MV[0:p, t, :], STATS[0:p, t, :]).then_inc(s.step, 1)
        n += nt
        e.wait_ge(s.step, n)
        mean, var = MV[0:p, 0:nt, 0], MV[0:p, 0:nt, 1]
        if mode == "rms":
            e.tensor_tensor(VE[0:p, 0:nt], mean, mean, ALU.mult).then_inc(s.step, 1)
            e.wait_ge(s.step, n + 1)
            e.scalar_tensor_tensor(VE[0:p, 0:nt], VE[0:p, 0:nt], eps, var, ALU.add, ALU.add).then_inc(s.var_ready, 1)
            n += 1
        elif mode == "unbiased":
            e.tensor_scalar(VE[0:p, 0:nt], var, D / (D - 1.0), None, ALU.mult).then_inc(s.var_ready, 1)
        else:
            e.tensor_scalar(VE[0:p, 0:nt], var, eps, None, ALU.add).then_inc(s.var_ready, 1)
        e.wait_ge(s.std_ready, 1)
        if mode == "unbiased":
            e.tensor_scalar(SD[0:p, 0:nt], SD[0:p, 0:nt], eps, None, ALU.add).then_inc(s.step, 1)
            n += 1
            e.wait_ge(s.step, n)
        e.reciprocal(RS[0:p, 0:nt], SD[0:p, 0:nt]).then_inc(s.step, 1)
        n += 1
        e.wait_ge(s.step, n)
        for c in range(nt // per):
            for t in range(per * c, per * c + per):
                if mode == "rms":
                    e.tensor_scalar(dst[0:p, t, :], src[0:p, t, :], RS[0:p, t:t + 1], None, ALU.mult).then_inc(s.step, 1)
                else:
                    e.tensor_scalar(dst[0:p, t, :], src[0:p, t, :], MV[0:p, t, 0:1], RS[0:p, t:t + 1],
                                    ALU.subtract, ALU.mult).then_inc(s.step, 1)
            n += per
            e.wait_ge(s.step, n)
            d = dst[0:p, per * c:per * c + per, :]
            gb = g[0:p, :].unsqueeze(1).broadcast_to([p, per, D])
            if b is None:
                e.tensor_tensor(d, d, gb, ALU.mult).then_inc(s.normed, 1)
            else:
                e.tensor_tensor(d, d, gb, ALU.mult).then_inc(s.step, 1)
                n += 1
                e.wait_ge(s.step, n)
                e.tensor_tensor(d, d, b[0:p, :].unsqueeze(1).broadcast_to([p, per, D]), ALU.add).then_inc(s.normed, 1)

    def ln_scalar(e, s, nt=NT, p=P):
        e.wait_ge(s.var_ready, 1)
        e.activation(SD[0:p, 0:nt], VE[0:p, 0:nt], ACT.Sqrt).then_inc(s.std_ready, 1)

    def turn_tensor(e, s, src, ready=None, ctx_taken=None):
        for c in range(NC):
            if c == 3 and ctx_taken is not None:
                e.wait_ge(ctx_taken, 1)
            if ready is not None:
                e.wait_ge(ready, c + 1)
            for k in range(KT):
                for j in range(4):
                    t = e.transpose(PS[:, 2 * c + k, j * P:(j + 1) * P], src(4 * c + j, k), ID[:, :])
                t.then_inc(s.turned, 1)

    def turn_scalar(e, s):
        for c in range(NC):
            for k in range(KT):
                e.wait_ge(s.turned, 2 * c + k + 1)
                e.activation(XTF[:, k, c * CH:(c + 1) * CH], PS[:, 2 * c + k, :], ACT.Copy).then_inc(s.taken, 1)

    def tokens(src3):
        return lambda t, k: src3[:, t, k * P:(k + 1) * P]

    def turn_ctx_tensor(e, s, src, ready=None, value=1):
        if ready is not None:
            e.wait_ge(ready, value)
        for b in range(B):
            for k in range(KT):
                e.transpose(PS[:, 7, (k * B + b) * P:(k * B + b) * P + SC], src[0:SC, b, k * P:(k + 1) * P],
                            ID[0:SC, 0:SC]).then_inc(s.turned, 1)

    def turn_ctx_scalar(e, s):
        e.wait_ge(s.turned, B * KT)
        e.activation(CTXT[:, :, :].rearrange("p k (b n) -> p k b n", b=B),
                     PS[:, 7, :].rearrange("p (k b n) -> p k b n", k=KT, b=B)[:, :, :, 0:SC],
                     ACT.Copy).then_inc(s.taken, 1)

    RBUF = Y[:, 0:1024].rearrange("p (s n) -> p s n", s=2)
    P3 = Y[:, 1024:2560].bitcast(BF16).rearrange("p (s k n) -> p s k n", s=2, k=3)
    VT = Y[:, 2560:3584].rearrange("p (s n) -> p s n", s=2)
    P2 = STK[:, 0, 0:2048].rearrange("p (s k n) -> p s k n", s=2, k=2)

    def project_tensor(e, s, feat, vals):
        for i, it in enumerate(feat):
            need(e, s.evacuated, i - 3)
            for j, (l, r) in enumerate(it.mms):
                m = e.matmul(PS[0:P, i % 4, 0:it.n], l, r, start=(j == 0), stop=(j == len(it.mms) - 1))
            m.then_inc(s.product, 1)
        for i, v in enumerate(vals):
            need(e, s.v_taken, i - 3)
            for sl, mms in v.mms:
                for j, (l, r) in enumerate(mms):
                    m = e.matmul(PS[0:v.p, 4 + i % 4, sl], l, r, start=(j == 0), stop=(j == len(mms) - 1))
            m.then_inc(s.v_product, 1)

    def project_scalar(e, s, feat):
        for i, it in enumerate(feat):
            e.wait_ge(s.product, i + 1)
            need(e, s.split, i - 1)
            e.activation(RBUF[:, i % 2, 0:it.n], PS[:, i % 4, 0:it.n], it.func, bias=it.bias).then_inc(s.evacuated, 1)

    def project_vector(e, s, feat, vals, parts, relu):
        steps = 0
        def step(ins):
            nonlocal steps
            ins.then_inc(s.step, 1)
            steps += 1
            e.wait_ge(s.step, steps)
        vw = 32 if parts == 3 else 64
        hv = D // (16 if parts == 3 else 64)
        if parts == 3:
            step(e.memset(VT[:, :, :], 1.0))
        def value(i):
            v = vals[i]
            e.wait_ge(s.v_product, i + 1)
            if i >= 2:
                e.wait_ge(s.v_stored[i % 2], 16 * (i // 2))
            dst = VT[0:v.p, i % 2, 0:hv * vw].rearrange("p (h w) -> p h w", w=vw)[:, :, 0:D // hv]
            src = PS[0:v.p, 4 + i % 4, 0:D].rearrange("p (h w) -> p h w", h=hv)
            if v.row is None:
                e.tensor_copy(dst, src).then_inc(s.v_taken, 1)
            else:
                r = v.row[0:v.p, :].rearrange("p (h w) -> p h w", h=hv)
                e.tensor_tensor(dst, src, r, ALU.add).then_inc(s.v_taken, 1)
            if relu:
                e.wait_ge(s.v_taken, i + 1)
                e.tensor_scalar(dst, dst, 0.0, None, ALU.max).then_inc(s.v_ready, 1)
        for i, it in enumerate(feat):
            e.wait_ge(s.evacuated, i + 1)
            if i >= 2:
                e.wait_ge(s.stored[i % 2], 16 * parts * (i // 2))
            r = RBUF[:, i % 2, 0:it.n]
            if parts == 3:
                p1, p2, p3 = (P3[:, i % 2, k, 0:it.n] for k in range(3))
                step(e.tensor_copy(p1, r))
                step(e.tensor_tensor(r, r, p1, ALU.subtract))
                step(e.tensor_copy(p2, r))
                e.tensor_tensor(p3, r, p2, ALU.subtract).then_inc(s.split, 1)
            else:
                hi, lo = P2[:, i % 2, 0, 0:it.n], P2[:, i % 2, 1, 0:it.n]
                step(e.tensor_copy(hi, r))
                e.tensor_tensor(lo, r, hi.bitcast(F32), ALU.subtract).then_inc(s.split, 1)
        for i in range(len(vals)):
            value(i)

    def project_sync(e, s, feat, vals, parts, relu):
        for i, it in enumerate(feat):
            e.wait_ge(s.split, i + 1)
            for k in range(parts):
                src = (P3 if parts == 3 else P2.bitcast(F32))[:, i % 2, k, 0:it.n]
                e.dma_start(it.dst(k), it.src(src)).then_inc(s.stored[i % 2], 16)
        for i, v in enumerate(vals):
            e.wait_ge(s.v_ready if relu else s.v_taken, i + 1)
            e.dma_start(v.dst, VT[0:v.p, i % 2, 0:v.g * 128].rearrange("p (g w) -> p g w", g=v.g)).then_inc(s.v_stored[i % 2], 16)
        for u in range(2):
            e.wait_ge(s.stored[u], 16 * parts * ((len(feat) + 1 - u) // 2))
            e.wait_ge(s.v_stored[u], 16 * ((len(vals) + 1 - u) // 2))

    def project(stage):
        return sems(stage, ProjectSems, 11)

    def q_items(w, off, dst, bias, func, diag=False):
        its = []
        for c in range(NC):
            b, half = c // 2, c % 2
            for m in range(KT):
                if diag:
                    mms = [(w, XTF[:, m, c * CH:(c + 1) * CH])]
                else:
                    mms = [(w[:, k, off + m * P:off + (m + 1) * P], XTF[:, k, c * CH:(c + 1) * CH]) for k in range(KT)]
                its.append(FeatureItem(
                    mms=mms, n=CH, func=func, bias=0.0 if bias is None else COL[:, bias + m:bias + m + 1],
                    src=lambda x: x,
                    dst=lambda k, b=b, m=m, h=half: dst(k, b, m)[:, h * CH:(h + 1) * CH]))
        return its

    def c_items(w, off, dst, bias, func, diag=False):
        its = []
        for m in range(KT):
            if diag:
                mms = [(w, CTXT[:, m, :])]
            else:
                mms = [(w[:, k, off + m * P:off + (m + 1) * P], CTXT[:, k, :]) for k in range(KT)]
            its.append(FeatureItem(
                mms=mms, n=B * SC, func=func, bias=0.0 if bias is None else COL[:, bias + m:bias + m + 1],
                src=lambda x: x.rearrange("p (b n) -> p b n", b=B),
                dst=lambda k, m=m: dst(k, m)))
        return its

    q3_dst = lambda k, b, m: Q3[b * 2 + m, k].rearrange("d h n -> (d h) n")
    k3_dst = lambda k, b, m: K3[b * 2 + m, 2 - k].rearrange("d h n -> (d h) n")
    c3_dst = lambda k, m: C3[:, m, 2 - k].rearrange("b d h n -> (d h) b n")
    q2_dst = lambda k, b, m: Q2[k, b * D + m * P:b * D + (m + 1) * P, :]
    k2_dst = lambda k, b, m: K2[k, b * D + m * P:b * D + (m + 1) * P, :]
    c2_dst = lambda k, m: C2[k].rearrange("(b f) n -> f b n", b=B)[m * P:(m + 1) * P]

    def v_items(w, off, rowv, dst, ngroup, tile0):
        its = []
        for t in range(NT):
            b = t // TB
            mms = [(XTF[:, k, t * P:(t + 1) * P], w[:, k, off:off + D]) for k in range(KT)]
            its.append(ValueItem(mms=[(slice(0, D), mms)], p=P, row=rowv, g=ngroup,
                                       dst=dst[b, :, :, t % TB + tile0, :].rearrange("g p w -> p g w")))
        return its

    def vc_items(w, off, rowv, dst, ngroup, diag=False):
        its = []
        for b in range(B):
            lhs = [CTXT[:, k, b * SC:(b + 1) * SC] for k in range(KT)]
            if diag:
                mms = [(slice(k * P, (k + 1) * P), [(lhs[k], w)]) for k in range(KT)]
            else:
                mms = [(slice(0, D), [(lhs[k], w[:, k, off:off + D]) for k in range(KT)])]
            its.append(ValueItem(mms=mms, p=SC, row=rowv, g=ngroup,
                                       dst=dst[b, :, 0:SC, 0, :].rearrange("g p w -> p g w")))
        return its

    m_rows = MaxRows(lasting("max_rows_slot", 3))

    def attention(stage, dh, groups, ctx_keys=False, self_keys=False, causal=False, window=False, scale=1.0,
                  masked=False, query_mask=False, constants_kept=False):
        A = Attention(dh=dh, n=groups, ctx=ctx_keys, self_keys=self_keys, causal=causal, window=window, scale=scale,
                            masked=masked, query_mask=query_mask)
        A.s = sems(stage, AttentionSems, 18)
        A.nh = 4 if dh == 16 else 2
        A.slots = (3 if self_keys else 7) if dh == 16 else (2 if self_keys else 3)
        A.turn = 3
        A.loop = self_keys and not masked
        A.ahead = 1 if self_keys else 2
        A.pairs = A.nh // 2
        A.tiles = []
        for c in range(2):
            n_self = 0 if not self_keys else 4 * (c + 1) if causal else TB
            keys = [("ctx", 0)] * ctx_keys + [("self", j) for j in range(n_self)]
            for i, (kind, j) in enumerate(keys):
                diag = causal and kind == "self" and j >= 4 * c
                A.tiles.append(KeyTile(c=c, kind=kind, j=j, diag=diag, q0=P * (j - 4 * c) if diag else 0,
                                               first=i == 0, last=i == len(keys) - 1, index=len(A.tiles)))
        A.nt = len(A.tiles)
        A.nt0 = sum(t.c == 0 for t in A.tiles)
        A.steps = A.nt * A.pairs
        A.chunks = []
        if ctx_keys and not window:
            n, size = A.nh * TB, 5 if self_keys else 6
            A.chunks += [("ctx", i, min(size, n - i), 0) for i in range(0, n, size)]
        if self_keys:
            A.chunks += [("self", h, i, half) for h in range(A.nh) for i in range(TB) for half in range(2)
                         if not causal or i * P >= half * CH]
        A.outs = ("E",) if dh == 16 else ("D", "E")
        A.parts = 3 if dh == 16 else 2
        A.work = [order(A, r) for r in range(-1, A.n + 1)]
        A.rows_before = list(m_rows.total)
        for g in range(0 if window else groups):
            m_rows.total[g % 3] += 16 * A.parts
        q_loads, kv_loads = (3, 4 * (ctx_keys + self_keys)) if dh == 16 else (3, 4)
        A.loads = q_loads + kv_loads * self_keys
        A.first_loads = (13 if dh == 16 else 4) * (not self_keys)
        A.constants_kept = constants_kept
        return A

    def order(A, r):
        def products(dg):
            return [("A", dg, i) for i in range(len(A.chunks))]
        m = [("M", 1, 0)] * (not A.window)
        if r == -1:
            return [products(1) + m + (products(2) if A.ahead == 2 else [])]
        if r == A.n:
            return [[("C", -1, 1)] + [(w, -1, 1) for w in A.outs]]
        o = [[] for _ in range(A.nt + 1)]
        if r > 0:
            o[0].append(("C", -1, 1))
        if A.ahead == 2 and r + 1 < A.n:
            o[0] += m
        if r > 0:
            o[1] += [(w, -1, 1) for w in A.outs]
        start = 6 if A.self and A.dh == 64 else 0
        span = A.nt - 2 if A.ahead == 1 else A.nt + 1
        if r + A.ahead < A.n:
            for x in products(A.ahead):
                o[start + x[2] * (span - start) // len(A.chunks)].append(x)
        o[min(A.nt0 + 1, A.nt)].insert(0, ("C", 0, 0))
        o[min(A.nt0 + 2, A.nt)] += [(w, 0, 0) for w in A.outs]
        if A.ahead == 1 and r + 1 < A.n:
            o[span] = m + o[span]
        return o

    def numbered(A, i, r):
        def count(k):
            return sum(x[0] != "C" for items in A.work[k + 1] for x in items)
        first = sum(count(k) for k in range(-1, r))
        turn = sum(count(k + 1) for k in range(A.turn)) if A.loop else 0
        assert turn % 2 == 0
        n, res = 0, []
        for items in A.work[r + 1]:
            row = []
            for w, dg, k in items:
                row.append((w, dg, k, i * turn + (first + n), 6 + (first + n) % 2))
                n += w != "C"
            res.append(row)
        return res

    def each_step(A, e, run):
        run(0, -1)
        run(0, 0)
        if A.loop:
            with e.Fori(0, (A.n - 2) // A.turn) as i:
                for r in range(A.turn):
                    run(i, r + 1)
        else:
            for r in range(1, A.n - 1):
                run(0, r)
        run(0, A.n - 1)
        run(0, A.n)

    def loaded_value(A, i, k):
        return (i + (k // A.slots + 1)) * (16 * A.loads) + 16 * A.first_loads * (slot_of(A, k) == 0)

    def slot_of(A, k):
        return k % A.slots

    STK1 = STK[:, :, :].rearrange("p u n -> p (u n)")
    VS1 = VS[:, :, :].rearrange("p u n -> p (u n)")

    V_SLOTS = [VS[:, 0, :], VS[:, 1, :], WB[:, 2048:2048 + 1152]]

    def slot16(A, u):
        if A.self:
            at = u * (2048 + 2 * (P + T))
            q, k = STK1[:, at:at + 2048], STK1[:, at + 2048:at + 2048 + 2 * (P + T)]
        else:
            q, k = STK1[:, (u + 1) * 2048:(u + 2) * 2048], STK1[:, 0:2048]
        return q.bitcast(BF16).rearrange("p (h n) -> p h n", h=4), \
            k.bitcast(BF16).rearrange("p (h n) -> p h n", h=4 if A.self else 32)

    def slot64(A, u):
        if A.self:
            return [STK1[:, u * 8192 + 2048 * i:u * 8192 + 2048 * (i + 1)].rearrange("p (h n) -> p h n", h=2)
                    for i in range(4)]
        q = [STK1[:, u * 4096 + 2048 * i:u * 4096 + 2048 * (i + 1)] for i in range(2)]
        return [x.rearrange("p (h n) -> p h n", h=2) for x in q] + \
            [STK1[:, 12288 + 1024 * i:12288 + 1024 * (i + 1)].rearrange("p (h n) -> p h n", h=8) for i in range(2)]

    def head_of_k(A, g, h):
        return h if A.self else g * A.nh + h

    def slot_v(A, g, u):
        return V_SLOTS[u] if A.self else VS1[:, g * P:(g + 1) * P]

    def load_group(e, A, g, u):
        sem = A.s.loaded[u]
        if A.dh == 16:
            q, k = slot16(A, u)
            row = 0
            for (q0, q1), (k0, k1) in zip(Q_RUNS, K_RUNS):
                sl = slice(row, row + 16 * (q1 - q0))
                row = sl.stop
                def rows(parts, a, b):
                    m = parts[g // 2, a:b, :, 4 * (g % 2):4 * (g % 2) + 4, :]
                    return m.rearrange("k d h n -> (k d) h n")
                e.dma_start(q[sl, :, :], rows(Q3, q0, q1)).then_inc(sem, 16)
                if A.self:
                    e.dma_start(k[sl, :, P:P + T], rows(K3, k0, k1)).then_inc(sem, 16)
                    e.dma_start(k[sl, :, 0:SC], rows(C3.rearrange("b m k d h n -> (b m) k d h n"), k0, k1)).then_inc(sem, 16)
            if A.self:
                v = V16.rearrange("b g p t w -> (b g p) (t w)")
                e.dma_start(V_SLOTS[u][:, 128:1152], v[g * P:(g + 1) * P, 128:1152]).then_inc(sem, 16)
                e.dma_start(V_SLOTS[u][0:SC, 0:128], v[g * P:g * P + SC, 0:128]).then_inc(sem, 16)
        else:
            qa, qb, ka, kb = (x.bitcast(F32) for x in slot64(A, u))
            def rows(parts, part):
                return parts[part, g * P:(g + 1) * P, :].rearrange("(h d) n -> d h n", h=2)
            loads = [(qa[0:64], rows(Q2, 0)), (qa[64:P], rows(Q2, 1)), (qb[0:64], rows(Q2, 0))]
            if A.self:
                loads += [(ka[0:64], rows(K2, 0)), (ka[64:P], rows(K2, 0)), (kb[0:64], rows(K2, 1)),
                          (VS[:, u, 0:1024], V64.rearrange("b g p t w -> (b g) p (t w)")[g])]
            for dst, src in loads:
                e.dma_start(dst, src).then_inc(sem, 16)

    def load_context(e, A):
        sem = A.s.loaded[0]
        if A.dh == 16:
            k, V = slot16(A, 0)[1], V16
            loads = []
            for m in range(B * 2):
                row = 0
                for k0, k1 in K_RUNS:
                    src = C3[m // 2, m % 2, k0:k1].rearrange("k d h n -> (k d) h n")
                    loads.append((k[row:row + 16 * (k1 - k0), 8 * m:8 * m + 8, 0:SC], src))
                    row += 16 * (k1 - k0)
        else:
            (ka, kb), V = (x.bitcast(F32) for x in slot64(A, 0)[2:]), V64
            part = [C2[i].rearrange("(h d) n -> d h n", d=64) for i in range(2)]
            loads = [(ka[0:64, :, 0:SC], part[0]), (ka[64:P, :, 0:SC], part[0]), (kb[0:64, :, 0:SC], part[1])]
        loads.append((VS1[0:SC, 0:A.n * P].rearrange("p (g w) -> p g w", g=A.n),
                      V.rearrange("b g p t w -> p (b g) t w")[0:SC, :, 0, :]))
        for dst, src in loads:
            e.dma_start(dst, src).then_inc(sem, 16)

    def first_loads(e, A):
        e.wait_ge(A.s.cleared, 1)
        if not A.self:
            load_context(e, A)
        load_group(e, A, 0, 0)

    def attention_sync(e, A):
        s = A.s
        for g in range(1, A.n):
            need(e, s.pv_tile, (g - A.slots + 1) * A.nt)
            load_group(e, A, g, slot_of(A, g))

    def fill(e, where, value):
        e.memset(where, value)
        e.drain()

    def clear_slots(e, A):
        s = A.s
        if A.ctx:
            for u in range(A.slots if A.self else 1):
                fill(e, V_SLOTS[u][:, 0:P] if A.self else VS1[:, 0:A.n * P], 0.0)
        for u in range(0 if A.constants_kept else A.slots):
            if A.dh == 16:
                if A.self or u == 0:
                    k = slot16(A, u)[1]
                    fill(e, k[:, :, 0:P], 0.0)
                    fill(e, k[K16:K16 + M_ROWS, :, 0:SC], 1.0)
                if A.self:
                    fill(e, k[K16:K16 + M_ROWS, :, P:P + T], 1.0)
            else:
                qa, qb, ka, kb = (x.bitcast(F32) for x in slot64(A, u))
                fill(e, qb[64:96, :, :], 0.0)
                if A.self or u == 0:
                    if A.ctx:
                        fill(e, ka[:, :, :], 0.0)
                        fill(e, kb[0:64, :, :], 0.0)
                    fill(e, kb[64:96, :, :], 0.0)
                    fill(e, kb[64:66, :, 0:T if A.self else SC], 1.0)
        e.drain().then_inc(s.cleared, 1)

    def attention_gpsimd(e, A):
        s = A.s
        if A.window:
            return
        def run(i, r):
            k = r + 1
            if k >= A.n:
                return
            u = slot_of(A, k)
            e.wait_ge(s.loaded[u], loaded_value(A, i, k))
            e.wait_ge(s.max_split, i * A.turn + (k + 1))
            e.sem_inc(s.sending, 1)
            for part in range(A.parts):
                if A.dh == 16:
                    dst, src = slot16(A, u)[0][K16 + part:K16 + part + 1], MP[0:32, k % 3, part, :]
                else:
                    dst, src = slot64(A, u)[1][64 + part:65 + part].bitcast(F32), MPR[0:16, k % 3, part, :].bitcast(F32)
                e.dma_start(dst.rearrange("o h (t n) -> o (h t) n", n=P), src).then_inc(m_rows.sems[k % 3], 16)
        each_step(A, e, run)

    def attention_tensor(e, A):
        s = A.s

        def chunk(w, dg, k, n, bank, i, r):
            need(e, s.chunk_free, n - 1)
            if w == "A":
                v = slot_of(A, r + dg)
                if k == 0:
                    e.wait_ge(s.loaded[v], loaded_value(A, i, r + dg))
                kind, h, qt, half = A.chunks[k]
                q, keys = slot16(A, v) if A.dh == 16 else slot64(A, v)[0::2]
                rows = K16 if A.dh == 16 else P
                if kind == "ctx":
                    wide = SC if A.dh == 16 else SC + 1
                    for j in range(qt):
                        hj, tj = divmod(h + j, TB)
                        add_mask = A.masked and A.dh == 16
                        o = PS[:, bank, j * 80:j * 80 + wide]
                        m = e.matmul(o, q[0:rows, hj, tj * P:(tj + 1) * P],
                                     keys[0:rows, head_of_k(A, r + dg, hj), 0:wide], start=True, stop=not add_mask, skip_group_check=True)
                        if add_mask:
                            b = (r + dg) // (A.n // B)
                            m = e.matmul(o, IDB[:, :], MB[:, b * SC:(b + 1) * SC], start=False, stop=True,
                                         skip_group_check=True)
                else:
                    wide = min(CH, (qt + 1) * P - half * CH) if A.causal else CH
                    diag = A.causal and qt // 4 == half
                    k0 = half * CH + (P if A.dh == 16 else 0)
                    m = e.matmul(PS[:, bank, 0:wide], q[0:rows, h, qt * P:(qt + 1) * P], keys[0:rows, h, k0:k0 + wide],
                                 start=True, stop=not diag, skip_group_check=True)
                    if diag:
                        m = e.matmul(PS[:, bank, wide - P:wide], IDB[:, :], CM_S[:, :], start=False, stop=True,
                                     skip_group_check=True)
            elif w == "M":
                e.wait_ge(s.max_ready, i * A.turn + (r + dg + 1))
                m = e.transpose(PS[0:A.nh * TB, bank, 0:P], MX[:, 0:A.nh * TB], ID[:, :])
            else:
                e.wait_ge(s.copied, (i * A.turn + (r + dg)) * 2 + (k + 1))
                rows = OT[:, :] if w == "E" else OD[:, :]
                p = P if w == "E" else 64
                for j in range(4):
                    m = e.transpose(PS[:, bank, j * p:(j + 1) * p], rows[:, j * P:(j + 1) * P], ID[0:p, 0:p])
            m.then_inc(s.chunk_ready, 1)

        def scores(t, pair, i, r):
            st = t.index * A.pairs + pair
            need(e, s.gated if A.window else s.p_ready, (i * A.turn + r) * A.steps + (st - 1))
            for hh in range(2):
                h, bank = 2 * pair + hh, 2 * (st % 2) + hh
                o = PS[:, bank, 0:CH - t.q0]
                qs = slice(t.c * CH + t.q0, (t.c + 1) * CH)
                if A.dh == 16:
                    q, k = slot16(A, slot_of(A, r))
                    rows = K16 + M_ROWS * (not A.window)
                    k0 = 0 if t.kind == "ctx" else P + t.j * P
                    m = e.matmul(o, k[0:rows, head_of_k(A, r, h), k0:k0 + P], q[0:rows, h, qs], start=True, stop=not t.diag,
                                 skip_group_check=True)
                    if t.diag:
                        m = e.matmul(PS[:, bank, 0:P], IDB[:, :], CM_T[:, :], start=False, stop=True, skip_group_check=True)
                else:
                    qa, qb, ka, kb = slot64(A, slot_of(A, r))
                    ks = slice(t.j * P, (t.j + 1) * P)
                    hk = head_of_k(A, r, h)
                    e.matmul(o, ka[:, hk, ks], qa[:, h, qs], start=True, stop=False)
                    m = e.matmul(o, kb[0:96, hk, ks], qb[0:96, h, qs], start=False, stop=True)
            m.then_inc(s.s_ready, 1)

        def with_v(t, part, i, r):
            if part == 0:
                e.wait_ge(s.p_ready, (i * A.turn + r) * A.steps + (t.index + 1) * A.pairs)
                if t.first:
                    need(e, s.copied, (i * A.turn + r - 1) * 2 + (t.c + 1) if A.dh == 16 else (i * A.turn + r) * 2 + t.c)
            bank = 4 + t.c if A.dh == 16 else 4
            w = P // A.nh
            vt = t.j + (1 if t.kind == "self" and A.dh == 16 else 0)
            V = slot_v(A, r, slot_of(A, r))[:, vt * P:(vt + 1) * P].rearrange("p (h w) -> p h w", h=A.nh)
            for h in range(part * A.pairs, (part + 1) * A.pairs):
                m = e.matmul(PS[w * h:w * (h + 1), bank, t.q0:CH], V[:, h, :],
                             PB[:, t.index % 2, h // 2, h % 2, 0:CH - t.q0], start=t.first, stop=t.last,
                             skip_group_check=True)
                if A.dh == 64:
                    ones = ONESC if t.kind == "ctx" else ONES
                    m = e.matmul(PS[32 * h:32 * (h + 1), 5, :], ones[:, :], PB[:, t.index % 2, 0, h, :],
                                 start=t.first, stop=t.last, skip_group_check=True)
            if part == 1:
                m.then_inc(s.pv_tile, 1)

        def run(i, r):
            work = numbered(A, i, r)
            if A.window and 0 <= r < A.n:
                e.wait_ge(s.loaded[slot_of(A, r)], loaded_value(A, i, r))
            if r in (-1, A.n):
                for x in work[0]:
                    if x[0] != "C":
                        chunk(*x, i, r)
                return
            if not A.window:
                e.wait_ge(m_rows.sems[r % 3], (i + (r // 3 + 1)) * (16 * A.parts) + A.rows_before[r % 3])
            for idx in range(A.nt + 1):
                pieces = []
                if idx < A.nt:
                    pieces += [(scores, A.tiles[idx], k) for k in range(A.pairs)]
                if idx > 0:
                    pieces += [(with_v, A.tiles[idx - 1], k) for k in range(2)]
                chunks = [x for x in work[idx] if x[0] != "C"]
                done = 0
                for k, (piece, t, part) in enumerate(pieces):
                    piece(t, part, i, r)
                    upto = (k + 1) * len(chunks) // len(pieces)
                    for x in chunks[done:upto]:
                        chunk(*x, i, r)
                    done = upto
        each_step(A, e, run)

    def attention_scalar(e, A):
        s = A.s
        def run(i, r):
            if r in (-1, A.n):
                return
            g = i * A.turn + r
            for t in A.tiles:
                for pair in range(A.pairs):
                    st = t.index * A.pairs + pair
                    e.wait_ge(s.gated if A.window else s.s_ready, g * A.steps + (st + 1))
                    need(e, s.pv_tile, g * A.nt + (t.index - 1))
                    dst = PB[:, t.index % 2, pair, :, 0:CH - t.q0]
                    if A.window:
                        e.activation(dst, dst, ACT.Square, scale=A.scale).then_inc(s.p_ready, 1)
                    else:
                        bias = 0.0
                        if A.masked:
                            b = g // (A.n // B)
                            col = b if t.kind == "ctx" else b * TB + t.j
                            bias = KB[:, col:col + 1]
                        e.activation(dst, PS[:, 2 * (st % 2):2 * (st % 2) + 2, 0:CH - t.q0], ACT.Exp, scale=A.scale,
                                     bias=bias).then_inc(s.p_ready, 1)
        each_step(A, e, run)

    def attention_vector(e, A):
        s = A.s
        maxp = MXP[:, 0:A.nh * TB * 3].rearrange("p (h t s) -> p h t s", h=A.nh, t=TB)
        maxf = MXP[:, 0:A.nh * TB * 3].rearrange("p (h s) -> p h s", s=3)
        e.memset(MXP[:, :], LOWEST)
        e.drain()

        def gate(t, r, g):
            st = t.index * A.pairs + r
            e.wait_ge(s.s_ready, g * A.steps + (st + 1))
            need(e, s.pv_tile, g * A.nt + (t.index - 1))
            win = MB[:, ds(g // (A.n // B) * T + t.c * CH, CH)].unsqueeze(1).broadcast_to([P, 2, CH])
            e.scalar_tensor_tensor(PB[:, t.index % 2, r, :, :], PS[:, 2 * (st % 2):2 * (st % 2) + 2, :], 0.0, win,
                                   ALU.max, ALU.mult).then_inc(s.gated, 1)

        def part_of_max(i, n, bank, g):
            kind, h, qt, half = A.chunks[i]
            if A.masked and A.dh == 64:
                need(e, s.chunk_free, n)
            if kind == "ctx":
                src = PS[:, bank, 0:qt * 80].rearrange("p (j n) -> p j n", j=qt)[:, :, 0:SC]
                if A.masked and A.dh == 64:
                    m = MB[:, ds(g // (A.n // B) * SC, SC)].unsqueeze(1).broadcast_to([P, qt, SC])
                    tmp = SCR[:, 0:qt * SC].rearrange("p (j n) -> p j n", j=qt)
                    e.tensor_tensor(tmp, src, m, ALU.add)
                    e.drain()
                    src = tmp
                e.tensor_reduce(maxf[:, h:h + qt, 2], src, AX.X, ALU.max).then_inc(s.chunk_free, 1)
            elif A.masked:
                k0 = g // (A.n // B) * T + half * CH
                e.tensor_tensor_reduce(SCR[:, :], PS[:, bank, :], MB[:, k0:k0 + CH], 1.0, LOWEST, ALU.add, ALU.max,
                                       maxp[:, h, qt, half:half + 1]).then_inc(s.chunk_free, 1)
            else:
                wide = min(CH, (qt + 1) * P - half * CH)
                e.tensor_reduce(maxp[:, h, qt, half:half + 1], PS[:, bank, 0:wide], AX.X, ALU.max).then_inc(s.chunk_free, 1)
            if i == len(A.chunks) - 1:
                e.drain()
                e.tensor_reduce(MX[:, 0:A.nh * TB].rearrange("p (h t) -> p h t", h=A.nh), maxp, AX.X, ALU.max)\
                    .then_inc(s.max_ready, 1)

        def split_max(v, bank):
            w = A.nh * TB
            mt = MT[0:w, :]
            e.tensor_scalar(mt, PS[0:w, bank, 0:P], -1.0, None, ALU.mult).then_inc(s.chunk_free, 1)
            e.drain()
            if A.dh == 16:
                p1, p2, p3 = (MP[0:w, v, k, :] for k in range(3))
                e.tensor_copy(p1, mt)
                e.drain()
                e.tensor_tensor(mt, mt, p1, ALU.subtract)
                e.drain()
                e.tensor_copy(p2, mt)
                e.drain()
                e.tensor_tensor(p3, mt, p2, ALU.subtract).then_inc(s.max_split, 1)
            else:
                hi, lo = MPR[0:w, v, 0, :], MPR[0:w, v, 1, :]
                e.tensor_copy(hi, mt)
                e.drain()
                e.tensor_tensor(lo, mt, hi.bitcast(F32), ALU.subtract).then_inc(s.max_split, 1)

        def reciprocal(den, g, c):
            rc = RC[:, 0:4 * A.nh].rearrange("p (j h) -> p j h", j=4)
            if A.window:
                e.tensor_scalar(rc, den, 1e-6, None, ALU.max)
                e.drain()
                den = rc
            r = e.reciprocal(rc, den)
            if A.query_mask:
                t0 = g // (A.n // B) * TB + 4 * c
                e.drain()
                r = e.tensor_tensor(rc, rc, QM[:, t0:t0 + 4].unsqueeze(2).broadcast_to([P, 4, A.nh]), ALU.mult)
            return r

        def output(w, n, bank, g, c):
            if w == "D":
                den = PS[:, bank, 0:256].rearrange("p (j h w) -> p j h w", j=4, h=2)[:, :, :, 0]
                reciprocal(den, g, c).then_inc(s.chunk_free, 1)
                return
            o = PS[:, bank, :].rearrange("p (j h w) -> p j h w", j=4, h=A.nh)
            if A.dh == 16:
                reciprocal(o[:, :, :, 16], g, c)
            e.drain()
            per = A.n // B
            b = g // per
            dst = Y[:, :].rearrange("p (b c j g w) -> p b c j g w", b=B, c=2, j=4, g=per)[
                :, ds(b, 1), c, :, ds(g % per, 1), :].rearrange("p o j q (h w) -> p (o j q) h w", h=A.nh)
            rc = RC[:, 0:4 * A.nh].rearrange("p (j h) -> p j h", j=4).unsqueeze(3).broadcast_to([P, 4, A.nh, A.dh])
            e.tensor_tensor(dst, o[:, :, :, 0:A.dh], rc, ALU.mult).then_inc(s.chunk_free, 1)

        def run(i, r):
            g = i * A.turn + r
            for idx, items in enumerate(numbered(A, i, r)):
                if A.window and r not in (-1, A.n) and idx < A.nt:
                    for pair in range(A.pairs):
                        gate(A.tiles[idx], pair, g)
                for w, dg, k, n, bank in items:
                    if w == "C":
                        last = A.nt0 if k == 0 else A.nt
                        e.wait_ge(s.pv_tile, (g + dg) * A.nt + last)
                        if A.dh == 64:
                            e.tensor_copy(OD[:, :], PS[0:64, 5, :])
                        e.tensor_copy(OT[:, :], PS[:, 4 + k if A.dh == 16 else 4, :]).then_inc(s.copied, 1)
                        continue
                    e.wait_ge(s.chunk_ready, n + 1)
                    if w == "A":
                        part_of_max(k, n, bank, g + dg)
                    elif w == "M":
                        split_max((r + dg) % 3, bank)
                    else:
                        output(w, n, bank, g + dg, k)
        each_step(A, e, run)

    HID = Y[:, :].rearrange("p (m n) -> p m n", m=F // P)
    MT_F = F // P

    def ffn_tensor(e, s, w1, w2):
        def hidden(i):
            c, m = divmod(i, MT_F)
            need(e, s.hid_ready, i - 3)
            for k in range(KT):
                mm = e.matmul(PS[:, i % 4, :], w1[:, k, m * P:(m + 1) * P], XTF[:, k, c * CH:(c + 1) * CH],
                              start=k == 0, stop=k == KT - 1)
            mm.then_inc(s.hid_product, 1)

        def second(i):
            c, m = divmod(i, MT_F)
            e.wait_ge(s.hid_ready, i + 1)
            if m == 0:
                need(e, s.added, 2 * (c - 1))
            for t in range(4):
                mm = e.matmul(PS[:, 4 + 2 * (c % 2) + t // 2, t % 2 * D:(t % 2 + 1) * D], HID[:, m, t * P:(t + 1) * P],
                              w2[:, m, :], start=m == 0 and t % 2 == 0, stop=m == MT_F - 1, skip_group_check=True)
            mm.then_inc(s.hid_used, 1)
        n = NC * MT_F
        for i in range(n + 2):
            if i < n:
                hidden(i)
            if i >= 2:
                second(i - 2)

    def ffn_scalar(e, s, func, col):
        for i in range(NC * MT_F):
            e.wait_ge(s.hid_product, i + 1)
            need(e, s.hid_used, i - 7)
            m = i % MT_F
            e.activation(HID[:, m, :], PS[:, i % 4, :], func, bias=COL[:, col + m:col + m + 1]).then_inc(s.hid_ready, 1)

    def add_row(e, r):
        e.tensor_tensor(X[:, :, :], X[:, :, :], r.unsqueeze(1).broadcast_to([P, NT, D]), ALU.add)
        e.drain()

    def ffn_vector(e, s, b2):
        add_row(e, b2)
        for c in range(NC):
            e.wait_ge(s.hid_used, (c + 1) * MT_F)
            for k in range(2):
                x = X[:, 4 * c + 2 * k:4 * c + 2 * k + 2, :]
                e.tensor_tensor(x, x, PS[:, 4 + 2 * (c % 2) + k, :].rearrange("p (t d) -> p t d", t=2), ALU.add)\
                    .then_inc(s.added, 1)

    def square_tensor(e, s, w, base=0):
        for j in range(NT // 2):
            need(e, s.taken2, j - 3)
            for t in range(2):
                for k in range(KT):
                    tt = 2 * j + t
                    m = e.matmul(PS[:, j % 4, t * D:(t + 1) * D], XTF[:, k, tt * P:(tt + 1) * P], w[:, k, :],
                                 start=k == 0, stop=k == KT - 1, skip_group_check=True)
            m.then_inc(s.product2, 1)

    def square_vector(e, s, bias=None, leaky=None):
        if bias is not None:
            add_row(e, bias)
        for j in range(NT // 2):
            e.wait_ge(s.product2, j + 1)
            o = PS[:, j % 4, :].rearrange("p (t d) -> p t d", t=2)
            x = X[:, 2 * j:2 * j + 2, :]
            if leaky is None:
                e.tensor_tensor(x, x, o, ALU.add).then_inc(s.taken2, 1)
            else:
                y = SCR[:, :].rearrange("p (t d) -> p t d", t=2)
                z = OT[:, :].rearrange("p (t d) -> p t d", t=2)
                e.tensor_tensor(y, o, leaky.unsqueeze(1).broadcast_to([P, 2, D]), ALU.add).then_inc(s.taken2, 1)
                e.drain()
                e.scalar_tensor_tensor(z, y, 0.2, y, ALU.mult, ALU.max)
                e.drain()
                e.tensor_tensor(x, x, z, ALU.add)

    def add_attention(e):
        e.tensor_tensor(X2, X2, Y[:, :], ALU.add)
        e.drain()

    def key_masks_vector(e, layer):
        e.tensor_reduce(KSUM[:, :], X[:, :, :], AX.X, ALU.add)
        e.drain()
        e.tensor_scalar(QM[:, :], KSUM[:, :], 0.0, None, ALU.not_equal)
        if layer == 0:
            e.tensor_reduce(KC[0:SC, :], CTXN[0:SC, :, :], AX.X, ALU.add)
            e.drain()
            e.tensor_scalar(KZ[0:SC, 0:B], KC[0:SC, :], 0.0, None, ALU.is_equal)
            e.drain()
            e.tensor_scalar(KB[0:SC, 0:B], KZ[0:SC, 0:B], NEG1, None, ALU.mult)
        else:
            e.tensor_scalar(KZ[:, :], KSUM[:, :], 0.0, None, ALU.is_equal)
            e.drain()
            e.tensor_scalar(KB[:, :], KZ[:, :], NEG1, None, ALU.mult)

    turn = lambda n: sems(n, TurnSems, 2)
    sq = lambda n: sems(n, SquareSems, 2)
    ff = lambda n: sems(n, FeedForwardSems, 4)
    mk = lambda n: sems(n, KeyMaskSems, 5)

    L = [6 + 5 * l for l in range(3)]
    at0 = attention(3, 16, 8, ctx_keys=True, self_keys=True, causal=True, scale=0.25)
    at1 = [attention(L[0] + 2, 64, 4, ctx_keys=True, scale=0.125, masked=True, query_mask=True)] + \
          [attention(L[l] + 2, 64, 4, self_keys=True, scale=0.125, masked=True, query_mask=True, constants_kept=l == 2)
           for l in (1, 2)]
    at2 = attention(23, 16, 8, ctx_keys=True, window=True, scale=0.25)
    at3 = attention(28, 16, 8, ctx_keys=True, scale=0.0625, masked=True)
    p0, p1, p2, p3 = project(2), [project(l + 1) for l in L], project(22), project(27)
    ln0, ln02, ln0f = ln(1), ln(4), ln(4)
    ln1 = [ln(l + 3) for l in L]
    ln2, ln2c = ln(21), ln(21)
    ln3, ln3o = ln(31), ln(33)
    tn0, tn0c, tn0f = turn(1), turn(1), turn(4)
    tn1, tn1f, m1 = [turn(l) for l in L], [turn(l + 3) for l in L], [mk(l) for l in L]
    tn2, tn2c, tn2o = turn(21), turn(21), turn(24)
    tn3, tn3c, tn3o, tn3f = turn(26), turn(26), turn(29), turn(31)
    sq1, sq2, sq3 = [sq(l + 4) for l in L], sq(25), sq(30)
    ff0, ff3 = ff(5), ff(32)

    ID_F, RELU = ACT.Identity, ACT.Relu
    feat0 = q_items(W0.qkv, 0, q3_dst, COLS["L0q"], ID_F) + q_items(W0.qkv, D, k3_dst, COLS["L0k"], ID_F) + \
        c_items(W0.ckv, 0, c3_dst, COLS["L0c"], ID_F)
    val0 = v_items(W0.qkv, 2 * D, row(RA, ROWS_L0, "bv"), V16, 4, 1) + vc_items(W0.ckv, D, row(RA, ROWS_L0, "bcv"), V16, 4)
    feat1, val1 = [], []
    for l in range(3):
        w, bq, bk, bv = W1[l], COLS["L1q"] + 2 * l, COLS["L1k"] + 2 * l, row(RB, ROWS_L1, f"bv{l}")
        feat1.append(q_items(w["q"], 0, q2_dst, bq, RELU) +
                     (c_items(w["k"], 0, c2_dst, bk, RELU) if l == 0 else q_items(w["k"], 0, k2_dst, bk, RELU)))
        val1.append(vc_items(w["v"], 0, bv, V64, 2) if l == 0 else v_items(w["v"], 0, bv, V64, 2, 0))
    feat2 = q_items(W2["q"], 0, q3_dst, None, ID_F) + c_items(W2["k"], 0, c3_dst, None, ID_F)
    val2 = vc_items(W2["v"], 0, None, V16, 4)
    feat3 = q_items(W3.bd[3], 0, q3_dst, None, ID_F, diag=True) + c_items(W3.bd[4], 0, c3_dst, None, ID_F, diag=True)
    val3 = vc_items(W3.bd[2], 0, None, V16, 4, diag=True)

    r3 = lambda n: RA[:, ROWS_L3.index(n), :]
    r2 = lambda n: RA[:, 6 + ROWS_L2.index(n), :]

    block = ctx.enter_context(nc.Block())

    @block.sync
    def _(e):
        nxt = lambda: next_stage(e, "sync")
        load_sync(e)
        nxt()
        nxt()
        project_sync(e, p0, feat0, val0, 3, False)
        first_loads(e, at0)
        nxt()
        attention_sync(e, at0)
        nxt()
        nxt()
        nxt()
        load_block3(e)
        for l in range(3):
            if l == 0:
                load_layer(e, 1, ld.w1b)
            if l == 1:
                load_layer(e, 2, ld.w1c)
            if l == 2:
                load_block2(e)
            m = m1[l]
            n = B if l == 0 else NT
            p = SC if l == 0 else P
            e.wait_ge(m.row_cast, 1)
            km = KM.rearrange("t p -> (t p)")[0:n * p]
            e.dma_start(km.rearrange("(t p) -> t p", p=p), KZB[0:n, 0:p]).then_inc(m.stored, 16)
            e.wait_ge(m.stored, 16)
            e.dma_start(MB[:, 0:n * p], km.partition_broadcast(P)).then_inc(m.spread, 16)
            e.wait_ge(m.spread, 16)
            e.wait_ge([ld.w1a, ld.w1b, ld.w1c][l], 64)
            nxt()
            project_sync(e, p1[l], feat1[l], val1[l], 2, True)
            first_loads(e, at1[l])
            nxt()
            attention_sync(e, at1[l])
            nxt()
            nxt()
            nxt()
        e.dma_start(VS[:, :, :].rearrange("p u n -> p (u n)")[:, 0:TOK].bitcast(I32),
                    a["idx"].rearrange("b t -> (b t)").partition_broadcast(P)).then_inc(ld.masks, 16)
        e.wait_ge(ld.w2, 64)
        e.wait_ge(ld.w3, 16 * W3_LOADS)
        nxt()
        project_sync(e, p2, feat2, val2, 3, False)
        first_loads(e, at2)
        nxt()
        attention_sync(e, at2)
        nxt()
        nxt()
        nxt()
        e.dma_start(CTXN[0:SC, :, :], a["ctx"].rearrange("b s d -> s b d")).then_inc(ld.ctx, 16)
        e.wait_ge(ld.ctx, 16)
        nxt()
        project_sync(e, p3, feat3, val3, 3, False)
        first_loads(e, at3)
        nxt()
        attention_sync(e, at3)
        nxt()
        nxt()
        nxt()
        nxt()
        nxt()
        o = out.rearrange("b (t p) d -> p (b t) d", p=P)
        for c in range(NC):
            e.wait_ge(ln3o.normed, c + 1)
            e.dma_start(o[:, 4 * c:4 * c + 4, :], X[:, 4 * c:4 * c + 4, :]).then_inc(ld.out, 16)
        e.wait_ge(ld.out, 16 * NC)

    @block.gpsimd
    def _(e):
        nxt = lambda: next_stage(e, "gpsimd")
        load_pool(e)
        nxt()
        nxt()
        clear_slots(e, at0)
        nxt()
        attention_gpsimd(e, at0)
        nxt()
        nxt()
        nxt()
        e.memset(WA[:, 4608:4992], 0.0).then_inc(ld.cleared, 1)
        for l in range(3):
            nxt()
            clear_slots(e, at1[l])
            nxt()
            attention_gpsimd(e, at1[l])
            nxt()
            nxt()
            nxt()
        nxt()
        clear_slots(e, at2)
        nxt()
        attention_gpsimd(e, at2)
        for _ in range(4):
            nxt()
        clear_slots(e, at3)
        nxt()
        attention_gpsimd(e, at3)
        for _ in range(5):
            nxt()

    @block.tensor
    def _(e):
        nxt = lambda: next_stage(e, "tensor")
        nxt()
        turn_ctx_tensor(e, tn0c, CTXN)
        turn_tensor(e, tn0, tokens(Y3), ln0.normed, tn0c.taken)
        nxt()
        project_tensor(e, p0, feat0, val0)
        nxt()
        attention_tensor(e, at0)
        nxt()
        turn_tensor(e, tn0f, tokens(Y3), ln0f.normed)
        nxt()
        ffn_tensor(e, ff0, W0.w1, W0.w2)
        nxt()
        for l in range(3):
            turn_tensor(e, tn1[l], tokens(X))
            n, p = (B, SC) if l == 0 else (NT, P)
            e.wait_ge(m1[l].row_ready, 1)
            e.wait_ge(tn1[l].taken, 1)
            e.transpose(PS[0:n, 0, 0:p], KZ[0:p, 0:n], ID[0:p, 0:p]).then_inc(m1[l].turned, 1)
            nxt()
            project_tensor(e, p1[l], feat1[l], val1[l])
            nxt()
            attention_tensor(e, at1[l])
            nxt()
            turn_tensor(e, tn1f[l], tokens(X), ln1[l].normed)
            nxt()
            square_tensor(e, sq1[l], W1[l]["f"])
            nxt()
        turn_ctx_tensor(e, tn2c, CTXN, ln2c.normed)
        turn_tensor(e, tn2, tokens(Y3), ln2.normed, tn2c.taken)
        nxt()
        project_tensor(e, p2, feat2, val2)
        nxt()
        attention_tensor(e, at2)
        nxt()
        turn_tensor(e, tn2o, tokens(Y3))
        nxt()
        square_tensor(e, sq2, W2["o"])
        nxt()
        turn_ctx_tensor(e, tn3c, CTXN, ld.ctx, 16)
        turn_tensor(e, tn3, tokens(X), None, tn3c.taken)
        nxt()
        project_tensor(e, p3, feat3, val3)
        nxt()
        attention_tensor(e, at3)
        nxt()
        turn_tensor(e, tn3o, tokens(Y3))
        nxt()
        square_tensor(e, sq3, W3.out)
        nxt()
        turn_tensor(e, tn3f, tokens(X), ln3.normed)
        nxt()
        ffn_tensor(e, ff3, W3.w1, W3.w2)
        nxt()

    @block.scalar
    def _(e):
        nxt = lambda: next_stage(e, "scalar")
        nxt()
        turn_ctx_scalar(e, tn0c)
        ln_scalar(e, ln0)
        turn_scalar(e, tn0)
        nxt()
        project_scalar(e, p0, feat0)
        nxt()
        attention_scalar(e, at0)
        nxt()
        ln_scalar(e, ln02)
        ln_scalar(e, ln0f)
        turn_scalar(e, tn0f)
        nxt()
        ffn_scalar(e, ff0, ACT.Gelu, COLS["L0f"])
        nxt()
        for l in range(3):
            turn_scalar(e, tn1[l])
            n, p = (B, SC) if l == 0 else (NT, P)
            e.wait_ge(m1[l].turned, 1)
            e.activation(KZB[0:n, 0:p], PS[0:n, 0, 0:p], ACT.Copy, scale=NEG1 * 8).then_inc(m1[l].row_cast, 1)
            nxt()
            project_scalar(e, p1[l], feat1[l])
            nxt()
            attention_scalar(e, at1[l])
            nxt()
            ln_scalar(e, ln1[l])
            turn_scalar(e, tn1f[l])
            nxt()
            nxt()
        ln_scalar(e, ln2c, B, SC)
        turn_ctx_scalar(e, tn2c)
        ln_scalar(e, ln2)
        turn_scalar(e, tn2)
        nxt()
        project_scalar(e, p2, feat2)
        nxt()
        attention_scalar(e, at2)
        nxt()
        turn_scalar(e, tn2o)
        nxt()
        nxt()
        turn_ctx_scalar(e, tn3c)
        turn_scalar(e, tn3)
        nxt()
        project_scalar(e, p3, feat3)
        nxt()
        attention_scalar(e, at3)
        nxt()
        turn_scalar(e, tn3o)
        nxt()
        nxt()
        ln_scalar(e, ln3)
        turn_scalar(e, tn3f)
        nxt()
        ffn_scalar(e, ff3, ACT.Relu, COLS["L3f"])
        nxt()
        ln_scalar(e, ln3o)

    @block.vector
    def _(e):
        nxt = lambda: next_stage(e, "vector")
        nxt()
        ln_vector(e, ln0, X, Y3, row(RA, ROWS_L0, "g1"), row(RA, ROWS_L0, "be1"), "layer", 1e-5)
        nxt()
        project_vector(e, p0, feat0, val0, 3, False)
        nxt()
        attention_vector(e, at0)
        nxt()
        add_attention(e)
        ln_vector(e, ln02, X, Y3, row(RA, ROWS_L0, "g2"), row(RA, ROWS_L0, "be2"), "layer", 1e-5)
        e.drain()
        ln_vector(e, ln0f, Y3, Y3, row(RA, ROWS_L0, "gf"), row(RA, ROWS_L0, "bf"), "layer", 1e-5)
        nxt()
        ffn_vector(e, ff0, row(RA, ROWS_L0, "b2"))
        nxt()
        for l in range(3):
            key_masks_vector(e, l)
            e.drain().then_inc(m1[l].row_ready, 1)
            nxt()
            project_vector(e, p1[l], feat1[l], val1[l], 2, True)
            nxt()
            attention_vector(e, at1[l])
            nxt()
            add_attention(e)
            ln_vector(e, ln1[l], X, X, row(RB, ROWS_L1, f"gamma{l}"), row(RB, ROWS_L1, f"beta{l}"), "unbiased", 1e-8)
            nxt()
            square_vector(e, sq1[l], leaky=row(RB, ROWS_L1, f"bff{l}"))
            nxt()
        e.wait_ge(ld.w3, 16 * W3_LOADS)
        ln_vector(e, ln2c, CTXN, CTXN, r2("gkv"), None, "rms", 1.1920929e-07, B, SC, B)
        e.drain()
        ln_vector(e, ln2, X, Y3, r2("gq"), None, "rms", 1.1920929e-07)
        for j in range(2):
            e.tensor_copy(W3.bd[3 + j].rearrange("p (d h) -> p d h", h=8), W3.bd[j].rearrange("p (h d) -> p d h", h=8))
        e.wait_ge(ld.masks, 16)
        ix = VS[:, :, :].rearrange("p u n -> p (u n)")[:, 0:TOK]
        e.tensor_scalar(ix, ix.bitcast(I32), POS[:, 0:1], None, ALU.subtract)
        e.drain()
        e.tensor_tensor(ix, ix, ix, ALU.mult)
        e.drain()
        e.tensor_scalar(MB[:, :], ix, 1.0, None, ALU.is_le)
        nxt()
        project_vector(e, p2, feat2, val2, 3, False)
        nxt()
        attention_vector(e, at2)
        nxt()
        nxt()
        square_vector(e, sq2)
        nxt()
        e.tensor_scalar(MB[:, 0:B * SC], MI[:, 0:B * SC], 0.0, NEG3_ROUND, ALU.is_equal, ALU.mult)
        e.tensor_scalar(KB[0:SC, 0:B], MI[0:SC, B * SC:B * SC + B], 0.0, NEG3_ROUND / 16, ALU.is_equal, ALU.mult)
        nxt()
        project_vector(e, p3, feat3, val3, 3, False)
        nxt()
        attention_vector(e, at3)
        nxt()
        nxt()
        square_vector(e, sq3, bias=r3("bout"))
        nxt()
        ln_vector(e, ln3, X, X, r3("g1"), r3("beta1"), "layer", 1e-5)
        nxt()
        ffn_vector(e, ff3, r3("bff2"))
        nxt()
        ln_vector(e, ln3o, X, X, r3("g2"), r3("beta2"), "layer", 1e-5)


def kernel(**inputs):
    import numpy as np
    import concourse.bacc as bacc
    from concourse.bass_utils import run_bass_kernel_spmd

    g = {k: np.asarray(v) for k, v in inputs.items()}
    l0, l1, l2, l3 = (lambda n, p=f"L{i}_xattn_": g[p + n] for i in range(4))
    cols = lambda v: v.reshape(-1, P).T
    by = lambda v: np.concatenate([v[..., i:i + P].reshape(v.shape[:-1] + (8, 16)).swapaxes(-1, -2)
                                   .reshape(v.shape[:-1] + (P,)) for i in range(0, v.shape[-1], P)], axis=-1)
    qk = lambda v, n: np.concatenate([by(v[..., :n]), v[..., n:]], axis=-1)
    arrays = {
        "x": g["x"], "ctx": g["ctx_1024"], "idx": g["itok_BxS_0_255"],
        "mask": g["mask_Bx1x1xS2_if1"].reshape(B, SC),
        "w_qkv": qk(l0("w_qkv"), 2 * D), "w_ckv": qk(l0("w_ckv"), D), "w1": l0("w1"), "w2": l0("w2"),
        "Wq": l1("Wq"), "Wk": l1("Wk"), "Wv": l1("Wv"), "Wf": l1("Wff"),
        "W2q": by(l2("Wq").T), "W2k": by(l2("Wk").T), "W2v": l2("Wv").T, "W2o": l2("Wo").T,
        "w3q": l3("wq"), "w3k": l3("wk"), "w3v": l3("wv"), "w3_out": l3("w_out"), "w3_1": l3("w_ff1"), "w3_2": l3("w_ff2"),
        "rows0": np.stack([l0("b_qkv")[2 * D:], l0("b_ckv")[D:], l0("b2"), l0("g1"), l0("be1"), l0("g2"), l0("be2"),
                           l0("gf"), l0("bf")]),
        "rows1": np.concatenate([l1("bv"), l1("gamma"), l1("beta"), l1("bff")]),
        "rows23": np.stack([l3("b_out"), l3("g1"), l3("beta1"), l3("b_ff2"), l3("g2"), l3("beta2"),
                            l2("gamma_q"), l2("gamma_kv")]),
        "cols": np.concatenate([cols(by(l0("b_qkv")[:2 * D])), cols(by(l0("b_ckv")[:D])), cols(l0("b1")),
                                cols(l1("bq").reshape(-1)), cols(l1("bk").reshape(-1)), cols(l3("b_ff1"))], axis=1),
    }
    nc = bacc.Bacc("TRN2", target_bir_lowering=False, num_devices=1)
    sent, args = {}, {}
    for name, v in arrays.items():
        v = np.ascontiguousarray(v)
        sent[f"in_{name}"] = v
        args[name] = nc.dram_tensor(f"in_{name}", v.shape, mybir.dt.from_np(v.dtype), kind="ExternalInput").ap()
    res = nc.dram_tensor("out_0", (B, T, D), F32, kind="ExternalOutput").ap()
    build(nc, args, res)
    r = run_bass_kernel_spmd(nc, [sent], core_ids=[0])
    return r.results[0]["out_0"]
```

```python
from contextlib import ExitStack

import concourse.bass as bass
from concourse import mybir

F32 = mybir.dt.float32
F32R = mybir.dt.float32r
BF16 = mybir.dt.bfloat16
I32 = mybir.dt.int32
ALU = mybir.AluOpType
ACT = mybir.ActivationFunctionType
AX = mybir.AxisListType
ds = bass.ds

B, T, D, F, SC = 2, 1024, 256, 1024, 77
P = 128
TOK = B * T
NT = TOK // P
TB = T // P
CH = 512
NC = TOK // CH
KT = D // P

ROWS_L0 = ["bv", "bcv", "b2", "g2", "be2"]
ROWS_L1 = ["bv0", "bv1", "bv2", "gamma0", "gamma1", "gamma2", "beta0", "beta1", "beta2", "bff0", "bff1", "bff2"]
ROWS_L3 = ["bout", "g1", "beta1", "bff2", "g2", "beta2"]
COLS = {"L0q": 0, "L0k": 2, "L0c": 4, "L0f": 6, "L1q": 14, "L1k": 20, "L3f": 26, "g1": 34, "be1": 36,
        "gf": 38, "bf": 40, "gamma": 42, "beta": 48, "gq": 54, "L3g1": 56, "L3beta1": 58}
NCOLS = 60

MASKED = -1.0e37
NEG1 = -4294967296.0
NEG3_ROUND = -9.972771014849226e+19
LOWEST = -3.0e38

Q_RUNS = [(0, 3), (0, 2), (0, 1)]
K_RUNS = [(0, 3), (1, 3), (2, 3)]
K16 = 96
M_ROWS = 3
SEMAPHORES = 23


class LoadSems:
    def __init__(self, s):
        (self.x, self.w0, self.w1a, self.w1b, self.w1c, self.w2, self.w3, self.ctx, self.masks, self.cleared,
         self.out) = s[0:11]
        self.x_chunks = s[11:15]


class NormSems:
    def __init__(self, s):
        self.var_ready, self.std_ready, self.scale_ready, self.normed, self.weighted, self.finished = s


class TurnSems:
    def __init__(self, s):
        self.turned, self.taken = s


class SquareSems:
    def __init__(self, s):
        self.product2, self.taken2 = s


class FeedForwardSems:
    def __init__(self, s):
        self.hid_product, self.hid_ready, self.hid_high, self.hid_split, self.hid_used, self.added, \
            self.x_high, self.x_split = s


class SplitSems:
    def __init__(self, s):
        self.w_high, = s


class KeyMaskSems:
    def __init__(self, s):
        self.row_ready, self.turned, self.row_cast, self.stored, self.spread = s


class ProjectSems:
    def __init__(self, s):
        self.product, self.evacuated, self.split, self.step, self.v_product, self.v_taken, self.v_ready = s[0:7]
        self.stored, self.v_stored, self.first_part = s[7:11], s[11:15], s[15]


class AttentionSems:
    def __init__(self, s):
        (self.s_ready, self.p_ready, self.gated, self.pv_tile, self.copied, self.chunk_ready, self.chunk_free,
         self.max_ready, self.max_split, self.cleared, self.summed, self.denominated, self.tile_summed) = s[0:13]
        self.loaded = s[13:20]
        self.rows_sent = s[20:23]


class FeatureItem:
    def __init__(self, mms, n, func, bias, reverse, dst):
        self.mms, self.n, self.func, self.bias, self.reverse, self.dst = mms, n, func, bias, reverse, dst


class ValueItem:
    def __init__(self, mms, p, row, g, dst):
        self.mms, self.p, self.row, self.g, self.dst = mms, p, row, g, dst


class KeyTile:
    def __init__(self, c, kind, j, diag, q0, first, last, index):
        self.c, self.kind, self.j, self.diag, self.q0 = c, kind, j, diag, q0
        self.first, self.last, self.index = first, last, index


class Attention:
    def __init__(self, dh, n, ctx, self_keys, causal, window, scale, masked, query_mask):
        self.dh, self.n, self.ctx, self.self, self.causal = dh, n, ctx, self_keys, causal
        self.window, self.scale, self.masked, self.query_mask = window, scale, masked, query_mask


class Weights:
    def __init__(self, qkv=None, ckv=None, w1=None, w2=None, out=None, bd=None):
        self.qkv, self.ckv, self.w1, self.w2, self.out, self.bd = qkv, ckv, w1, w2, out, bd


def build(nc, a, out):
    with ExitStack() as ctx:
        program(nc, ctx, a, out)


def program(nc, ctx, a, out):
    def sb(name, shape, dt=F32):
        return ctx.enter_context(nc.sbuf_tensor(name, shape, dt))

    def lasting(prefix, n):
        return [ctx.enter_context(nc.semaphore(f"{prefix}_{i}")) for i in range(n)]

    sets = [[ctx.enter_context(nc.semaphore(f"set{r}_{i}")) for i in range(SEMAPHORES)] for r in range(3)]
    taken = {}

    def sems(stage, kind, count):
        n = taken.get(stage, 0)
        taken[stage] = n + count
        assert taken[stage] <= SEMAPHORES
        return kind(sets[stage % 3][n:n + count])

    def dram(name, shape, dt):
        return nc.dram_tensor(name, shape, dt, kind="Internal").ap()

    X = sb("x_res", [P, NT, D])
    Y = sb("y_tok", [P, NT * D])
    XT = sb("x_feat", [P, NT * D])
    WA = sb("w_even", [P, 6656])
    WB = sb("w_odd", [P, 4096])
    RA = sb("rows_even", [P, len(ROWS_L3) + 1, D])
    RB = sb("rows_odd", [P, len(ROWS_L1), D])
    STK = sb("stacks", [P, 2, 8192], F32R)
    VS = sb("v_group", [P, 2, 1152])
    OT = sb("o_feat", [P, CH])
    OD = sb("o_denom", [64, CH])
    SCR = sb("scratch", [P, CH])
    MB = sb("mask_rows", [P, TOK], BF16)
    COL = sb("cols", [P, NCOLS])
    CTXN = sb("ctx_tok", [P, B, D])
    CTXT = sb("ctx_feat", [P, KT, B * SC])
    ID = sb("ident", [P, P])
    IDB = sb("ident_bf", [P, P], BF16)
    CM_S = sb("causal_q_rows", [P, P], BF16)
    CM_T = sb("causal_k_rows", [P, P], BF16)
    ONES = sb("ones", [P, 32])
    ONESC = sb("ones_ctx", [P, 32])
    STATS = sb("stats", [P, NT, 6])
    MV = sb("mean_var", [P, NT, 2])
    VE = sb("var_eps", [P, NT])
    SD = sb("std", [P, NT])
    RS = sb("rstd", [P, NT])
    NB = sb("minus_mean_rstd", [P, NT])
    MXP = sb("max_parts", [P, 96])
    MX = sb("max_rows", [P, 32])
    MT = sb("neg_max", [32, P])
    MP = sb("neg_max_parts", [32, 3, 3, P], BF16)
    MPR = sb("neg_max_parts_r", [16, 3, 2, P], F32R)
    RC = sb("recip", [P, 16])
    KC = sb("ctx_key_sum", [P, B])
    KZ = sb("key_zero", [P, NT])
    KB = sb("key_bias", [P, NT])
    QM = sb("query_mask", [P, NT])
    KSUM = sb("key_sum", [P, NT])
    KZB = sb("key_zero_rows", [NT, P], BF16)
    MI = sb("mask_int", [P, B * SC + B], I32)
    POS = sb("position", [P, 1])
    POSI = sb("position_int", [P, 1], I32)
    PS = ctx.enter_context(nc.psum_tensor("banks", [P, 8, CH], F32))

    Y3 = Y[:, :].rearrange("p (t d) -> p t d", d=D)
    XTF = XT[:, :].rearrange("p (k n) -> p k n", k=KT)
    PSUMS = XT[:, :].rearrange("p (c r h n) -> p c r h n", c=2, r=2, h=2)[:, :, 1]
    PB = XT[:, :].rearrange("p (s r h n) -> p s r h n", s=2, r=2, h=2)

    Q3 = dram("q_parts", (B * 2, 3, 16, 8, T), BF16)
    K3 = dram("k_parts", (B * 2, 3, 16, 8, T), BF16)
    C3 = dram("kctx_parts", (3, 16, 8, 2, B, SC), BF16)
    Q2 = dram("q_parts_r", (2, B * D, T), F32)
    K2 = dram("k_parts_r", (2, B * D, T), F32)
    C2 = dram("kctx_parts_r", (2, D, B, SC), F32)
    V16 = dram("v16", (B, 4, P, 9, 128), F32)
    V64 = dram("v64", (B, 2, P, 8, 128), F32)
    KM = dram("key_mask_row", (NT, P), BF16)

    stage_done = ctx.enter_context(nc.semaphore("stage_done"))
    stages = {}

    def next_stage(e, who):
        e.drain().then_inc(stage_done, 1)
        stages[who] = stages.get(who, 0) + 1
        e.wait_ge(stage_done, 5 * stages[who])
        if who == "gpsimd":
            for sem in sets[(stages[who] - 1) % 3]:
                e.sem_clear(sem)

    def need(e, sem, value):
        if not (isinstance(value, int) and value <= 0):
            e.wait_ge(sem, value)

    def wview(W, off, k, n):
        return W[:, off:off + k * n].rearrange("p (k n) -> p k n", k=k)

    W0 = Weights(qkv=wview(WA, 0, KT, 768), ckv=wview(WA, 1536, KT, 512),
                         w1=wview(WA, 2560, KT, F), w2=wview(WA, 4608, F // P, D))
    W1 = [{n: wview(WB, (l % 2 * 4 + j) * 512, KT, D) for j, n in enumerate("qkvf")} for l in range(3)]
    W2 = {n: wview(WB, 2048 + j * 512, KT, D) for j, n in enumerate("qkvo")}
    W3 = Weights(w1=wview(WA, 0, KT, F), w2=wview(WA, 2048, F // P, D), out=wview(WA, 4096, KT, D),
                         bd=[WA[:, 4608 + 128 * j:4608 + 128 * (j + 1)] for j in range(5)])

    def row(R, names, name):
        return R[:, names.index(name), :]

    ld = LoadSems(lasting("load", 15))

    def kp(w):
        return w.rearrange("(k p) n -> p k n", p=P)

    def load_sync(e):
        xs = a["x"].rearrange("b (t p) d -> p (b t) d", p=P)
        for c in range(NC):
            e.dma_start(X[:, 4 * c:4 * c + 4, :], xs[:, 4 * c:4 * c + 4, :]).then_inc(ld.x_chunks[c], 16)
            if c == 0:
                e.dma_start(COL[:, :], a["cols"]).then_inc(ld.x, 16)
                e.dma_start(CTXN[0:SC, :, :], a["ctx"].rearrange("b s d -> s b d")).then_inc(ld.x, 16)
        for w, name in ((W0.qkv, "w_qkv"), (W0.ckv, "w_ckv")):
            e.dma_start(w, kp(a[name])).then_inc(ld.w0, 16)
        e.dma_start(RA[:, 0:len(ROWS_L0), :], a["rows0"].partition_broadcast(P)).then_inc(ld.w0, 16)
        e.wait_ge(ld.x, 32)

    def load_more(e):
        for w, name in ((W0.w1, "w1"), (W0.w2, "w2")):
            e.dma_start(w, kp(a[name])).then_inc(ld.w1c, 16)
        e.dma_start(RB[:, :, :], a["rows1"].partition_broadcast(P)).then_inc(ld.w1a, 16)
        load_layer(e, 0, ld.w1a)

    def load_layer(e, l, sem):
        for n in "qkvf":
            e.dma_start(W1[l][n], kp(a["W" + n][l])).then_inc(sem, 16)

    def load_block2(e):
        for n in "qkvo":
            e.dma_start(W2[n], kp(a["W2" + n])).then_inc(ld.w2, 16)

    def load_block3(e):
        e.dma_start(RA[:, :, :], a["rows23"].partition_broadcast(P)).then_inc(ld.w3, 16)
        for w, n in ((W3.w1, "w3_1"), (W3.w2, "w3_2"), (W3.out, "w3_out")):
            e.dma_start(w, kp(a[n])).then_inc(ld.w3, 16)
        e.wait_ge(ld.cleared, 1)
        for j, n in enumerate("qkv"):
            for h in range(8):
                e.dma_start(W3.bd[j][16 * h:16 * h + 16, 16 * h:16 * h + 16], a["w3" + n]).then_inc(ld.w3, 16)
        e.dma_start(MI[:, 0:B * SC], a["mask"].rearrange("b s -> (b s)").partition_broadcast(P)).then_inc(ld.w3, 16)
        e.dma_start(MI[0:SC, B * SC:B * SC + B], a["mask"].rearrange("b s -> s b"), allow_slow_non_contiguous=True).then_inc(ld.w3, 16)
    W3_LOADS = 4 + 24 + 2

    def load_pool(e):
        fill(e, ID[:, :], 0.0)
        fill(e, IDB[:, :], 0.0)
        fill(e, CM_S[:, :], 0.0)
        fill(e, CM_T[:, :], 0.0)
        fill(e, ONES[:, :], 1.0)
        fill(e, ONESC[:, :], 1.0)
        fill(e, KB[:, :], 0.0)
        e.iota(POSI[:, :], pattern=[[0, 1]], base=0, channel_multiplier=1)
        e.drain()
        e.tensor_copy(POS[:, :], POSI[:, :])
        e.drain()
        for m in (ID, IDB):
            e.affine_select(out=m[:, :], in_=m[:, :], compare_op=ALU.not_equal, fill=1.0,
                            base=0, pattern=[[-1, P]], channel_multiplier=1)
            e.drain()
        e.drain()
        e.affine_select(out=ONESC[:, :], in_=ONESC[:, :], compare_op=ALU.is_ge, fill=0.0,
                        base=SC - 1, pattern=[[0, 32]], channel_multiplier=-1)
        e.drain()
        e.affine_select(out=CM_S[:, :], in_=CM_S[:, :], compare_op=ALU.is_ge, fill=MASKED,
                        base=0, pattern=[[-1, P]], channel_multiplier=1)
        e.drain()
        e.affine_select(out=CM_T[:, :], in_=CM_T[:, :], compare_op=ALU.is_ge, fill=MASKED,
                        base=0, pattern=[[1, P]], channel_multiplier=-1)

    def ln(stage):
        return sems(stage, NormSems, 6)

    def four(src3, c, p=P):
        return src3[0:p, 4 * c:4 * c + 4, :]

    def wide(r):
        return r.unsqueeze(1).broadcast_to([P, 4, D])

    def ln_steps(e, s, src, mode, eps, add=None, weighted=None, arrived=None):
        def statistics(c):
            if arrived is not None:
                e.wait_ge(arrived[c], 16)
            if add is not None:
                e.tensor_tensor(four(src, c), four(src, c), four(add, c), ALU.add)
                e.drain()
            for t in range(4 * c, 4 * c + 4):
                e.bn_stats(STATS[:, t, :], src[:, t, :])
            e.drain()
            for t in range(4 * c, 4 * c + 4):
                e.bn_aggr(MV[:, t, :], STATS[:, t, :])
            e.drain()
            v = slice(4 * c, 4 * c + 4)
            mean, var = MV[:, v, 0], MV[:, v, 1]
            if mode == "rms":
                e.tensor_tensor(VE[:, v], mean, mean, ALU.mult)
                e.drain()
                e.scalar_tensor_tensor(VE[:, v], VE[:, v], eps, var, ALU.add, ALU.add).then_inc(s.var_ready, 1)
            elif mode == "unbiased":
                e.tensor_scalar(VE[:, v], var, D / (D - 1.0), None, ALU.mult).then_inc(s.var_ready, 1)
            else:
                e.tensor_scalar(VE[:, v], var, eps, None, ALU.add).then_inc(s.var_ready, 1)

        def scales(c):
            v = slice(4 * c, 4 * c + 4)
            e.wait_ge(s.std_ready, c + 1)
            if mode == "unbiased":
                e.tensor_scalar(SD[:, v], SD[:, v], eps, None, ALU.add)
                e.drain()
            if mode == "rms":
                e.reciprocal(RS[:, v], SD[:, v]).then_inc(s.scale_ready, 1)
                return
            e.reciprocal(RS[:, v], SD[:, v])
            e.drain()
            e.scalar_tensor_tensor(NB[:, v], MV[:, v, 0], -1.0, RS[:, v], ALU.mult, ALU.mult).then_inc(s.scale_ready, 1)

        def add_bias(c):
            e.wait_ge(s.weighted, c + 1)
            e.tensor_tensor(four(weighted[0], c), four(weighted[0], c), wide(weighted[1]), ALU.add).then_inc(s.finished, 1)

        return statistics, scales, add_bias

    def ln_vector(e, s, src, mode, eps, add=None, weighted=None, arrived=None):
        statistics, scales, add_bias = ln_steps(e, s, src, mode, eps, add, weighted, arrived)
        for c in range(NC + 1):
            if c < NC:
                statistics(c)
            if c > 0:
                scales(c - 1)
            if weighted and c > 2:
                add_bias(c - 3)
        if weighted:
            for c in range(NC - 2, NC):
                add_bias(c)

    def ln_gpsimd(e, s, z, g, dst):
        for c in range(NC):
            e.wait_ge(s.normed, c + 1)
            e.tensor_tensor(four(dst, c), four(z, c), wide(g), ALU.mult).then_inc(s.weighted, 1)

    def square_root(e, s, c):
        v = slice(4 * c, 4 * c + 4)
        e.wait_ge(s.var_ready, c + 1)
        e.activation(SD[:, v], VE[:, v], ACT.Sqrt).then_inc(s.std_ready, 1)

    def normalise(e, s, c, src, dst, mode):
        e.wait_ge(s.scale_ready, c + 1)
        for t in range(4 * c, 4 * c + 4):
            z = e.activation(dst[:, t, :], src[:, t, :], ACT.Identity, scale=RS[:, t:t + 1],
                             bias=0.0 if mode == "rms" else NB[:, t:t + 1])
        z.then_inc(s.normed, 1)

    def ln_scalar(e, s, src, dst, mode, tn=None, cols=None):
        for c in range(NC + 2):
            if c < NC:
                square_root(e, s, c)
            if 0 < c <= NC:
                normalise(e, s, c - 1, src, dst, mode)
            if tn is not None and c > 1:
                take_turned(e, tn, c - 2, cols)

    def ctx_rms_vector(e, s, g, eps):
        for b in range(B):
            e.bn_stats(STATS[0:SC, b, :], CTXN[0:SC, b, :])
        e.drain()
        for b in range(B):
            e.bn_aggr(MV[0:SC, b, :], STATS[0:SC, b, :])
        e.drain()
        mean, var = MV[0:SC, 0:B, 0], MV[0:SC, 0:B, 1]
        e.tensor_tensor(VE[0:SC, 0:B], mean, mean, ALU.mult)
        e.drain()
        e.scalar_tensor_tensor(VE[0:SC, 0:B], VE[0:SC, 0:B], eps, var, ALU.add, ALU.add).then_inc(s.var_ready, 1)
        e.wait_ge(s.std_ready, 1)
        e.reciprocal(RS[0:SC, 0:B], SD[0:SC, 0:B])
        e.drain()
        for b in range(B):
            e.scalar_tensor_tensor(CTXN[0:SC, b, :], CTXN[0:SC, b, :], RS[0:SC, b:b + 1], g[0:SC, :],
                                   ALU.mult, ALU.mult).then_inc(s.normed, 1)

    def ctx_rms_scalar(e, s):
        e.wait_ge(s.var_ready, 1)
        e.activation(SD[0:SC, 0:B], VE[0:SC, 0:B], ACT.Sqrt).then_inc(s.std_ready, 1)

    def turn_chunk(e, s, c, src, ready=None):
        if ready is not None:
            e.wait_ge(ready, c + 1)
        for k in range(KT):
            n = 2 * c + k
            need(e, s.taken, n - 3)
            for j in range(4):
                t = e.transpose(PS[:, 4 + n % 4, j * P:(j + 1) * P], src(4 * c + j, k), ID[:, :])
            t.then_inc(s.turned, 1)

    def take_turned(e, s, c, cols=None):
        for k in range(KT):
            n = 2 * c + k
            scale, bias = cols or (None, None)
            e.wait_ge(s.turned, n + 1)
            e.activation(XTF[:, k, c * CH:(c + 1) * CH], PS[:, 4 + n % 4, :], ACT.Identity,
                         scale=1.0 if scale is None else COL[:, scale + k:scale + k + 1],
                         bias=0.0 if bias is None else COL[:, bias + k:bias + k + 1]).then_inc(s.taken, 1)

    def turn_tensor(e, s, src, ready=None):
        for c in range(NC):
            turn_chunk(e, s, c, src, ready)

    def turn_scalar(e, s, cols=None):
        for c in range(NC):
            take_turned(e, s, c, cols)

    def turn_square_tensor(e, tn, sq, w, src, ready=None):
        for c in range(NC + 1):
            if c < NC:
                turn_chunk(e, tn, c, src, ready)
            if c > 0:
                e.wait_ge(tn.taken, 2 * c)
                square_tensor(e, sq, w, range(2 * c - 2, 2 * c))

    def tokens(src3):
        return lambda t, k: src3[:, t, k * P:(k + 1) * P]

    def turn_ctx_tensor(e, s, src, ready=None, value=1):
        if ready is not None:
            e.wait_ge(ready, value)
        for b in range(B):
            for k in range(KT):
                e.transpose(PS[:, 3, (k * B + b) * P:(k * B + b) * P + SC], src[0:SC, b, k * P:(k + 1) * P],
                            ID[0:SC, 0:SC]).then_inc(s.turned, 1)

    def turn_ctx_scalar(e, s):
        e.wait_ge(s.turned, B * KT)
        e.activation(CTXT[:, :, :].rearrange("p k (b n) -> p k b n", b=B),
                     PS[:, 3, :].rearrange("p (k b n) -> p k b n", k=KT, b=B)[:, :, :, 0:SC],
                     ACT.Copy).then_inc(s.taken, 1)

    RBUF = Y[:, 0:1024].rearrange("p (s n) -> p s n", s=2)
    P3 = Y[:, 1024:4096].bitcast(BF16).rearrange("p (s k n) -> p s k n", s=4, k=3)
    P2 = [x.rearrange("p (k n) -> p k n", k=2) for x in
          [Y[:, 1024 * i:1024 * (i + 1)].bitcast(F32R) for i in (1, 2, 3)] + [STK[:, 1, 0:1024]]]
    VT = [SCR[:, :], OT[:, :], VS[:, 1, P:P + CH], VS[:, 1, P + CH:P + 2 * CH]]

    def part(parts, it, i, k):
        k = parts - 1 - k if it.reverse else k
        return (P3[:, i % 4] if parts == 3 else P2[i % 4])[:, k, 0:it.n]

    def in_order(sections):
        nf = nv = 0
        for feat, vals in sections:
            for it in feat:
                yield True, it, nf
                nf += 1
            for v in vals:
                yield False, v, nv
                nv += 1

    def project_tensor(e, s, sections):
        for is_feature, it, i in in_order(sections):
            if is_feature:
                need(e, s.split, i - 3)
                for j, (l, r) in enumerate(it.mms):
                    m = e.matmul(PS[0:P, i % 4, 0:it.n], l, r, start=(j == 0), stop=(j == len(it.mms) - 1))
                m.then_inc(s.product, 1)
            else:
                need(e, s.v_taken, i - 3)
                for sl, mms in it.mms:
                    for j, (l, r) in enumerate(mms):
                        m = e.matmul(PS[0:it.p, 4 + i % 4, sl], l, r, start=(j == 0), stop=(j == len(mms) - 1))
                m.then_inc(s.v_product, 1)

    def project_scalar(e, s, sections, parts):
        for is_feature, it, i in in_order(sections):
            if not is_feature:
                continue
            e.wait_ge(s.product, i + 1)
            need(e, s.split, i - 1)
            e.activation(RBUF[:, i % 2, 0:it.n], PS[:, i % 4, 0:it.n], it.func, bias=it.bias).then_inc(s.evacuated, 1)
            if i >= 4:
                e.wait_ge(s.stored[i % 4], 16 * (i // 4))
            e.activation(part(parts, it, i, 0), PS[:, i % 4, 0:it.n], it.func, bias=it.bias).then_inc(s.first_part, 1)

    def project_vector(e, s, sections, parts, relu):
        steps = 0
        def step(ins):
            nonlocal steps
            ins.then_inc(s.step, 1)
            steps += 1
            e.wait_ge(s.step, steps)
        vw = 32 if parts == 3 else 64
        hv = D // (16 if parts == 3 else 64)
        if parts == 3:
            for v in VT[1:min(4, sum(len(x[1]) for x in sections))]:
                e.memset(v, 1.0)
            step(e.memset(VT[0], 1.0))
        def value(v, i):
            e.wait_ge(s.v_product, i + 1)
            if i >= 4:
                e.wait_ge(s.v_stored[i % 4], 16 * (i // 4))
            dst = VT[i % 4][0:v.p, 0:hv * vw].rearrange("p (h w) -> p h w", w=vw)[:, :, 0:D // hv]
            src = PS[0:v.p, 4 + i % 4, 0:D].rearrange("p (h w) -> p h w", h=hv)
            if v.row is None:
                e.tensor_copy(dst, src).then_inc(s.v_taken, 1)
            else:
                r = v.row[0:v.p, :].rearrange("p (h w) -> p h w", h=hv)
                e.tensor_tensor(dst, src, r, ALU.add).then_inc(s.v_taken, 1)
            if relu:
                e.wait_ge(s.v_taken, i + 1)
                e.tensor_scalar(dst, dst, 0.0, None, ALU.max).then_inc(s.v_ready, 1)
        for is_feature, it, i in in_order(sections):
            if not is_feature:
                value(it, i)
                continue
            e.wait_ge(s.first_part, i + 1)
            r = RBUF[:, i % 2, 0:it.n]
            p1 = part(parts, it, i, 0)
            if parts == 3:
                p2, p3 = (part(parts, it, i, k) for k in (1, 2))
                step(e.tensor_tensor(r, r, p1, ALU.subtract))
                step(e.tensor_copy(p2, r))
                e.tensor_tensor(p3, r, p2, ALU.subtract).then_inc(s.split, 1)
            else:
                e.tensor_tensor(part(parts, it, i, 1), r, p1.bitcast(F32), ALU.subtract).then_inc(s.split, 1)

    def project_sync(e, s, sections, parts, relu, A):
        def stored_after(feat, val):
            for u in range(4):
                need(e, s.stored[u], 16 * ((feat + 3 - u) // 4))
            for u in range(4):
                need(e, s.v_stored[u], 16 * ((val + 3 - u) // 4))
        loads, feat, val = [], 0, 0
        for k, (f, v) in enumerate(sections[:-1]):
            feat, val = feat + len(f), val + len(v)
            loads.append((feat + val + 1, load_context if k == 0 and not A.self else load_first, feat, val))
        nf = nv = 0
        pieces = [0] * len(loads)
        def load(k, upto):
            if pieces[k] == 0:
                stored_after(*loads[k][2:])
                if k == 0:
                    e.wait_ge(A.s.cleared, 1)
            while pieces[k] < upto:
                loads[k][1](e, A, pieces[k])
                pieces[k] += 1
        for number, (is_feature, it, i) in enumerate(in_order(sections)):
            if is_feature:
                e.wait_ge(s.split, i + 1)
                src = P3[:, i % 4] if parts == 3 else P2[i % 4].bitcast(F32)
                e.dma_start(it.dst, src[:, :, 0:it.n]).then_inc(s.stored[i % 4], 16)
                nf += 1
            else:
                e.wait_ge(s.v_ready if relu else s.v_taken, i + 1)
                e.dma_start(it.dst, VT[i % 4][0:it.p, 0:it.g * 128].rearrange("p (g w) -> p g w", g=it.g))\
                    .then_inc(s.v_stored[i % 4], 16)
                nv += 1
            for k, x in enumerate(loads):
                if number + 1 >= x[0] and pieces[k] < LOAD_PIECES:
                    load(k, pieces[k] + 1)
        for k in range(len(loads)):
            if pieces[k] < LOAD_PIECES:
                load(k, LOAD_PIECES)
        stored_after(nf, nv)

    def project(stage):
        return sems(stage, ProjectSems, 16)

    def q_items(b, w, off, dst, bias, func, diag=False):
        its = []
        for half in range(T // CH):
            c = b * (T // CH) + half
            for m in range(KT):
                if diag:
                    mms = [(w, XTF[:, m, c * CH:(c + 1) * CH])]
                else:
                    mms = [(w[:, k, off + m * P:off + (m + 1) * P], XTF[:, k, c * CH:(c + 1) * CH]) for k in range(KT)]
                its.append(FeatureItem(
                    mms=mms, n=CH, func=func, bias=0.0 if bias is None else COL[:, bias + m:bias + m + 1],
                    reverse=dst is k3_dst, dst=dst(b, m)[:, :, half * CH:(half + 1) * CH]))
        return its

    def c_items(w, off, dst, bias, func, diag=False):
        its = []
        for m in range(KT):
            if diag:
                mms = [(w, CTXT[:, m, :])]
            else:
                mms = [(w[:, k, off + m * P:off + (m + 1) * P], CTXT[:, k, :]) for k in range(KT)]
            its.append(FeatureItem(
                mms=mms, n=B * SC, func=func, bias=0.0 if bias is None else COL[:, bias + m:bias + m + 1],
                reverse=dst is c3_dst, dst=dst(m)))
        return its

    q3_dst = lambda b, m: Q3[b * 2 + m].rearrange("k d h n -> (d h) k n")
    k3_dst = lambda b, m: K3[b * 2 + m].rearrange("k d h n -> (d h) k n")
    c3_dst = lambda m: C3[:, :, :, m].rearrange("k d h b n -> (d h) k (b n)")
    q2_dst = lambda b, m: Q2[:, b * D + m * P:b * D + (m + 1) * P, :].rearrange("k f n -> f k n")
    k2_dst = lambda b, m: K2[:, b * D + m * P:b * D + (m + 1) * P, :].rearrange("k f n -> f k n")
    c2_dst = lambda m: C2[:, m * P:(m + 1) * P].rearrange("k f b n -> f k (b n)")

    def v_items(b, w, off, rowv, dst, ngroup, tile0):
        its = []
        for t in range(b * TB, (b + 1) * TB):
            mms = [(XTF[:, k, t * P:(t + 1) * P], w[:, k, off:off + D]) for k in range(KT)]
            its.append(ValueItem(mms=[(slice(0, D), mms)], p=P, row=rowv, g=ngroup,
                                       dst=dst[b, :, :, t % TB + tile0, :].rearrange("g p w -> p g w")))
        return its

    def vc_items(w, off, rowv, dst, ngroup, diag=False):
        its = []
        for b in range(B):
            lhs = [CTXT[:, k, b * SC:(b + 1) * SC] for k in range(KT)]
            if diag:
                mms = [(slice(k * P, (k + 1) * P), [(lhs[k], w)]) for k in range(KT)]
            else:
                mms = [(slice(0, D), [(lhs[k], w[:, k, off:off + D]) for k in range(KT)])]
            its.append(ValueItem(mms=mms, p=SC, row=rowv, g=ngroup,
                                       dst=dst[b, :, 0:SC, 0, :].rearrange("g p w -> p g w")))
        return its


    def attention(stage, dh, groups, ctx_keys=False, self_keys=False, causal=False, window=False, scale=1.0,
                  masked=False, query_mask=False, constants_kept=False):
        A = Attention(dh=dh, n=groups, ctx=ctx_keys, self_keys=self_keys, causal=causal, window=window, scale=scale,
                            masked=masked, query_mask=query_mask)
        A.sums = dh == 64 and self_keys
        A.s = sems(stage, AttentionSems, 23)
        A.nh = 4 if dh == 16 else 2
        A.slots = (3 if self_keys else 7) if dh == 16 else (2 if self_keys else 3)
        A.turn = 3
        A.loop = self_keys and not masked
        A.ahead = 1 if self_keys else 2
        A.pairs = A.nh // 2
        A.tiles = []
        for c in range(2):
            n_self = 0 if not self_keys else 4 * (c + 1) if causal else TB
            keys = [("ctx", 0)] * ctx_keys + [("self", j) for j in range(n_self)]
            keys.sort(key=lambda x: (x[0] == "self") + (x[0] == "self" and not (causal and x[1] >= 4 * c)))
            for i, (kind, j) in enumerate(keys):
                diag = causal and kind == "self" and j >= 4 * c
                A.tiles.append(KeyTile(c=c, kind=kind, j=j, diag=diag, q0=P * (j - 4 * c) if diag else 0,
                                               first=i == 0, last=i == len(keys) - 1, index=len(A.tiles)))
        A.nt = len(A.tiles)
        A.nt0 = sum(t.c == 0 for t in A.tiles)
        A.steps = A.nt * A.pairs
        A.chunks = []
        if ctx_keys and not window:
            n, size = A.nh * TB, 5 if self_keys else 6
            A.chunks += [("ctx", i, min(size, n - i), 0) for i in range(0, n, size)]
        if self_keys:
            products = [[(i, half)] for i in range(TB) for half in range(2)]
            if causal:
                products = [[(i, 0)] for i in range(3, TB)] + [[(7, 1)], [(0, 0), (2, 0)], [(4, 1), (6, 1)], [(1, 0), (5, 1)]]
            A.chunks += [("self", h, p, 0) for h in range(A.nh) for p in products]
        A.outs = ("E",) if dh == 16 else ("D", "E")
        A.parts = 3 if dh == 16 else 2
        A.work = [order(A, r) for r in range(-1, A.n + 1)]
        q_loads, kv_loads = (3, 4 * (ctx_keys + self_keys)) if dh == 16 else (3, 4)
        A.loads = q_loads + kv_loads * self_keys
        if dh == 64 and self_keys:
            A.loads = 4
        A.first_loads = (4 if dh == 16 else 7) * (not self_keys)
        A.constants_kept = constants_kept
        return A

    def order(A, r):
        def products(dg):
            return [("A", dg, i) for i in range(len(A.chunks))]
        m = [("M", 1, 0)] * (not A.window)
        if r == -1:
            return [products(1) + m + (products(2) if A.ahead == 2 else [])]
        if r == A.n:
            return [[("C", -1, 1)] + [(w, -1, 1) for w in A.outs]]
        o = [[] for _ in range(A.nt + 1)]
        late = int(A.sums)
        if r > 0:
            o[late].append(("C", -1, 1))
        if A.ahead == 2 and r + 1 < A.n:
            o[0] += m
        if r > 0:
            o[1 + late] += [(w, -1, 1) for w in A.outs]
        start = 3 if A.self and A.dh == 64 else 0
        span = A.nt + 1 if A.ahead == 2 else A.nt - 3 if A.dh == 16 else A.nt - 2
        if r + A.ahead < A.n:
            for x in products(A.ahead):
                o[start + x[2] * (span - start) // len(A.chunks)].append(x)
        o[min(A.nt0 + 1, A.nt)].insert(0, ("C", 0, 0))
        o[min(A.nt0 + 2, A.nt)] += [(w, 0, 0) for w in A.outs]
        if A.ahead == 1 and r + 1 < A.n:
            o[span] = m + o[span]
        return o

    def numbered(A, i, r):
        def count(k):
            return sum(x[0] != "C" for items in A.work[k + 1] for x in items)
        first = sum(count(k) for k in range(-1, r))
        turn = sum(count(k + 1) for k in range(A.turn)) if A.loop else 0
        assert turn % 2 == 0
        n, res = 0, []
        for items in A.work[r + 1]:
            row = []
            for w, dg, k in items:
                row.append((w, dg, k, i * turn + (first + n), 6 + (first + n) % 2))
                n += w != "C"
            res.append(row)
        return res

    def each_step(A, e, run):
        run(0, -1)
        run(0, 0)
        if A.loop:
            with e.Fori(0, (A.n - 2) // A.turn) as i:
                for r in range(A.turn):
                    run(i, r + 1)
        else:
            for r in range(1, A.n - 1):
                run(0, r)
        run(0, A.n - 1)
        run(0, A.n)

    def loaded_value(A, i, k):
        return (i + (k // A.slots + 1)) * (16 * A.loads) + 16 * A.first_loads * (slot_of(A, k) == 0)

    def slot_of(A, k):
        return k % A.slots

    STK1 = STK[:, :, :].rearrange("p u n -> p (u n)")
    VS1 = VS[:, :, :].rearrange("p u n -> p (u n)")

    V_SLOTS = [VS[:, 0, :], VS[:, 1, :], WB[:, 2048:2048 + 1152]]

    def slot16(A, u):
        if A.self:
            at = u * (2048 + 2 * (P + T))
            q, k = STK1[:, at:at + 2048], STK1[:, at + 2048:at + 2048 + 2 * (P + T)]
        else:
            q, k = STK1[:, (u + 1) * 2048:(u + 2) * 2048], STK1[:, 0:2048]
        return q.bitcast(BF16).rearrange("p (h n) -> p h n", h=4), \
            k.bitcast(BF16).rearrange("p (h n) -> p h n", h=4 if A.self else 32)

    def slot64(A, u):
        if A.self:
            return [STK1[:, u * 8192 + 2048 * i:u * 8192 + 2048 * (i + 1)].rearrange("p (h n) -> p h n", h=2)
                    for i in range(4)]
        q = [STK1[:, u * 4096 + 2048 * i:u * 4096 + 2048 * (i + 1)] for i in range(2)]
        return [x.rearrange("p (h n) -> p h n", h=2) for x in q] + \
            [STK1[:, 12288 + 1024 * i:12288 + 1024 * (i + 1)].rearrange("p (h n) -> p h n", h=8) for i in range(2)]

    def head_of_k(A, g, h):
        if A.self:
            return h
        return g * A.nh + h if A.dh == 64 else (4 * (g % 2) + h) * 2 * B + g // 2 % 2 * B + g // 4

    def slot_v(A, g, u):
        return V_SLOTS[u] if A.self else VS1[:, g * P:(g + 1) * P]

    def load_group(e, A, g, u, pieces=(0, 1, 2, 3)):
        sem = A.s.loaded[u]
        if A.dh == 16:
            q, k = slot16(A, u)
            row = 0
            for piece, ((q0, q1), (k0, k1)) in enumerate(zip(Q_RUNS, K_RUNS)):
                sl = slice(row, row + 16 * (q1 - q0))
                row = sl.stop
                if piece not in pieces:
                    continue
                def rows(parts, a, b):
                    return parts[g // 2, a:b, :, 4 * (g % 2):4 * (g % 2) + 4, :].rearrange("k d h n -> (k d) h n")
                context = C3[k0:k1, :, 4 * (g % 2):4 * (g % 2) + 4, g // 2 % 2, g // 4].rearrange("k d h n -> (k d) h n")
                e.dma_start(q[sl, :, :], rows(Q3, q0, q1)).then_inc(sem, 16)
                if A.self:
                    e.dma_start(k[sl, :, P:P + T], rows(K3, k0, k1)).then_inc(sem, 16)
                    e.dma_start(k[sl, :, 0:SC], context).then_inc(sem, 16)
            if A.self and 3 in pieces:
                v = V16.rearrange("b g p t w -> (b g p) (t w)")
                e.dma_start(V_SLOTS[u][:, 128:1152], v[g * P:(g + 1) * P, 128:1152]).then_inc(sem, 16)
                e.dma_start(V_SLOTS[u][0:SC, 0:128], v[g * P:g * P + SC, 0:128]).then_inc(sem, 16)
        else:
            qa, qb, ka, kb = (x.bitcast(F32) for x in slot64(A, u))
            def rows(parts, part):
                return parts[part, g * P:(g + 1) * P, :].rearrange("(h d) n -> d h n", h=2)
            loads = [(0, qa[0:64], rows(Q2, 0)), (1, qa[64:P], rows(Q2, 1)), (2, qb[0:64], rows(Q2, 0))]
            if A.self:
                loads += [(0, ka[0:64], rows(K2, 0)), (1, ka[64:P], rows(K2, 0)), (2, kb[0:64], rows(K2, 1)),
                          (3, VS[:, u, 0:1024], V64.rearrange("b g p t w -> (b g) p (t w)")[g])]
            for piece, dst, src in loads:
                if piece in pieces:
                    e.dma_start(dst, src).then_inc(A.s.loaded[u + 2] if A.self and piece >= 2 else sem, 16)

    def load_context(e, A, piece):
        sem = A.s.loaded[0]
        if piece == 3:
            V = V16 if A.dh == 16 else V64
            e.dma_start(VS1[0:SC, 0:A.n * P].rearrange("p (g w) -> p g w", g=A.n),
                        V.rearrange("b g p t w -> p (b g) t w")[0:SC, :, 0, :]).then_inc(sem, 16)
        elif A.dh == 16:
            k = slot16(A, 0)[1]
            row = sum(16 * (k1 - k0) for k0, k1 in K_RUNS[:piece])
            k0, k1 = K_RUNS[piece]
            e.dma_start(k[row:row + 16 * (k1 - k0), :, 0:SC],
                        C3[k0:k1].rearrange("k d h m b n -> (k d) (h m b) n")).then_inc(sem, 16)
        else:
            ka, kb = (x.bitcast(F32) for x in slot64(A, 0)[2:])
            dst, part = [(ka[0:64], 0), (ka[64:P], 0), (kb[0:64], 1)][piece]
            for b in range(B):
                e.dma_start(dst[:, 4 * b:4 * b + 4, 0:SC],
                            C2[part, :, b].rearrange("(h d) n -> d h n", d=64)).then_inc(sem, 16)

    LOAD_PIECES = 4

    def load_first(e, A, piece):
        load_group(e, A, 0, 0, (piece,))

    def attention_sync(e, A):
        s = A.s
        def load(g):
            if g < A.n:
                need(e, s.pv_tile, (g - A.slots + 1) * A.nt)
                load_group(e, A, g, slot_of(A, g))
        def send_rows(g):
            u = slot_of(A, g)
            e.wait_ge(s.loaded[u], loaded_value(A, 0, g))
            if A.self and A.dh == 64:
                e.wait_ge(s.loaded[u + 2], (g // A.slots + 1) * 48)
            e.wait_ge(s.max_split, g + 1)
            for part in range(A.parts):
                if A.dh == 16:
                    dst, src = slot16(A, u)[0][K16 + part:K16 + part + 1], MP[0:32, g % 3, part, :]
                else:
                    dst, src = slot64(A, u)[1][64 + part:65 + part].bitcast(F32), MPR[0:16, g % 3, part, :].bitcast(F32)
                e.dma_start(dst.rearrange("o h (t n) -> o (h t) n", n=P), src).then_inc(s.rows_sent[g % 3], 16)
        first = 1 if A.self else 2
        lead = A.slots - 1 if A.self else 3
        for g in range(1, first + 1):
            load(g)
        if not A.window:
            send_rows(0)
        for g in range(first + 1, lead + 1):
            load(g)
        for g in range(A.n - 1):
            if not A.window:
                send_rows(g + 1)
            load(g + lead + 1)

    def fill(e, where, value):
        e.memset(where, value)
        e.drain()

    def clear_slots(e, A):
        s = A.s
        if A.ctx:
            for u in range(A.slots if A.self else 1):
                fill(e, V_SLOTS[u][:, 0:P] if A.self else VS1[:, 0:A.n * P], 0.0)
        for u in range(0 if A.constants_kept else A.slots):
            if A.dh == 16:
                if A.self or u == 0:
                    k = slot16(A, u)[1]
                    fill(e, k[:, :, 0:P], 0.0)
                    fill(e, k[K16:K16 + M_ROWS, :, 0:SC], 1.0)
                if A.self:
                    fill(e, k[K16:K16 + M_ROWS, :, P:P + T], 1.0)
            else:
                qa, qb, ka, kb = (x.bitcast(F32) for x in slot64(A, u))
                fill(e, qb[64:96, :, :], 0.0)
                if A.self or u == 0:
                    if A.ctx:
                        fill(e, ka[:, :, :], 0.0)
                        fill(e, kb[0:64, :, :], 0.0)
                    fill(e, kb[64:96, :, :], 0.0)
                    fill(e, kb[64:66, :, 0:T if A.self else SC], 1.0)
        e.drain().then_inc(s.cleared, 1)

    def attention_gpsimd(e, A):
        s = A.s
        for r in range(A.n if A.sums else 0):
            for t in A.tiles:
                e.wait_ge(s.p_ready, r * A.steps + t.index + 1)
                p, total = PB[:, t.index % 2, 0, :, :], PSUMS[:, t.c, :, :]
                if t.first:
                    if r > 0:
                        e.wait_ge(s.denominated, 2 * r + t.c - 1)
                    e.tensor_scalar(total, p, 1.0, None, ALU.mult)
                else:
                    e.tensor_tensor(total, total, p, ALU.add)
                e.drain().then_inc(s.tile_summed, 1)
                if t.last:
                    e.sem_inc(s.summed, 1)

    def attention_tensor(e, A):
        s = A.s

        def chunk(w, dg, k, n, bank, i, r):
            need(e, s.chunk_free, n - 1)
            if w == "A":
                v = slot_of(A, r + dg)
                if k == 0:
                    e.wait_ge(s.loaded[v], loaded_value(A, i, r + dg))
                kind, h, qt, half = A.chunks[k]
                q, keys = slot16(A, v) if A.dh == 16 else slot64(A, v)[0::2]
                rows = K16 if A.dh == 16 else P
                if kind == "ctx":
                    wide = SC if A.dh == 16 else SC + 1
                    for j in range(qt):
                        hj, tj = divmod(h + j, TB)
                        add_mask = A.masked and A.dh == 16
                        o = PS[:, bank, j * 80:j * 80 + wide]
                        m = e.matmul(o, q[0:rows, hj, tj * P:(tj + 1) * P],
                                     keys[0:rows, head_of_k(A, r + dg, hj), 0:wide], start=True, stop=not add_mask, skip_group_check=True)
                        if add_mask:
                            b = (r + dg) // (A.n // B)
                            m = e.matmul(o, IDB[:, :], MB[:, b * SC:(b + 1) * SC], start=False, stop=True,
                                         skip_group_check=True)
                else:
                    at = 0
                    for qt, half in qt:
                        wide = min(CH, (qt + 1) * P - half * CH) if A.causal else CH
                        diag = A.causal and qt // 4 == half
                        k0 = half * CH + (P if A.dh == 16 else 0)
                        m = e.matmul(PS[:, bank, at:at + wide], q[0:rows, h, qt * P:(qt + 1) * P],
                                     keys[0:rows, h, k0:k0 + wide], start=True, stop=not diag, skip_group_check=True)
                        at += wide
                        if diag:
                            m = e.matmul(PS[:, bank, at - P:at], IDB[:, :], CM_S[:, :], start=False, stop=True,
                                         skip_group_check=True)
            elif w == "M":
                e.wait_ge(s.max_ready, i * A.turn + (r + dg + 1))
                m = e.transpose(PS[0:A.nh * TB, bank, 0:P], MX[:, 0:A.nh * TB], ID[:, :])
            else:
                e.wait_ge(s.copied, (i * A.turn + (r + dg)) * 2 + (k + 1))
                rows = OT[:, :] if w == "E" else OD[:, :]
                p = P if w == "E" else 64
                for j in range(4):
                    m = e.transpose(PS[:, bank, j * p:(j + 1) * p], rows[:, j * P:(j + 1) * P], ID[0:p, 0:p])
            m.then_inc(s.chunk_ready, 1)

        def scores(t, pair, i, r):
            st = t.index * A.pairs + pair
            need(e, s.gated if A.window else s.p_ready, (i * A.turn + r) * A.steps + (st - 1))
            for hh in range(2):
                h, bank = 2 * pair + hh, 2 * (st % 2) + hh
                o = PS[:, bank, 0:CH - t.q0]
                qs = slice(t.c * CH + t.q0, (t.c + 1) * CH)
                if A.dh == 16:
                    q, k = slot16(A, slot_of(A, r))
                    rows = K16 + M_ROWS * (not A.window)
                    k0 = 0 if t.kind == "ctx" else P + t.j * P
                    m = e.matmul(o, k[0:rows, head_of_k(A, r, h), k0:k0 + P], q[0:rows, h, qs], start=True, stop=not t.diag,
                                 skip_group_check=True)
                    if t.diag:
                        m = e.matmul(PS[:, bank, 0:P], IDB[:, :], CM_T[:, :], start=False, stop=True, skip_group_check=True)
                else:
                    qa, qb, ka, kb = slot64(A, slot_of(A, r))
                    ks = slice(t.j * P, (t.j + 1) * P)
                    hk = head_of_k(A, r, h)
                    e.matmul(o, ka[:, hk, ks], qa[:, h, qs], start=True, stop=False)
                    m = e.matmul(o, kb[0:96, hk, ks], qb[0:96, h, qs], start=False, stop=True)
            m.then_inc(s.s_ready, 1)

        def with_v(t, part, i, r):
            if part == 0:
                e.wait_ge(s.p_ready, (i * A.turn + r) * A.steps + (t.index + 1) * A.pairs)
                if t.first:
                    need(e, s.copied, (i * A.turn + r - 1) * 2 + (t.c + 1) if A.dh == 16 else (i * A.turn + r) * 2 + t.c)
            bank = 4 + t.c if A.dh == 16 else 4
            w = P // A.nh
            vt = t.j + (1 if t.kind == "self" and A.dh == 16 else 0)
            V = slot_v(A, r, slot_of(A, r))[:, vt * P:(vt + 1) * P].rearrange("p (h w) -> p h w", h=A.nh)
            for h in range(part * A.pairs, (part + 1) * A.pairs):
                m = e.matmul(PS[w * h:w * (h + 1), bank, t.q0:CH], V[:, h, :],
                             PB[:, t.index % 2, h // 2, h % 2, 0:CH - t.q0], start=t.first, stop=t.last,
                             skip_group_check=True)
                if A.dh == 64 and A.ctx:
                    m = e.matmul(PS[32 * h:32 * (h + 1), 5, :], ONESC[:, :], PB[:, t.index % 2, 0, h, :],
                                 start=t.first, stop=t.last, skip_group_check=True)
            if part == 1:
                m.then_inc(s.pv_tile, 1)

        def denominators(g, c):
            e.wait_ge(s.summed, 2 * g + c + 1)
            need(e, s.copied, 2 * g + c)
            for h in range(2):
                m = e.matmul(PS[32 * h:32 * (h + 1), 5, :], ONES[:, :], PSUMS[:, c, h, :], start=True, stop=True,
                             skip_group_check=True)
            m.then_inc(s.denominated, 1)

        def run(i, r):
            work = numbered(A, i, r)
            if A.window and 0 <= r < A.n:
                e.wait_ge(s.loaded[slot_of(A, r)], loaded_value(A, i, r))
            if r == A.n and A.sums:
                denominators(r - 1, 1)
            if r in (-1, A.n):
                for x in work[0]:
                    if x[0] != "C":
                        chunk(*x, i, r)
                return
            if A.self and A.dh == 64:
                e.wait_ge(s.loaded[slot_of(A, r) + 2], (r // A.slots + 1) * 48)
            if not A.window:
                e.wait_ge(s.rows_sent[r % 3], (i + (r // 3 + 1)) * (16 * A.parts))
            for idx in range(A.nt + 1):
                if A.sums and (idx == A.nt0 + 1 or (idx == 1 and r > 0)):
                    denominators(r - (idx == 1), int(idx == 1))
                pieces = []
                if idx < A.nt:
                    pieces += [(scores, A.tiles[idx], k) for k in range(A.pairs)]
                if idx > 0:
                    pieces += [(with_v, A.tiles[idx - 1], k) for k in range(2)]
                chunks = [x for x in work[idx] if x[0] != "C"]
                done = 0
                for k, (piece, t, part) in enumerate(pieces):
                    piece(t, part, i, r)
                    upto = (k + 1) * len(chunks) // len(pieces)
                    for x in chunks[done:upto]:
                        chunk(*x, i, r)
                    done = upto
        each_step(A, e, run)

    def attention_scalar(e, A):
        s = A.s
        def run(i, r):
            if r in (-1, A.n):
                return
            g = i * A.turn + r
            for t in A.tiles:
                for pair in range(A.pairs):
                    st = t.index * A.pairs + pair
                    e.wait_ge(s.gated if A.window else s.s_ready, g * A.steps + (st + 1))
                    need(e, s.pv_tile, g * A.nt + (t.index - 1))
                    if A.sums:
                        need(e, s.tile_summed, g * A.nt + (t.index - 1))
                    dst = PB[:, t.index % 2, pair, :, 0:CH - t.q0]
                    if A.window:
                        e.activation(dst, dst, ACT.Square, scale=A.scale).then_inc(s.p_ready, 1)
                    else:
                        bias = 0.0
                        if A.masked:
                            b = g // (A.n // B)
                            col = b if t.kind == "ctx" else b * TB + t.j
                            bias = KB[:, col:col + 1]
                        e.activation(dst, PS[:, 2 * (st % 2):2 * (st % 2) + 2, 0:CH - t.q0], ACT.Exp, scale=A.scale,
                                     bias=bias).then_inc(s.p_ready, 1)
        each_step(A, e, run)

    def attention_vector(e, A):
        s = A.s
        maxp = MXP[:, 0:A.nh * TB * 3].rearrange("p (h t s) -> p h t s", h=A.nh, t=TB)
        maxf = MXP[:, 0:A.nh * TB * 3].rearrange("p (h s) -> p h s", s=3)
        e.memset(MXP[:, :], LOWEST)
        e.drain()

        def gate(t, r, g):
            st = t.index * A.pairs + r
            e.wait_ge(s.s_ready, g * A.steps + (st + 1))
            need(e, s.pv_tile, g * A.nt + (t.index - 1))
            win = MB[:, ds(g // (A.n // B) * T + t.c * CH, CH)].unsqueeze(1).broadcast_to([P, 2, CH])
            e.scalar_tensor_tensor(PB[:, t.index % 2, r, :, :], PS[:, 2 * (st % 2):2 * (st % 2) + 2, :], 0.0, win,
                                   ALU.max, ALU.mult).then_inc(s.gated, 1)

        def part_of_max(i, n, bank, g):
            kind, h, qt, half = A.chunks[i]
            if A.masked and A.dh == 64:
                need(e, s.chunk_free, n - 1)
            scratch = (SCR[:, :], WA[:, 5248:5248 + CH])[i % 2]
            if kind == "ctx":
                src = PS[:, bank, 0:qt * 80].rearrange("p (j n) -> p j n", j=qt)[:, :, 0:SC]
                if A.masked and A.dh == 64:
                    m = MB[:, ds(g // (A.n // B) * SC, SC)].unsqueeze(1).broadcast_to([P, qt, SC])
                    tmp = scratch[:, 0:qt * SC].rearrange("p (j n) -> p j n", j=qt)
                    e.tensor_tensor(tmp, src, m, ALU.add)
                    e.drain()
                    src = tmp
                e.tensor_reduce(maxf[:, h:h + qt, 2], src, AX.X, ALU.max).then_inc(s.chunk_free, 1)
            elif A.masked:
                qt, half = qt[0]
                k0 = g // (A.n // B) * T + half * CH
                e.tensor_tensor_reduce(scratch, PS[:, bank, :], MB[:, k0:k0 + CH], 1.0, LOWEST, ALU.add, ALU.max,
                                       maxp[:, h, qt, half:half + 1]).then_inc(s.chunk_free, 1)
            else:
                at = 0
                for qt, half in qt:
                    wide = min(CH, (qt + 1) * P - half * CH)
                    m = e.tensor_reduce(maxp[:, h, qt, half:half + 1], PS[:, bank, at:at + wide], AX.X, ALU.max)
                    at += wide
                m.then_inc(s.chunk_free, 1)
            if i == len(A.chunks) - 1:
                e.drain()
                e.tensor_reduce(MX[:, 0:A.nh * TB].rearrange("p (h t) -> p h t", h=A.nh), maxp, AX.X, ALU.max)\
                    .then_inc(s.max_ready, 1)

        def split_max(v, bank):
            w = A.nh * TB
            mt = MT[0:w, :]
            p1 = MP[0:w, v, 0, :] if A.dh == 16 else MPR[0:w, v, 0, :]
            e.tensor_scalar(p1, PS[0:w, bank, 0:P], -1.0, None, ALU.mult)
            e.tensor_scalar(mt, PS[0:w, bank, 0:P], -1.0, None, ALU.mult).then_inc(s.chunk_free, 1)
            e.drain()
            if A.dh == 16:
                p2, p3 = (MP[0:w, v, k, :] for k in (1, 2))
                e.tensor_tensor(mt, mt, p1, ALU.subtract)
                e.drain()
                e.tensor_copy(p2, mt)
                e.drain()
                e.tensor_tensor(p3, mt, p2, ALU.subtract).then_inc(s.max_split, 1)
            else:
                e.tensor_tensor(MPR[0:w, v, 1, :], mt, p1.bitcast(F32), ALU.subtract).then_inc(s.max_split, 1)

        def reciprocal(den, g, c):
            rc = RC[:, 0:4 * A.nh].rearrange("p (j h) -> p j h", j=4)
            if A.window:
                e.tensor_scalar(rc, den, 1e-6, None, ALU.max)
                e.drain()
                den = rc
            r = e.reciprocal(rc, den)
            if A.query_mask:
                t0 = g // (A.n // B) * TB + 4 * c
                e.drain()
                r = e.tensor_tensor(rc, rc, QM[:, t0:t0 + 4].unsqueeze(2).broadcast_to([P, 4, A.nh]), ALU.mult)
            return r

        def output(w, n, bank, g, c):
            if w == "D":
                den = PS[:, bank, 0:256].rearrange("p (j h w) -> p j h w", j=4, h=2)[:, :, :, 0]
                reciprocal(den, g, c).then_inc(s.chunk_free, 1)
                return
            o = PS[:, bank, :].rearrange("p (j h w) -> p j h w", j=4, h=A.nh)
            if A.dh == 16:
                reciprocal(o[:, :, :, 16], g, c)
            e.drain()
            per = A.n // B
            b = g // per
            dst = Y[:, :].rearrange("p (b c j g w) -> p b c j g w", b=B, c=2, j=4, g=per)[
                :, ds(b, 1), c, :, ds(g % per, 1), :].rearrange("p o j q (h w) -> p (o j q) h w", h=A.nh)
            rc = RC[:, 0:4 * A.nh].rearrange("p (j h) -> p j h", j=4).unsqueeze(3).broadcast_to([P, 4, A.nh, A.dh])
            e.tensor_tensor(dst, o[:, :, :, 0:A.dh], rc, ALU.mult).then_inc(s.chunk_free, 1)

        def run(i, r):
            g = i * A.turn + r
            for idx, items in enumerate(numbered(A, i, r)):
                if A.window and r not in (-1, A.n) and idx < A.nt:
                    for pair in range(A.pairs):
                        gate(A.tiles[idx], pair, g)
                for w, dg, k, n, bank in items:
                    if w == "C":
                        last = A.nt0 if k == 0 else A.nt
                        e.wait_ge(s.pv_tile, (g + dg) * A.nt + last)
                        if A.sums:
                            e.wait_ge(s.denominated, 2 * (g + dg) + k + 1)
                        if A.dh == 64:
                            e.tensor_copy(OD[:, :], PS[0:64, 5, :])
                        e.tensor_copy(OT[:, :], PS[:, 4 + k if A.dh == 16 else 4, :]).then_inc(s.copied, 1)
                        continue
                    e.wait_ge(s.chunk_ready, n + 1)
                    if w == "A":
                        part_of_max(k, n, bank, g + dg)
                    elif w == "M":
                        split_max((r + dg) % 3, bank)
                    else:
                        output(w, n, bank, g + dg, k)
        each_step(A, e, run)

    HID = [SCR[:, :], OT[:, :]]
    W_H, W_L = (STK1[:, 4096 * i:4096 * (i + 1)] for i in range(2))
    XH, XL = (STK1[:, 8192 + 2048 * i:8192 + 2048 * (i + 1)].rearrange("p (s k n) -> p s k n", s=2, k=KT) for i in range(2))
    HID_H, HID_L = (STK1[:, 12288 + 2048 * i:12288 + 2048 * (i + 1)].rearrange("p (s n) -> p s n", s=4) for i in range(2))
    MT_F = F // P

    def split_weights_scalar(e, s, w):
        for i in range(8):
            a = slice(CH * i, CH * (i + 1))
            h = e.activation(W_H[:, a], w[:, a], ACT.Copy)
        h.then_inc(s.w_high, 1)

    def split_weights_gpsimd(e, s, w):
        e.wait_ge(s.w_high, 1)
        e.tensor_tensor(W_L, w, W_H.bitcast(F32), ALU.subtract)

    def split_tokens_scalar(e, s, c):
        if c < NC:
            need(e, s.hid_product, (c - 1) * MT_F)
            e.activation(XH[:, c % 2], XTF[:, :, c * CH:(c + 1) * CH], ACT.Copy).then_inc(s.x_high, 1)

    def split_tokens_vector(e, s, c):
        if c < NC:
            e.wait_ge(s.x_high, c + 1)
            e.tensor_tensor(XL[:, c % 2], XTF[:, :, c * CH:(c + 1) * CH], XH[:, c % 2].bitcast(F32), ALU.subtract)\
                .then_inc(s.x_split, 1)

    def ffn_tensor(e, s):
        w1h, w1l = (w[:, 0:2048].rearrange("p (k n) -> p k n", k=KT) for w in (W_H, W_L))
        w2h, w2l = (w[:, 2048:4096].rearrange("p (m n) -> p m n", m=MT_F) for w in (W_H, W_L))

        def hidden(i):
            c, m = divmod(i, MT_F)
            need(e, s.hid_high, i - 3)
            if m == 0:
                e.wait_ge(s.x_split, c + 1)
            ms = slice(m * P, (m + 1) * P)
            for k in range(KT):
                for w, x in ((w1h, XH), (w1h, XL), (w1l, XH)):
                    mm = e.matmul(PS[:, i % 4, :], w[:, k, ms], x[:, c % 2, k, :],
                                  start=k == 0 and w is w1h and x is XH, stop=k == KT - 1 and w is w1l)
            mm.then_inc(s.hid_product, 1)

        def second(i):
            c, m = divmod(i, MT_F)
            e.wait_ge(s.hid_split, i + 1)
            if m == 0:
                need(e, s.added, 2 * (c - 1))
            for t in range(4):
                o = PS[:, 4 + 2 * (c % 2) + t // 2, t % 2 * D:(t % 2 + 1) * D]
                ts = slice(t * P, (t + 1) * P)
                for h, w in ((HID_H, w2h), (HID_H, w2l), (HID_L, w2h)):
                    mm = e.matmul(o, h[:, i % 4, ts], w[:, m, :], start=m == 0 and t % 2 == 0 and h is HID_H and w is w2h,
                                  stop=m == MT_F - 1 and h is HID_L, skip_group_check=True)
            mm.then_inc(s.hid_used, 1)
        n = NC * MT_F
        for i in range(n + 3):
            if i < n:
                hidden(i)
            if i >= 3:
                second(i - 3)

    def ffn_scalar(e, s, func, col, last=None):
        split_tokens_scalar(e, s, 0)
        for i in range(NC * MT_F):
            if i % MT_F == 2:
                split_tokens_scalar(e, s, i // MT_F + 1)
            e.wait_ge(s.hid_product, i + 1)
            need(e, s.hid_split, i - 1)
            m = i % MT_F
            bias = COL[:, col + m:col + m + 1]
            e.activation(HID[i % 2], PS[:, i % 4, :], func, bias=bias).then_inc(s.hid_ready, 1)
            need(e, s.hid_used, i - 3)
            e.activation(HID_H[:, i % 4, :], PS[:, i % 4, :], func, bias=bias).then_inc(s.hid_high, 1)
            if last is not None and i > MT_F:
                if m == 5:
                    square_root(e, last, i // MT_F - 1)
                if m == 6:
                    normalise(e, last, i // MT_F - 1, X, Y3, "layer")
        if last is not None:
            square_root(e, last, NC - 1)
            normalise(e, last, NC - 1, X, Y3, "layer")

    def add_row(e, r):
        e.tensor_tensor(X[:, :, :], X[:, :, :], r.unsqueeze(1).broadcast_to([P, NT, D]), ALU.add)
        e.drain()

    def ffn_vector(e, s, b2, last=None):
        if last is not None:
            statistics, scales, add_bias = ln_steps(e, last, X, "layer", 1e-5, weighted=(X, r3("beta2")))
        split_tokens_vector(e, s, 0)
        add_row(e, b2)
        def add_sums(c):
            e.wait_ge(s.hid_used, (c + 1) * MT_F)
            for k in range(2):
                x = X[:, 4 * c + 2 * k:4 * c + 2 * k + 2, :]
                e.tensor_tensor(x, x, PS[:, 4 + 2 * (c % 2) + k, :].rearrange("p (t d) -> p t d", t=2), ALU.add)\
                    .then_inc(s.added, 1)
        for i in range(NC * MT_F):
            if i % MT_F == 2:
                split_tokens_vector(e, s, i // MT_F + 1)
            e.wait_ge(s.hid_high, i + 1)
            e.tensor_tensor(HID_L[:, i % 4, :], HID[i % 2], HID_H[:, i % 4, :].bitcast(F32), ALU.subtract)\
                .then_inc(s.hid_split, 1)
            if i % MT_F == 4 and i > MT_F:
                add_sums(i // MT_F - 1)
                if last is not None:
                    e.drain()
                    statistics(i // MT_F - 1)
            if last is not None and i > MT_F and i % MT_F == 5:
                scales(i // MT_F - 1)
            if last is not None and i > MT_F and i % MT_F == 7:
                add_bias(i // MT_F - 1)
        add_sums(NC - 1)
        if last is not None:
            e.drain()
            for step in (statistics, scales, add_bias):
                step(NC - 1)

    def square_tensor(e, s, w, pairs_of_tiles):
        for j in pairs_of_tiles:
            need(e, s.taken2, j - 3)
            for t in range(2):
                for k in range(KT):
                    tt = 2 * j + t
                    m = e.matmul(PS[:, j % 4, t * D:(t + 1) * D], XTF[:, k, tt * P:(tt + 1) * P], w[:, k, :],
                                 start=k == 0, stop=k == KT - 1, skip_group_check=True)
            m.then_inc(s.product2, 1)

    def square_vector(e, s, bias=None, leaky=None):
        if bias is not None:
            add_row(e, bias)
        for j in range(NT // 2):
            e.wait_ge(s.product2, j + 1)
            o = PS[:, j % 4, :].rearrange("p (t d) -> p t d", t=2)
            x = X[:, 2 * j:2 * j + 2, :]
            if leaky is None:
                e.tensor_tensor(x, x, o, ALU.add).then_inc(s.taken2, 1)
            else:
                y = SCR[:, :].rearrange("p (t d) -> p t d", t=2)
                z = OT[:, :].rearrange("p (t d) -> p t d", t=2)
                e.tensor_tensor(y, o, leaky.unsqueeze(1).broadcast_to([P, 2, D]), ALU.add).then_inc(s.taken2, 1)
                e.drain()
                e.scalar_tensor_tensor(z, y, 0.2, y, ALU.mult, ALU.max)
                e.drain()
                e.tensor_tensor(x, x, z, ALU.add)

    def key_masks_vector(e, layer):
        e.tensor_reduce(KSUM[:, :], X[:, :, :], AX.X, ALU.add)
        e.drain()
        e.tensor_scalar(QM[:, :], KSUM[:, :], 0.0, None, ALU.not_equal)
        if layer == 0:
            e.tensor_reduce(KC[0:SC, :], CTXN[0:SC, :, :], AX.X, ALU.add)
            e.drain()
            e.tensor_scalar(KZ[0:SC, 0:B], KC[0:SC, :], 0.0, None, ALU.is_equal)
            e.drain()
            e.tensor_scalar(KB[0:SC, 0:B], KZ[0:SC, 0:B], NEG1, None, ALU.mult)
        else:
            e.tensor_scalar(KZ[:, :], KSUM[:, :], 0.0, None, ALU.is_equal)
            e.drain()
            e.tensor_scalar(KB[:, :], KZ[:, :], NEG1, None, ALU.mult)

    turn = lambda n: sems(n, TurnSems, 2)
    sq = lambda n: sems(n, SquareSems, 2)
    ff = lambda n: sems(n, FeedForwardSems, 8)
    mk = lambda n: sems(n, KeyMaskSems, 5)

    L = [6 + 4 * l for l in range(3)]
    at0 = attention(3, 16, 8, ctx_keys=True, self_keys=True, causal=True, scale=0.25)
    at1 = [attention(L[0] + 2, 64, 4, ctx_keys=True, scale=0.125, masked=True, query_mask=True)] + \
          [attention(L[l] + 2, 64, 4, self_keys=True, scale=0.125, masked=True, query_mask=True, constants_kept=l == 2)
           for l in (1, 2)]
    at2 = attention(20, 16, 8, ctx_keys=True, window=True, scale=0.25)
    at3 = attention(24, 16, 8, ctx_keys=True, scale=0.0625, masked=True)
    p0, p1, p2, p3 = project(2), [project(l + 1) for l in L], project(19), project(23)
    ln0, ln02, ln0f = ln(1), ln(4), ln(4)
    ln1 = [ln(l + 3) for l in L]
    ln2, ln2c = ln(18), ln(18)
    ln3, ln3o = ln(26), ln(27)
    tn0, tn0c, tn0f = turn(1), turn(1), turn(4)
    tn1, tn1f, m1 = [turn(l) for l in L], [turn(l + 3) for l in L], [mk(l) for l in L]
    tn2, tn2c, tn2o = turn(18), turn(18), turn(21)
    tn3, tn3c, tn3o, tn3f = turn(22), turn(22), turn(25), turn(26)
    sq1, sq2, sq3 = [sq(l + 3) for l in L], sq(21), sq(25)
    ff0, ff3 = ff(5), ff(27)
    sp0, sp3 = sems(4, SplitSems, 1), sems(26, SplitSems, 1)
    W0_FF, W3_FF = WA[:, 2560:6656], WA[:, 0:4096]

    ID_F, RELU = ACT.Identity, ACT.Relu
    bv0, bcv0 = row(RA, ROWS_L0, "bv"), row(RA, ROWS_L0, "bcv")
    sections0 = [(q_items(b, W0.qkv, 0, q3_dst, COLS["L0q"], ID_F) + q_items(b, W0.qkv, D, k3_dst, COLS["L0k"], ID_F),
                  v_items(b, W0.qkv, 2 * D, bv0, V16, 4, 1)) for b in range(B)]
    sections0[0] = (c_items(W0.ckv, 0, c3_dst, COLS["L0c"], ID_F) + sections0[0][0],
                    vc_items(W0.ckv, D, bcv0, V16, 4) + sections0[0][1])
    sections1 = []
    for l in range(3):
        w, bq, bk, bv = W1[l], COLS["L1q"] + 2 * l, COLS["L1k"] + 2 * l, row(RB, ROWS_L1, f"bv{l}")
        q = [q_items(b, w["q"], 0, q2_dst, bq, RELU) for b in range(B)]
        if l == 0:
            sections1.append([(c_items(w["k"], 0, c2_dst, bk, RELU), vc_items(w["v"], 0, bv, V64, 2)), (q[0], []), (q[1], [])])
        else:
            sections1.append([(q[b] + q_items(b, w["k"], 0, k2_dst, bk, RELU), v_items(b, w["v"], 0, bv, V64, 2, 0))
                              for b in range(B)])
    q = [q_items(b, W2["q"], 0, q3_dst, None, ID_F) for b in range(B)]
    sections2 = [(c_items(W2["k"], 0, c3_dst, None, ID_F), vc_items(W2["v"], 0, None, V16, 4)), (q[0], []), (q[1], [])]
    q = [q_items(b, W3.bd[3], 0, q3_dst, None, ID_F, diag=True) for b in range(B)]
    sections3 = [(c_items(W3.bd[4], 0, c3_dst, None, ID_F, diag=True), vc_items(W3.bd[2], 0, None, V16, 4, diag=True)),
                 (q[0], []), (q[1], [])]

    r3 = lambda n: RA[:, ROWS_L3.index(n), :]
    gkv = RA[:, len(ROWS_L3), :]
    col = lambda scale, bias, l=0: (COLS[scale] + 2 * l, None if bias is None else COLS[bias] + 2 * l)

    block = ctx.enter_context(nc.Block())

    @block.sync
    def _(e):
        nxt = lambda: next_stage(e, "sync")
        load_sync(e)
        nxt()
        e.wait_ge(ld.w0, 48)
        load_more(e)
        nxt()
        project_sync(e, p0, sections0, 3, False, at0)
        nxt()
        attention_sync(e, at0)
        e.wait_ge(ld.w1c, 32)
        nxt()
        nxt()
        nxt()
        for l in range(3):
            m = m1[l]
            n = B if l == 0 else NT
            p = SC if l == 0 else P
            e.wait_ge(m.row_cast, 1)
            km = KM.rearrange("t p -> (t p)")[0:n * p]
            e.dma_start(km.rearrange("(t p) -> t p", p=p), KZB[0:n, 0:p]).then_inc(m.stored, 16)
            e.wait_ge(m.stored, 16)
            e.dma_start(MB[:, 0:n * p], km.partition_broadcast(P)).then_inc(m.spread, 16)
            e.wait_ge(m.spread, 16)
            e.wait_ge([ld.w1a, ld.w1b, ld.w1c][l], [80, 64, 96][l])
            nxt()
            project_sync(e, p1[l], sections1[l], 2, True, at1[l])
            nxt()
            attention_sync(e, at1[l])
            nxt()
            if l == 0:
                load_layer(e, 1, ld.w1b)
                load_block3(e)
            nxt()
            if l == 0:
                load_layer(e, 2, ld.w1c)
            if l == 1:
                load_block2(e)
        e.dma_start(VS[:, :, :].rearrange("p u n -> p (u n)")[:, 0:TOK].bitcast(I32),
                    a["idx"].rearrange("b t -> (b t)").partition_broadcast(P)).then_inc(ld.masks, 16)
        e.wait_ge(ld.w2, 64)
        e.wait_ge(ld.w3, 16 * W3_LOADS)
        nxt()
        project_sync(e, p2, sections2, 3, False, at2)
        nxt()
        attention_sync(e, at2)
        nxt()
        nxt()
        e.dma_start(CTXN[0:SC, :, :], a["ctx"].rearrange("b s d -> s b d")).then_inc(ld.ctx, 16)
        e.wait_ge(ld.ctx, 16)
        nxt()
        project_sync(e, p3, sections3, 3, False, at3)
        nxt()
        attention_sync(e, at3)
        nxt()
        nxt()
        nxt()
        o = out.rearrange("b (t p) d -> p (b t) d", p=P)
        for c in range(NC):
            e.wait_ge(ln3o.finished, c + 1)
            e.dma_start(o[:, 4 * c:4 * c + 4, :], X[:, 4 * c:4 * c + 4, :]).then_inc(ld.out, 16)
        e.wait_ge(ld.out, 16 * NC)

    @block.gpsimd
    def _(e):
        nxt = lambda: next_stage(e, "gpsimd")
        load_pool(e)
        nxt()
        nxt()
        clear_slots(e, at0)
        nxt()
        nxt()
        ln_gpsimd(e, ln02, Y3, row(RA, ROWS_L0, "g2"), Y3)
        split_weights_gpsimd(e, sp0, W0_FF)
        nxt()
        nxt()
        e.memset(WA[:, 4608:4992], 0.0).then_inc(ld.cleared, 1)
        for l in range(3):
            nxt()
            clear_slots(e, at1[l])
            nxt()
            attention_gpsimd(e, at1[l])
            nxt()
            ln_gpsimd(e, ln1[l], Y3, row(RB, ROWS_L1, f"gamma{l}"), X)
            nxt()
        nxt()
        clear_slots(e, at2)
        nxt()
        for _ in range(3):
            nxt()
        clear_slots(e, at3)
        nxt()
        nxt()
        nxt()
        split_weights_gpsimd(e, sp3, W3_FF)
        ln_gpsimd(e, ln3, Y3, r3("g1"), X)
        nxt()
        ln_gpsimd(e, ln3o, Y3, r3("g2"), X)

    @block.tensor
    def _(e):
        nxt = lambda: next_stage(e, "tensor")
        nxt()
        turn_ctx_tensor(e, tn0c, CTXN)
        turn_tensor(e, tn0, tokens(Y3), ln0.normed)
        nxt()
        project_tensor(e, p0, sections0)
        nxt()
        attention_tensor(e, at0)
        nxt()
        turn_tensor(e, tn0f, tokens(Y3), ln0f.normed)
        nxt()
        ffn_tensor(e, ff0)
        nxt()
        for l in range(3):
            turn_tensor(e, tn1[l], tokens(X))
            n, p = (B, SC) if l == 0 else (NT, P)
            e.wait_ge(m1[l].row_ready, 1)
            e.transpose(PS[0:n, 0, 0:p], KZ[0:p, 0:n], ID[0:p, 0:p]).then_inc(m1[l].turned, 1)
            nxt()
            project_tensor(e, p1[l], sections1[l])
            nxt()
            attention_tensor(e, at1[l])
            nxt()
            turn_square_tensor(e, tn1f[l], sq1[l], W1[l]["f"], tokens(Y3), ln1[l].normed)
            nxt()
        turn_ctx_tensor(e, tn2c, CTXN, ln2c.normed, B)
        turn_tensor(e, tn2, tokens(Y3), ln2.normed)
        nxt()
        project_tensor(e, p2, sections2)
        nxt()
        attention_tensor(e, at2)
        nxt()
        turn_square_tensor(e, tn2o, sq2, W2["o"], tokens(Y3))
        nxt()
        turn_ctx_tensor(e, tn3c, CTXN, ld.ctx, 16)
        turn_tensor(e, tn3, tokens(X))
        nxt()
        project_tensor(e, p3, sections3)
        nxt()
        attention_tensor(e, at3)
        nxt()
        turn_square_tensor(e, tn3o, sq3, W3.out, tokens(Y3))
        nxt()
        turn_tensor(e, tn3f, tokens(Y3), ln3.normed)
        nxt()
        ffn_tensor(e, ff3)

    @block.scalar
    def _(e):
        nxt = lambda: next_stage(e, "scalar")
        nxt()
        turn_ctx_scalar(e, tn0c)
        ln_scalar(e, ln0, X, Y3, "layer", tn0, col("g1", "be1"))
        nxt()
        project_scalar(e, p0, sections0, 3)
        nxt()
        attention_scalar(e, at0)
        nxt()
        split_weights_scalar(e, sp0, W0_FF)
        ln_scalar(e, ln02, X, Y3, "layer")
        ln_scalar(e, ln0f, Y3, Y3, "layer", tn0f, col("gf", "bf"))
        nxt()
        ffn_scalar(e, ff0, ACT.Gelu, COLS["L0f"])
        nxt()
        for l in range(3):
            turn_scalar(e, tn1[l])
            n, p = (B, SC) if l == 0 else (NT, P)
            e.wait_ge(m1[l].turned, 1)
            e.activation(KZB[0:n, 0:p], PS[0:n, 0, 0:p], ACT.Copy, scale=NEG1 * 8).then_inc(m1[l].row_cast, 1)
            nxt()
            project_scalar(e, p1[l], sections1[l], 2)
            nxt()
            attention_scalar(e, at1[l])
            nxt()
            ln_scalar(e, ln1[l], X, Y3, "unbiased", tn1f[l], col("gamma", "beta", l))
            nxt()
        ctx_rms_scalar(e, ln2c)
        turn_ctx_scalar(e, tn2c)
        ln_scalar(e, ln2, X, Y3, "rms", tn2, col("gq", None))
        nxt()
        project_scalar(e, p2, sections2, 3)
        nxt()
        attention_scalar(e, at2)
        nxt()
        turn_scalar(e, tn2o)
        nxt()
        turn_ctx_scalar(e, tn3c)
        turn_scalar(e, tn3)
        nxt()
        project_scalar(e, p3, sections3, 3)
        nxt()
        attention_scalar(e, at3)
        nxt()
        turn_scalar(e, tn3o)
        nxt()
        split_weights_scalar(e, sp3, W3_FF)
        ln_scalar(e, ln3, X, Y3, "layer", tn3f, col("L3g1", "L3beta1"))
        nxt()
        ffn_scalar(e, ff3, ACT.Relu, COLS["L3f"], ln3o)

    @block.vector
    def _(e):
        nxt = lambda: next_stage(e, "vector")
        nxt()
        ln_vector(e, ln0, X, "layer", 1e-5, arrived=ld.x_chunks)
        nxt()
        project_vector(e, p0, sections0, 3, False)
        nxt()
        attention_vector(e, at0)
        nxt()
        ln_vector(e, ln02, X, "layer", 1e-5, add=Y3, weighted=(Y3, row(RA, ROWS_L0, "be2")))
        e.drain()
        ln_vector(e, ln0f, Y3, "layer", 1e-5)
        nxt()
        ffn_vector(e, ff0, row(RA, ROWS_L0, "b2"))
        nxt()
        for l in range(3):
            key_masks_vector(e, l)
            e.drain().then_inc(m1[l].row_ready, 1)
            nxt()
            project_vector(e, p1[l], sections1[l], 2, True)
            nxt()
            attention_vector(e, at1[l])
            nxt()
            ln_vector(e, ln1[l], X, "unbiased", 1e-8, add=Y3, weighted=(X, row(RB, ROWS_L1, f"beta{l}")))
            e.drain()
            square_vector(e, sq1[l], leaky=row(RB, ROWS_L1, f"bff{l}"))
            nxt()
        e.wait_ge(ld.w3, 16 * W3_LOADS)
        ctx_rms_vector(e, ln2c, gkv, 1.1920929e-07)
        e.drain()
        ln_vector(e, ln2, X, "rms", 1.1920929e-07)
        for j in range(2):
            e.tensor_copy(W3.bd[3 + j].rearrange("p (d h) -> p d h", h=8), W3.bd[j].rearrange("p (h d) -> p d h", h=8))
        e.wait_ge(ld.masks, 16)
        ix = VS[:, :, :].rearrange("p u n -> p (u n)")[:, 0:TOK]
        e.tensor_scalar(ix, ix.bitcast(I32), POS[:, 0:1], None, ALU.subtract)
        e.drain()
        e.tensor_tensor(ix, ix, ix, ALU.mult)
        e.drain()
        e.tensor_scalar(MB[:, :], ix, 1.0, None, ALU.is_le)
        nxt()
        project_vector(e, p2, sections2, 3, False)
        nxt()
        attention_vector(e, at2)
        nxt()
        square_vector(e, sq2)
        nxt()
        e.tensor_scalar(MB[:, 0:B * SC], MI[:, 0:B * SC], 0.0, NEG3_ROUND, ALU.is_equal, ALU.mult)
        e.tensor_scalar(KB[0:SC, 0:B], MI[0:SC, B * SC:B * SC + B], 0.0, NEG3_ROUND / 16, ALU.is_equal, ALU.mult)
        nxt()
        project_vector(e, p3, sections3, 3, False)
        nxt()
        attention_vector(e, at3)
        nxt()
        square_vector(e, sq3, bias=r3("bout"))
        nxt()
        ln_vector(e, ln3, X, "layer", 1e-5, weighted=(X, r3("beta1")))
        nxt()
        ffn_vector(e, ff3, r3("bff2"), ln3o)


def kernel(**inputs):
    import numpy as np
    import concourse.bacc as bacc
    from concourse.bass_utils import run_bass_kernel_spmd

    g = {k: np.asarray(v) for k, v in inputs.items()}
    l0, l1, l2, l3 = (lambda n, p=f"L{i}_xattn_": g[p + n] for i in range(4))
    cols = lambda v: v.reshape(-1, P).T
    by = lambda v: np.concatenate([v[..., i:i + P].reshape(v.shape[:-1] + (8, 16)).swapaxes(-1, -2)
                                   .reshape(v.shape[:-1] + (P,)) for i in range(0, v.shape[-1], P)], axis=-1)
    qk = lambda v, n: np.concatenate([by(v[..., :n]), v[..., n:]], axis=-1)
    arrays = {
        "x": g["x"], "ctx": g["ctx_1024"], "idx": g["itok_BxS_0_255"],
        "mask": g["mask_Bx1x1xS2_if1"].reshape(B, SC),
        "w_qkv": qk(l0("w_qkv"), 2 * D), "w_ckv": qk(l0("w_ckv"), D), "w1": l0("w1"), "w2": l0("w2"),
        "Wq": l1("Wq"), "Wk": l1("Wk"), "Wv": l1("Wv"), "Wf": l1("Wff"),
        "W2q": by(l2("Wq").T), "W2k": by(l2("Wk").T), "W2v": l2("Wv").T, "W2o": l2("Wo").T,
        "w3q": l3("wq"), "w3k": l3("wk"), "w3v": l3("wv"), "w3_out": l3("w_out"), "w3_1": l3("w_ff1"), "w3_2": l3("w_ff2"),
        "rows0": np.stack([l0("b_qkv")[2 * D:], l0("b_ckv")[D:], l0("b2"), l0("g2"), l0("be2")]),
        "rows1": np.concatenate([l1("bv"), l1("gamma"), l1("beta"), l1("bff")]),
        "rows23": np.stack([l3("b_out"), l3("g1"), l3("beta1"), l3("b_ff2"), l3("g2"), l3("beta2"),
                            l2("gamma_kv")]),
        "cols": np.concatenate([cols(by(l0("b_qkv")[:2 * D])), cols(by(l0("b_ckv")[:D])), cols(l0("b1")),
                                cols(l1("bq").reshape(-1)), cols(l1("bk").reshape(-1)), cols(l3("b_ff1")),
                                cols(l0("g1")), cols(l0("be1")), cols(l0("gf")), cols(l0("bf")),
                                cols(l1("gamma").reshape(-1)), cols(l1("beta").reshape(-1)), cols(l2("gamma_q")),
                                cols(l3("g1")), cols(l3("beta1"))], axis=1),
    }
    nc = bacc.Bacc("TRN2", target_bir_lowering=False, num_devices=1)
    sent, args = {}, {}
    for name, v in arrays.items():
        v = np.ascontiguousarray(v)
        sent[f"in_{name}"] = v
        args[name] = nc.dram_tensor(f"in_{name}", v.shape, mybir.dt.from_np(v.dtype), kind="ExternalInput").ap()
    res = nc.dram_tensor("out_0", (B, T, D), F32, kind="ExternalOutput").ap()
    build(nc, args, res)
    r = run_bass_kernel_spmd(nc, [sent], core_ids=[0])
    return r.results[0]["out_0"]
```
